# Optimizing a Trainium2 kernel written in Bass

```python
import numpy as np
import jax
import jax.numpy as jnp

def _softmax(x, axis=-1):
    return jax.nn.softmax(x, axis=axis)

def _gelu(x):
    return jax.nn.gelu(x, approximate=True)

def _silu(x):
    return jax.nn.silu(x)

def _sigmoid(x):
    return jax.nn.sigmoid(x)

def _layernorm(x, axis=-1, eps=1e-05):
    m = jnp.mean(x, axis=axis, keepdims=True)
    v = jnp.var(x, axis=axis, keepdims=True)
    return (x - m) / jnp.sqrt(v + eps)

def _scatter_add(tgt, idx, src, axis=0):
    return tgt.at[idx].add(src)

def _segment_sum(src, seg, n):
    return jax.ops.segment_sum(src, seg, n)
kernel_name = 'mk_xattn_ffn_d1_seqx_r8_339f2f'

def setup_inputs(seed: int=0):
    np.random.seed(seed)
    _w = jnp.asarray

    def _rec_inputs():
        import jax
        import jax.numpy as jnp
        _rk = jax.random.key(seed)
        x = -0.0003929 + 0.9999 * jax.random.normal(jax.random.fold_in(_rk, 1), (16, 56, 256), jnp.float32)
        _lenS = 56 - jax.random.randint(jax.random.fold_in(_rk, 7), (16,), 0, max(1, 56 // 4) + 1, jnp.int32)
        _lenS2 = 1500 - jax.random.randint(jax.random.fold_in(_rk, 8), (16,), 0, max(1, 1500 // 4) + 1, jnp.int32)
        _ctx_2048P = jax.random.normal(jax.random.fold_in(_rk, 11), (16, 16, 256), jnp.float32)
        _ctx_2048c = jax.random.dirichlet(jax.random.fold_in(_rk, 511), 0.3 * jnp.ones((16,), jnp.float32), (16, 1500))
        _ctx_2048t = jnp.einsum('bsk,bkd->bsd', _ctx_2048c, _ctx_2048P)
        _ctx_2048t = _ctx_2048t * jax.lax.rsqrt(jnp.mean(jnp.square(_ctx_2048t)) + 1e-12) * 0.953939
        ctx_2048 = 1.72703e-05 + 1.00003 * (_ctx_2048t + 0.3 * jax.random.normal(jax.random.fold_in(_rk, 611), (16, 1500, 256), jnp.float32))
        return (x, ctx_2048)
    x, ctx_2048 = _rec_inputs()

    def _L0_xattn_setup():
        import jax, jax.numpy as jnp
        import numpy as np
        DIM = 256
        H = 16
        D = 128
        INNER = H * D
        N_IMG = 257
        EPS = 1e-06

        def rms_norm(x, scale, eps=EPS):
            ms = jnp.mean(jnp.square(x), axis=-1, keepdims=True)
            return x * jax.lax.rsqrt(ms + eps) * scale

        def sdpa(q, k, v):
            scale = 1.0 / jnp.sqrt(jnp.asarray(D, q.dtype))
            scores = jnp.einsum('bshd,blhd->bhsl', q, k) * scale
            attn = jax.nn.softmax(scores, axis=-1)
            return jnp.einsum('bhsl,blhd->bshd', attn, v)
        key = jax.random.key(seed)
        ks = jax.random.split(key, 16)
        std = 1.0 / np.sqrt(DIM)
        inp = {'x': jax.random.normal(ks[0], (2, 512, DIM), jnp.float32), 'context': jax.random.normal(ks[1], (2, 769, DIM), jnp.float32), 'q_w': jax.random.normal(ks[2], (DIM, INNER), jnp.float32) * std, 'q_b': jnp.zeros((INNER,), jnp.float32), 'k_w': jax.random.normal(ks[3], (DIM, INNER), jnp.float32) * std, 'k_b': jnp.zeros((INNER,), jnp.float32), 'v_w': jax.random.normal(ks[4], (DIM, INNER), jnp.float32) * std, 'v_b': jnp.zeros((INNER,), jnp.float32), 'ki_w': jax.random.normal(ks[5], (DIM, INNER), jnp.float32) * std, 'ki_b': jnp.zeros((INNER,), jnp.float32), 'vi_w': jax.random.normal(ks[6], (DIM, INNER), jnp.float32) * std, 'vi_b': jnp.zeros((INNER,), jnp.float32), 'o_w': jax.random.normal(ks[7], (INNER, DIM), jnp.float32) * std, 'o_b': jnp.zeros((DIM,), jnp.float32), 'nq_s': jnp.ones((INNER,), jnp.float32), 'nkt_s': jnp.ones((INNER,), jnp.float32), 'nki_s': jnp.ones((INNER,), jnp.float32)}
        return inp
    _L0_xattn_all = _L0_xattn_setup()
    _L0_xattn_in = {k: v for k, v in _L0_xattn_all.items() if k in ('q_w', 'q_b', 'k_w', 'k_b', 'v_w', 'v_b', 'ki_w', 'ki_b', 'vi_w', 'vi_b', 'o_w', 'o_b', 'nq_s', 'nkt_s', 'nki_s')}
    del _L0_xattn_all

    def _L0_ffn_setup():
        import jax, jax.numpy as jnp
        import numpy as np
        B, S, D = (2, 256, 256)
        I = 128
        E = 32
        K = 4
        NS = 1
        ALPHA = 7.0

        def _clamped_swiglu(x, wg, wu, wd):
            g = jnp.clip(x @ wg.T, -ALPHA, ALPHA)
            u = jnp.clip(x @ wu.T, -ALPHA, ALPHA)
            return jax.nn.silu(g) * u @ wd.T
        key = jax.random.key(seed)
        ks = jax.random.split(key, 9)
        s = 0.02
        return {'hidden': jax.random.normal(ks[0], (B, S, D), jnp.float32), 'router_w': jax.random.normal(ks[1], (E, D), jnp.float32) * s, 'expert_bias': jax.random.normal(ks[2], (E,), jnp.float32) * s, 'gate_w': jax.random.normal(ks[3], (E, I, D), jnp.float32) * s, 'up_w': jax.random.normal(ks[4], (E, I, D), jnp.float32) * s, 'down_w': jax.random.normal(ks[5], (E, D, I), jnp.float32) * s, 'shared_gate_w': jax.random.normal(ks[6], (NS * I, D), jnp.float32) * s, 'shared_up_w': jax.random.normal(ks[7], (NS * I, D), jnp.float32) * s, 'shared_down_w': jax.random.normal(ks[8], (D, NS * I), jnp.float32) * s}
    _L0_ffn_all = _L0_ffn_setup()
    _L0_ffn_in = {k: v for k, v in _L0_ffn_all.items() if k in ('router_w', 'expert_bias', 'gate_w', 'up_w', 'down_w', 'shared_gate_w', 'shared_up_w', 'shared_down_w')}
    del _L0_ffn_all
    return {'x': x, 'ctx_2048': ctx_2048, 'L0_xattn_q_w': _L0_xattn_in['q_w'], 'L0_xattn_q_b': _L0_xattn_in['q_b'], 'L0_xattn_k_w': _L0_xattn_in['k_w'], 'L0_xattn_k_b': _L0_xattn_in['k_b'], 'L0_xattn_v_w': _L0_xattn_in['v_w'], 'L0_xattn_v_b': _L0_xattn_in['v_b'], 'L0_xattn_ki_w': _L0_xattn_in['ki_w'], 'L0_xattn_ki_b': _L0_xattn_in['ki_b'], 'L0_xattn_vi_w': _L0_xattn_in['vi_w'], 'L0_xattn_vi_b': _L0_xattn_in['vi_b'], 'L0_xattn_o_w': _L0_xattn_in['o_w'], 'L0_xattn_o_b': _L0_xattn_in['o_b'], 'L0_xattn_nq_s': _L0_xattn_in['nq_s'], 'L0_xattn_nkt_s': _L0_xattn_in['nkt_s'], 'L0_xattn_nki_s': _L0_xattn_in['nki_s'], 'L0_ffn_router_w': _L0_ffn_in['router_w'], 'L0_ffn_expert_bias': _L0_ffn_in['expert_bias'], 'L0_ffn_gate_w': _L0_ffn_in['gate_w'], 'L0_ffn_up_w': _L0_ffn_in['up_w'], 'L0_ffn_down_w': _L0_ffn_in['down_w'], 'L0_ffn_shared_gate_w': _L0_ffn_in['shared_gate_w'], 'L0_ffn_shared_up_w': _L0_ffn_in['shared_up_w'], 'L0_ffn_shared_down_w': _L0_ffn_in['shared_down_w']}

def reference(x, ctx_2048, L0_xattn_q_w, L0_xattn_q_b, L0_xattn_k_w, L0_xattn_k_b, L0_xattn_v_w, L0_xattn_v_b, L0_xattn_ki_w, L0_xattn_ki_b, L0_xattn_vi_w, L0_xattn_vi_b, L0_xattn_o_w, L0_xattn_o_b, L0_xattn_nq_s, L0_xattn_nkt_s, L0_xattn_nki_s, L0_ffn_router_w, L0_ffn_expert_bias, L0_ffn_gate_w, L0_ffn_up_w, L0_ffn_down_w, L0_ffn_shared_gate_w, L0_ffn_shared_up_w, L0_ffn_shared_down_w):
    import jax
    import jax.numpy as jnp

    def _L0_xattn_ref(x, context, q_w, q_b, k_w, k_b, v_w, v_b, ki_w, ki_b, vi_w, vi_b, o_w, o_b, nq_s, nkt_s, nki_s):
        import jax, jax.numpy as jnp
        import numpy as np
        DIM = 256
        H = 16
        D = 128
        INNER = H * D
        N_IMG = 257
        EPS = 1e-06

        def rms_norm(x, scale, eps=EPS):
            ms = jnp.mean(jnp.square(x), axis=-1, keepdims=True)
            return x * jax.lax.rsqrt(ms + eps) * scale

        def sdpa(q, k, v):
            scale = 1.0 / jnp.sqrt(jnp.asarray(D, q.dtype))
            scores = jnp.einsum('bshd,blhd->bhsl', q, k) * scale
            attn = jax.nn.softmax(scores, axis=-1)
            return jnp.einsum('bhsl,blhd->bshd', attn, v)
        B, S, _ = x.shape
        img_ctx = context[:, :N_IMG]
        txt_ctx = context[:, N_IMG:]
        q = rms_norm(x @ q_w + q_b, nq_s).reshape(B, S, H, D)
        k_txt = rms_norm(txt_ctx @ k_w + k_b, nkt_s).reshape(B, -1, H, D)
        v_txt = (txt_ctx @ v_w + v_b).reshape(B, -1, H, D)
        out_txt = sdpa(q, k_txt, v_txt)
        k_img = rms_norm(img_ctx @ ki_w + ki_b, nki_s).reshape(B, -1, H, D)
        v_img = (img_ctx @ vi_w + vi_b).reshape(B, -1, H, D)
        out_img = sdpa(q, k_img, v_img)
        out = (out_txt + out_img).reshape(B, S, INNER)
        return out @ o_w + o_b

    def _L0_ffn_ref(hidden, router_w, expert_bias, gate_w, up_w, down_w, shared_gate_w, shared_up_w, shared_down_w):
        import jax, jax.numpy as jnp
        import numpy as np
        B, S, D = (2, 256, 256)
        I = 128
        E = 32
        K = 4
        NS = 1
        ALPHA = 7.0

        def _clamped_swiglu(x, wg, wu, wd):
            g = jnp.clip(x @ wg.T, -ALPHA, ALPHA)
            u = jnp.clip(x @ wu.T, -ALPHA, ALPHA)
            return jax.nn.silu(g) * u @ wd.T
        Bb, Ss, Dd = hidden.shape
        flat = hidden.reshape(-1, Dd)
        T = flat.shape[0]
        logits = flat @ router_w.T
        scores = jnp.sqrt(jax.nn.softplus(logits))
        _, idx = jax.lax.top_k(scores + expert_bias, K)
        topv = jnp.take_along_axis(scores, idx, axis=1)
        topv = topv / (topv.sum(axis=-1, keepdims=True) + 1e-20)
        probs = jnp.zeros((T, E), flat.dtype).at[jnp.arange(T)[:, None], idx].set(topv)

        def body(acc, xs):
            wg, wu, wd, p = xs
            return (acc + p[:, None] * _clamped_swiglu(flat, wg, wu, wd), None)
        out, _ = jax.lax.scan(body, jnp.zeros_like(flat), (gate_w, up_w, down_w, probs.T))
        out = out + _clamped_swiglu(flat, shared_gate_w, shared_up_w, shared_down_w)
        return out.reshape(Bb, Ss, Dd)
    x = x + _L0_xattn_ref(_layernorm(x, axis=-1), ctx_2048, L0_xattn_q_w, L0_xattn_q_b, L0_xattn_k_w, L0_xattn_k_b, L0_xattn_v_w, L0_xattn_v_b, L0_xattn_ki_w, L0_xattn_ki_b, L0_xattn_vi_w, L0_xattn_vi_b, L0_xattn_o_w, L0_xattn_o_b, L0_xattn_nq_s, L0_xattn_nkt_s, L0_xattn_nki_s)
    x = x + _L0_ffn_ref(_layernorm(x, axis=-1), L0_ffn_router_w, L0_ffn_expert_bias, L0_ffn_gate_w, L0_ffn_up_w, L0_ffn_down_w, L0_ffn_shared_gate_w, L0_ffn_shared_up_w, L0_ffn_shared_down_w)
    return x

_drawn_inputs = setup_inputs


def setup_inputs(seed=0):
    import zlib

    import numpy as np

    out = dict(_drawn_inputs(seed))
    spreads = {'L0_xattn_q_b': (0.0, 0.1),
     'L0_xattn_k_b': (0.0, 0.8),
     'L0_xattn_v_b': (0.0, 0.1),
     'L0_xattn_ki_b': (0.0, 0.8),
     'L0_xattn_vi_b': (0.0, 0.1),
     'L0_xattn_o_b': (0.0, 0.1),
     'L0_xattn_nq_s': (1.0, 0.2),
     'L0_xattn_nkt_s': (1.0, 0.2),
     'L0_xattn_nki_s': (1.0, 0.2)}
    factors = {'L0_ffn_router_w': 8.0,
     'L0_ffn_expert_bias': 8.0,
     'L0_ffn_gate_w': 8.0,
     'L0_ffn_up_w': 8.0,
     'L0_ffn_down_w': 8.0,
     'L0_ffn_shared_gate_w': 8.0,
     'L0_ffn_shared_up_w': 8.0,
     'L0_ffn_shared_down_w': 8.0}
    for name, (base, spread) in spreads.items():
        noise = np.random.default_rng([zlib.crc32(name.encode()), seed]).standard_normal(out[name].shape)
        drawn = base * np.exp(spread * noise) if base else spread * noise
        out[name] = jnp.asarray(drawn.astype(out[name].dtype))
    for name, factor in factors.items():
        out[name] = (out[name] * factor).astype(out[name].dtype)
    return out
```

```python
import concourse.bass as bass
from concourse import mybir
from contextlib import ExitStack

F32 = mybir.dt.float32
F32R = mybir.dt.float32r
ACT = mybir.ActivationFunctionType
ALU = mybir.AluOpType
ds = bass.ds

P = 128
B, S, DIM = 16, 56, 256
NC = DIM // P
N = B * S
H, D = 16, 128
INNER = H * D
N_IMG, L = 257, 1500
GB = 4
NG = B // GB
GN = GB * S
HS = H * S
HALF = HS // 2
IMG_TILES = -(-N_IMG // P)
TXT_TILES = -(-(L - N_IMG) // P)
TILES = IMG_TILES + TXT_TILES
ROWS = [min(P, N_IMG - P * t) for t in range(IMG_TILES)] + \
       [min(P, L - N_IMG - P * t) for t in range(TXT_TILES)]
PREP = 2
UNITS = 2 * TILES
TOK = 112
NTOK = N // TOK
EPS_RMS, EPS_LN = 1e-6, 1e-5
E, K_TOP, I = 32, 4, 128
ALPHA = 7.0
SMALL = {"qb": 0, "nq": 16, "kb": 32, "nk": 64, "vb": 96, "ob": 128, "end": 130}
STAGE_RING, CTX_RING, WRING = 3, 4, 4
RANK_RING = 4
SAFE_SCORE = 79.0
CREDIT = {"scores_done": UNITS, "av_done": UNITS, "exp_done": 2, "probs_split": 2, "sum_added": 2,
          "sum_split": 4, "stage_used": TILES, "u_text_copied": 2, "o_copied": 2, "w_low": WRING, "w_used": 2, "y_done": WRING, "v_done": 2, "q_copied": 2, "squares_summed": 2,
          "q_scaled": 2, "u_copied": 2, "v_copied": 2, "v_split": 2, "y_added": 1, "recip_ready": 1, "o_scaled": 1, "norm_summed": 1, "max_tile_done": 1, "judgement_read": 1, "sum_wide": 1, "max_scores": 1}


def slot(t, ring):
    return t % ring if t < TILES - 1 else ring


def rank_slot(t):
    s = int(t >= IMG_TILES)
    start, end = (0, IMG_TILES) if s == 0 else (IMG_TILES, TILES)
    mine = lambda k: 2 * s + (k - start) % 2
    return mine(t), (0, t - 2) if t - 2 >= start else (1, max(k for k in range(start, end) if mine(k) == mine(t)))


def before(t, ring):
    if t == TILES - 1:
        return 1, t
    if t >= ring:
        return 0, t - ring
    return 1, max(k for k in range(TILES - 1) if k % ring == t)




def layer_norm(nc, ctx, tag, xT, keep, banks):
    sem = lambda n: ctx.enter_context(nc.semaphore(f"{tag}_{n}"))
    sums, mean, mean_wide, centred, squared, var, var_eps, rstd, rstd_wide = [
        sem(n) for n in ("sums", "mean", "mean_wide", "centred", "squared", "var", "var_eps", "rstd", "rstd_wide")]
    done = sem("done")
    mean_sb = ctx.enter_context(nc.sbuf_tensor(f"{tag}_mean_sb", [TOK, NTOK], F32))
    var_sb = ctx.enter_context(nc.sbuf_tensor(f"{tag}_var_sb", [TOK, NTOK], F32))
    rstd_sb = ctx.enter_context(nc.sbuf_tensor(f"{tag}_rstd_sb", [TOK, NTOK], F32))
    square = ctx.enter_context(nc.sbuf_tensor(f"{tag}_square", [P, NC, N], F32))
    compact, wide = banks[:, 0, 0:NTOK], banks[:, 1:3, 0:N // 2]

    def tensor(pe, ones, ident):
        def reduce_over_features(src, done_sem):
            for i in range(NTOK):
                for c in range(NC):
                    last = nc.tensor.matmul(compact[0:TOK, i:i + 1], src[:, c, TOK * i:TOK * i + TOK], ones[:, 0:1],
                                            start=c == 0, stop=c == NC - 1)
            last.then_inc(done_sem, 1)

        def widen(src, done_sem):
            for i in range(NTOK):
                half, at = divmod(TOK * i, N // 2)
                last = nc.tensor.matmul(wide[:, half, at:at + TOK], src[:, i:i + 1].to_broadcast([TOK, P]),
                                        ident[0:TOK, 0:TOK], start=True, stop=True)
            last.then_inc(done_sem, 1)

        reduce_over_features(xT, sums)
        pe.wait_ge(mean, 1)
        widen(mean_sb, mean_wide)
        pe.wait_ge(squared, NC)
        reduce_over_features(square, var)
        pe.wait_ge(rstd, 1)
        pe.wait_ge(centred, NC)
        widen(rstd_sb, rstd_wide)

    def vector(dve):
        dve.wait_ge(sums, 1)
        nc.vector.tensor_scalar(mean_sb[:, :], compact[0:TOK, :], 1.0 / DIM, None, ALU.mult).then_inc(mean, 1)
        dve.wait_ge(mean_wide, 1)
        for c in range(NC):
            nc.vector.tensor_tensor(keep(c), xT[:, c, :].rearrange("p (h n) -> p h n", h=2), wide,
                                    ALU.subtract).then_inc(centred, 1)
        for c in range(NC):
            dve.wait_ge(centred, c + 1)
            nc.vector.tensor_tensor(square[:, c, :].rearrange("p (h n) -> p h n", h=2), keep(c), keep(c),
                                    ALU.mult).then_inc(squared, 1)
        dve.wait_ge(var, 1)
        nc.vector.tensor_scalar(var_sb[:, :], compact[0:TOK, :], 1.0 / DIM, EPS_LN, ALU.mult, ALU.add)\
            .then_inc(var_eps, 1)
        dve.wait_ge(rstd_wide, 1)
        for c in range(NC):
            nc.vector.tensor_tensor(keep(c), keep(c), wide, ALU.mult).then_inc(done, 1)

    def pool(gp, minus_half):
        gp.wait_ge(var_eps, 1)
        nc.gpsimd.tensor_tensor(rstd_sb[:, :], var_sb[:, :], minus_half[0:TOK, 0:NTOK], ALU.pow).then_inc(rstd, 1)

    return tensor, vector, pool, done


def build(nc, xT_in, ctx_in, qw_in, kw_in, vw_in, small_in, router_in, bias_in, ffn_in, out):
    ctx = ExitStack()
    with ctx:
        def sb(name, shape, dt=F32, stack=ctx):
            return stack.enter_context(nc.sbuf_tensor(name, shape, dt))

        def sem(name, stack=ctx):
            return stack.enter_context(nc.semaphore(name))

        probs_dram = nc.dram_tensor("probs_by_expert", [E + 1, N], F32, kind="Internal").ap()
        psum = ctx.enter_context(nc.psum_tensor("psum", [P, 8, 512], F32))
        xT = sb("xT", [P, NC, N])
        ident = sb("ident", [P, P])
        ones = sb("ones", [P, P])
        minus_half = sb("minus_half", [P, 16])

        attn = ExitStack()
        with attn:
            small = sb("small", [P, SMALL["end"]], stack=attn)
            key_scale = sb("key_scale", [P, 2, H], stack=attn)
            bias_cols = sb("bias_cols", [P, H, 4], stack=attn)
            bias_high = sb("bias_high", [P, H, 4], F32R, attn)
            bias_low = sb("bias_low", [P, H, 4], F32R, attn)
            v_bias = sb("v_bias", [P, H], stack=attn)
            x_high = sb("x_high", [P, NC, N], F32R, attn)
            x_low = sb("x_low", [P, NC, N], F32R, attn)
            gram_high = sb("gram_high", [P, 2, NC, DIM], F32R, attn)
            gram_low = sb("gram_low", [P, 2, NC, DIM], F32R, attn)
            twice_wb = sb("twice_wb", [P, 2, DIM], stack=attn)
            bb_eps = sb("bb_eps", [P, 2], stack=attn)
            ones_r = sb("ones_r", [P, P], F32R, attn)
            rank_w = sb("rank_w", [P, RANK_RING, P], F32R, attn)
            prologue(nc, xT_in, kw_in, small_in, psum, xT, ident, ones, minus_half, small, key_scale, bias_cols,
                     bias_high, bias_low, v_bias, x_high, x_low, gram_high, gram_low, twice_wb, bb_eps, ones_r,
                     rank_w)
            attention(nc, ctx_in, qw_in, kw_in, vw_in, psum, xT, ident, ones, minus_half, small, key_scale,
                      bias_high, bias_low, v_bias, x_high, x_low, gram_high, gram_low, twice_wb, bb_eps, ones_r,
                      rank_w)
        experts(nc, router_in, bias_in, ffn_in, out, probs_dram, psum, xT, ident, ones, minus_half)


def prologue(nc, xT_in, kw_in, small_in, psum, xT, ident, ones, minus_half, small, key_scale, bias_cols, bias_high,
             bias_low, v_bias, x_high, x_low, gram_high, gram_low, twice_wb, bb_eps, ones_r, rank_w):
    ctx = ExitStack()
    with ctx:
        sb = lambda n, s, dt=F32: ctx.enter_context(nc.sbuf_tensor(n, s, dt))
        sem = lambda n: ctx.enter_context(nc.semaphore(n))
        KW = 4
        kw = sb("kw", [P, KW, 2 * DIM])
        xn = sb("xn", [P, NC, N])
        x_loaded, small_loaded = sem("x_loaded"), sem("small_loaded")
        kw_loaded = [sem(f"kw_loaded{i}") for i in range(KW)]
        kw_used, const_ready, ident_ready = sem("kw_used"), sem("const_ready"), sem("ident_ready")
        scale_ready, bias_ready, bias_high_ready, bias_split = (
            sem("scale_ready"), sem("bias_ready"), sem("bias_high_ready"), sem("bias_split"))
        gram_high_ready, gram_split = sem("gram_high_ready"), sem("gram_split")
        x_high_ready, x_split = sem("x_high_ready"), sem("x_split")
        ln_pe, ln_dve, ln_pool, ln_done = layer_norm(
            nc, ctx, "ln1", xT, lambda c: xn[:, c, :].rearrange("p (h n) -> p h n", h=2), psum[:, 0:3, :])
        kb = small[:, SMALL["kb"]:SMALL["kb"] + 2 * H].rearrange("p (s h) -> p s h", s=2)
        nk = small[:, SMALL["nk"]:SMALL["nk"] + 2 * H].rearrange("p (s h) -> p s h", s=2)
        nq = small[:, SMALL["nq"]:SMALL["nq"] + H]
        vb = small[:, SMALL["vb"]:SMALL["vb"] + 2 * H].rearrange("p (s h) -> p s h", s=2)
        block = ctx.enter_context(nc.Block())

        @block.sync
        def _(sp):
            sp.dma_start(xT[:, :, :], xT_in).then_inc(x_loaded, 16)
            sp.dma_start(small[:, :], small_in).then_inc(small_loaded, 16)
            for h in range(H):
                if h >= KW:
                    sp.wait_ge(kw_used, h - KW + 1)
                sp.dma_start(kw[:, h % KW, :], kw_in[h, :, :]).then_inc(kw_loaded[h % KW], 16)

        @block.gpsimd
        def _(gp):
            nc.gpsimd.memset(ident[:, :], 0.0).then_inc(ident_ready, 1)
            nc.gpsimd.memset(ones[:, :], 1.0).then_inc(const_ready, 1)
            nc.gpsimd.memset(minus_half[:, :], -0.5).then_inc(const_ready, 1)
            gp.wait_ge(ident_ready, 1)
            nc.gpsimd.affine_select(out=ident[:, :], in_=ident[:, :], compare_op=ALU.not_equal, fill=1.0, base=0,
                                    pattern=[[-1, P]], channel_multiplier=1).then_inc(const_ready, 1)
            ln_pool(gp, minus_half)

        @block.tensor
        def _(pe):
            pe.wait_ge(const_ready, 3)
            pe.wait_ge(x_loaded, 16)
            ln_pe(pe, ones, ident)
            pe.wait_ge(small_loaded, 16)
            pe.wait_ge(ln_done, NC)
            for h in range(H):
                pe.wait_ge(kw_loaded[h % KW], 16 * (h // KW + 1))
                for s in range(2):
                    w = kw[:, h % KW, s * DIM:(s + 1) * DIM]
                    b = small[:, SMALL["kb"] + s * H + h:SMALL["kb"] + s * H + h + 1]
                    flags = dict(start=h == 0, stop=h == H - 1)
                    for c in range(NC):
                        nc.tensor.matmul(psum[:, s * NC + c, 0:DIM], w[:, c * P:(c + 1) * P], w, **flags)
                    nc.tensor.matmul(psum[:, 4 + s, 0:DIM], b.to_broadcast([P, P]), w, **flags)
                    last = nc.tensor.matmul(psum[:, 6 + s, 0:1], b.to_broadcast([P, P]), b, **flags)
                last.then_inc(kw_used, 1)

        @block.scalar
        def _(act):
            act.wait_ge(bias_ready, 4)
            nc.scalar.activation(bias_high[:, :, :], bias_cols[:, :, :], ACT.Copy).then_inc(bias_high_ready, 1)
            for c in range(NC):
                act.wait_ge(ln_done, c + 1)
                nc.scalar.activation(x_high[:, c, :], xn[:, c, :], ACT.Copy).then_inc(x_high_ready, 1)
            act.wait_ge(kw_used, H)
            nc.scalar.activation(gram_high[:, :, :, :], psum[:, 0:4, 0:DIM].rearrange("p (s c) n -> p s c n", s=2),
                                 ACT.Copy).then_inc(gram_high_ready, 1)

        @block.vector
        def _(dve):
            dve.wait_ge(const_ready, 1)
            nc.vector.tensor_copy(ones_r[:, :], ones[:, :])
            nc.vector.tensor_scalar(rank_w[:, :, :], ones[:, 0:1].to_broadcast([P, RANK_RING, P]), 0.0, None,
                                    ALU.mult).then_inc(scale_ready, 1)
            dve.wait_ge(scale_ready, 1)
            for s in range(2):
                for row in (32 * s, 64 + 32 * s):
                    nc.vector.tensor_copy(rank_w[row:row + 1, 2 * s:2 * s + 2, :],
                                          ones[row:row + 1, :].unsqueeze(1).to_broadcast([1, 2, P]))\
                        .then_inc(scale_ready, 1)
            dve.wait_ge(small_loaded, 16)
            for s in range(2):
                nc.vector.scalar_tensor_tensor(key_scale[:, s, :], nk[:, s, :], float(D) ** -0.5, nq, ALU.mult,
                                               ALU.mult).then_inc(scale_ready, 1)
            dve.wait_ge(scale_ready, 7)
            for s in range(2):
                for i in range(2):
                    nc.vector.tensor_tensor(bias_cols[:, :, s + 2 * i], kb[:, s, :], key_scale[:, s, :], ALU.mult)\
                        .then_inc(bias_ready, 1)
            nc.vector.tensor_tensor(v_bias[:, :], vb[:, 0, :], vb[:, 1, :], ALU.add).then_inc(scale_ready, 1)
            dve.wait_ge(bias_high_ready, 1)
            dve.wait_ge(bias_ready, 4)
            nc.vector.tensor_tensor(bias_low[:, :, :], bias_cols[:, :, :], bias_high[:, :, :].bitcast(F32),
                                    ALU.subtract).then_inc(bias_split, 1)
            ln_dve(dve)
            for c in range(NC):
                dve.wait_ge(x_high_ready, c + 1)
                nc.vector.tensor_tensor(x_low[:, c, :], xn[:, c, :], x_high[:, c, :].bitcast(F32), ALU.subtract)\
                    .then_inc(x_split, 1)
            dve.wait_ge(gram_high_ready, 1)
            nc.vector.tensor_tensor(gram_low[:, :, :, :].rearrange("p s c n -> p (s c) n"), psum[:, 0:4, 0:DIM],
                                    gram_high[:, :, :, :].bitcast(F32).rearrange("p s c n -> p (s c) n"),
                                    ALU.subtract).then_inc(gram_split, 1)
            nc.vector.tensor_scalar(twice_wb[:, :, :], psum[:, 4:6, 0:DIM], 2.0, None, ALU.mult).then_inc(gram_split, 1)
            nc.vector.tensor_scalar(bb_eps[:, :], psum[:, 6:8, 0], 1.0 / INNER, EPS_RMS, ALU.mult, ALU.add)\
                .then_inc(gram_split, 1)


def attention(nc, ctx_in, qw_in, kw_in, vw_in, psum, xT, ident, ones, minus_half, small, key_scale, bias_high,
              bias_low, v_bias, x_high, x_low, gram_high, gram_low, twice_wb, bb_eps, ones_r, rank_w):
    ctx = ExitStack()
    with ctx:
        sb = lambda n, s, dt=F32: ctx.enter_context(nc.sbuf_tensor(n, s, dt))
        names = {}

        def sem(n):
            names[n] = ctx.enter_context(nc.semaphore(n))
            return names[n]

        rows_uo = sb("rows_uo", [P, GB * 4, HS])
        rank_rows = sb("rank_rows", [P, GB, HS], F32R)
        q_raw = sb("q_raw", [P, H, GN])
        q_square = sb("q_square", [P, 2, GN])
        square_w = sb("square_w", [P, H, 3])
        bound_sq = sb("bound_sq", [TOK, 2])
        bound_max = sb("bound_max", [TOK, 1])
        bound_row = sb("bound_row", [1, 1])
        is_safe = sb("is_safe", [1, 1], mybir.dt.int32)
        q_sum = sb("q_sum", [TOK, 2])
        q_ms = sb("q_ms", [TOK, 2])
        q_rms = sb("q_rms", [TOK, 2])
        q_rms_wide = sb("q_rms_wide", [P, GN])
        q_hat = sb("q_hat", [P, 2, GN])
        v_out = q_hat
        bias_wide_high = sb("bias_wide_high", [P, 2, P], F32R)
        bias_wide_low = sb("bias_wide_low", [P, 2, P], F32R)
        v_high = sb("v_high", [P, 2, GN], F32R)
        v_low = sb("v_low", [P, 2, GN], F32R)
        VCOLS = 3 * DIM
        w_stage = sb("w_stage", [P, WRING, 2 * DIM])
        v_stage = q_raw[:, :, :].rearrange("p h n -> p (h n)")[:, 0:WRING * VCOLS].rearrange("p (r n) -> p r n", r=WRING)
        UCOLS = 2 * NC * HS
        WCOLS, OCOLS, RCOLS = 2 * 2 * DIM, WRING * DIM, 2 * 4 * GN
        shared = sb("shared", [P, 2, max(UCOLS, WCOLS + OCOLS + RCOLS)], F32R)
        u_high, u_low = [shared[:, i, 0:UCOLS].rearrange("p (r n) -> p r n", r=4) for i in range(2)]
        w_high, w_low = [shared[:, i, 0:WCOLS].rearrange("p (r n) -> p r n", r=2) for i in range(2)]
        ow_high, ow_low = [shared[:, i, WCOLS:WCOLS + OCOLS].rearrange("p (r n) -> p r n", r=WRING) for i in range(2)]
        r_high, r_low = [shared[:, i, WCOLS + OCOLS:WCOLS + OCOLS + RCOLS].rearrange("p (r n) -> p r n", r=2)
                         for i in range(2)]
        stage = sb("stage", [P, STAGE_RING + 1, 2 * DIM])
        c_high = sb("c_high", [P, CTX_RING + 1, 2 * DIM], F32R)
        c_low = sb("c_low", [P, CTX_RING + 1, 2 * DIM], F32R)
        c_twice = sb("c_twice", [P, 2, DIM])
        junk = sb("junk", [P, 2, DIM], mybir.dt.bfloat16)
        key_lin = sb("key_lin", [P, 2])
        key_ms = sb("key_ms", [P, TILES])
        key_rms = sb("key_rms", [P, TILES])
        probs = sb("probs", [P, 2, HALF])
        p_high = sb("p_high", [P, 2, HALF], F32R)
        p_low = sb("p_low", [P, 2, HALF], F32R)
        zeros = sb("zeros", [P, 1])
        p_sum = sb("p_sum", [P, 4, HALF])
        p_sum_high = sb("p_sum_high", [P, HALF], F32R)
        p_sum_low = sb("p_sum_low", [P, HALF], F32R)
        recip = sb("recip", [P, HALF])

        BOUND_STEPS, START_STEPS = 5, 9
        O, SC, GRAM, SUM = 0, 4, 6, 7

        inverse_dram = nc.dram_tensor("inverse_rms", [B * TILES, 2, P], F32, kind="Internal").ap()
        negative_dram = nc.dram_tensor("negative_maxima", [B, 2 * HS // P, P], F32, kind="Internal").ap()
        flat = q_raw[:, :, :].rearrange("p h n -> p (h n)")
        max_run = flat[:, 0:2 * HS].rearrange("p (s n) -> p s n", s=4)
        max_twice = flat[:, 2 * HS:2 * HS + DIM]
        at = 2 * HS + DIM
        max_lin, max_ms, max_root, max_inverse = [flat[:, at + TILES * i:at + TILES * (i + 1)] for i in range(4)]
        max_cols = flat[:, at + 4 * TILES:at + 4 * TILES + 2 * HS // P]
        inverse = p_low[:, 0, 0:2 * TILES].rearrange("p (t r) -> p t r", r=2)
        negative = p_low[:, 1, 0:2 * HS // P]
        MAX_SLOT = 2
        (max_loaded, max_high, max_low, max_terms, max_scores, max_summed, max_rooted, max_tile_done, max_u_high,
         max_u_split, max_flipped, max_steps, max_found, max_listed, max_stored) = [sem(f"max_{n}") for n in (
             "loaded", "high", "low", "terms", "scores", "summed", "rooted", "tile_done", "u_high", "u_split",
             "flipped", "steps", "found", "listed", "stored")]
        start_ready = sem("start_ready")
        ctx_loaded = [sem(f"ctx_loaded{i}") for i in range(STAGE_RING + 1)]
        w_loaded = [sem(f"w_loaded{i}") for i in range(WRING)]
        rank_loaded = [sem(f"rank_loaded{i}") for i in range(RANK_RING)]
        zeros_stored = sem("zeros_stored")
        ctx_high, ctx_low, ctx_twice, stage_used = sem("ctx_high"), sem("ctx_low"), sem("ctx_twice"), sem("stage_used")
        gram_done, norm_summed, key_norm = sem("gram_done"), sem("norm_summed"), sem("key_norm")
        u_high_ready, u_split = sem("u_high_ready"), sem("u_split")
        scores_done, exp_done, probs_split, av_done = (
            sem("scores_done"), sem("exp_done"), sem("probs_split"), sem("av_done"))
        sum_added, sum_high_ready, sum_split = sem("sum_added"), sem("sum_high_ready"), sem("sum_split")
        sum_wide, recip_ready, o_copied, o_scaled = sem("sum_wide"), sem("recip_ready"), sem("o_copied"), sem("o_scaled")
        q_w_high_ready, w_high_ready, w_low_ready, w_used = sem("q_w_high_ready"), sem("w_high_ready"), sem("w_low"), sem("w_used")
        q_copied, squares_summed, q_reduced = sem("q_copied"), sem("squares_summed"), sem("q_reduced")
        bound_step, bound_flat, safe_known, judgement_read = (
            sem("bound_step"), sem("bound_flat"), sem("safe_known"), sem("judgement_read"))
        q_ms_ready, q_rms_ready, q_wide, q_wide_copied = (
            sem("q_ms_ready"), sem("q_rms_ready"), sem("q_wide"), sem("q_wide_copied"))
        q_scaled, q_high_ready, q_split, bias_copied = (
            sem("q_scaled"), sem("q_high_ready"), sem("q_split"), sem("bias_copied"))
        u_done, u_copied, rank_copied, u_text_copied = (
            sem("u_done"), sem("u_copied"), sem("rank_copied"), sem("u_text_copied"))
        o_high_ready, o_split, v_done, v_copied, v_high_ready, v_split = (
            sem("o_high_ready"), sem("o_split"), sem("v_done"), sem("v_copied"), sem("v_high_ready"), sem("v_split"))
        y_done, y_added = sem("y_done"), sem("y_added")
        block = ctx.enter_context(nc.Block())

        def last_unit_of_buffer(it, t):
            back, k = before(t, CTX_RING)
            return UNITS * (it - back) + 2 * k + 2 + CREDIT["av_done"]

        def w_index(g, phase, h):
            return 3 * H * g + H * phase + h

        def batches(eng, g, body, tail):
            body(GB * g, 0, False, True)
            with eng.Fori(1, GB - 1) as j:
                body(GB * g + j, j, True, True)
            body(GB * g + GB - 1, GB - 1, True, False)
            tail(GB * g + GB, GB)

        def heads(eng, main, prepare=None, first=True):
            def step(quad, i, last):
                if prepare is not None and not (last and i == WRING - 1):
                    n = i + 1
                    prepare(WRING * quad + n, n % 2, n % WRING, quad + n // WRING)
                main(WRING * quad + i, i % 2, i, quad)
            if prepare is not None and first:
                prepare(0, 0, 0, 0)
            with eng.Fori(0, H // WRING - 1) as quad:
                for i in range(WRING):
                    step(quad, i, False)
            for i in range(WRING):
                step(H // WRING - 1, i, True)

        def where_unsafe(eng, g, maxima, no_maxima):
            eng.wait_ge(safe_known, g + 1)
            eng.sem_inc(judgement_read, 1)
            safe = eng.value_load(is_safe[0:1, 0:1], min_val=0, max_val=1)
            eng.sem_inc(judgement_read, 1)
            with eng.If(safe == 0):
                with eng.Fori(0, GB) as j:
                    maxima(GB * g + j, j)
            with eng.Else():
                no_maxima()

        def ahead(it, t):
            return (it, t) if t < TILES else (it + 1, t - TILES)

        @block.sync
        def _(sp):
            def load_tile(it, t):
                back, k = before(t, STAGE_RING)
                sp.wait_ge(stage_used, TILES * (it - back) + k + 1 + CREDIT["stage_used"])
                sp.dma_start(stage[:, slot(t, STAGE_RING), :], ctx_in[ds(TILES * it + t, 1), :, :]
                             .rearrange("a p n -> p (a n)")).then_inc(ctx_loaded[slot(t, STAGE_RING)], 16)

            def load_weights(g, phase, src, stage_of, cols):
                def load(h, par, i, nth):
                    sp.wait_ge(w_low_ready, w_index(g, phase, h) - WRING + 1 + CREDIT["w_low"])
                    sp.dma_start(stage_of[:, i, 0:cols], src[ds(h, 1), :, :].rearrange("a p n -> p (a n)"))\
                        .then_inc(w_loaded[i], 16)
                heads(sp, load)

            def load_rank(it, t):
                i, (back, k) = rank_slot(t)
                sp.wait_ge(scores_done, UNITS * (it - back) + 2 * k + 2 + CREDIT["scores_done"])
                row = 32 * (i // 2) + 1
                sp.dma_start(rank_w[row:row + 2, i, :].bitcast(F32), inverse_dram[ds(TILES * it + t, 1), :, :]
                             .rearrange("a r n -> (a r) n")).then_inc(rank_loaded[i], 16)

            def maxima(it, bl):
                for t in range(TILES):
                    sp.wait_ge(max_tile_done, TILES * it + t + CREDIT["max_tile_done"])
                    sp.dma_start(stage[:, MAX_SLOT, :], ctx_in[ds(TILES * it + t, 1), :, :]
                                 .rearrange("a p n -> p (a n)")).then_inc(max_loaded, 16)
                sp.wait_ge(max_found, it + 1)
                sp.dma_start(negative_dram[ds(it, 1), :, :].rearrange("a k n -> n (a k)"), negative.bitcast(F32),
                             allow_slow_non_contiguous=True)\
                    .then_inc(max_listed, 16)
                sp.dma_start(inverse_dram[ds(TILES * it, TILES), :, :].rearrange("t r n -> n t r"), inverse.bitcast(F32),
                             allow_slow_non_contiguous=True)\
                    .then_inc(max_listed, 16)
                sp.wait_ge(max_listed, 32 * (it + 1))
                for s in range(2):
                    for row in (32 * s + 1, 32 * s + 2):
                        sp.dma_start(rank_rows[row:row + 1, ds(bl, 1), :].rearrange("p a n -> p (a n)").bitcast(F32),
                                     negative_dram[ds(it, 1), 7 * s:7 * s + 7, :].rearrange("a k n -> a (k n)"))\
                            .then_inc(max_stored, 16)

            def no_maxima():
                sp.sem_inc(max_loaded, 16 * GB * TILES)
                sp.sem_inc(max_listed, 32 * GB)
                sp.sem_inc(max_stored, 64 * GB)

            sp.wait_ge(start_ready, START_STEPS)
            sp.dma_start(inverse_dram.rearrange("a r n -> (a r n)").rearrange("(p n) -> p n", p=P),
                         p_sum[:, :, :].rearrange("p a n -> p (a n)")[:, 0:B * TILES * 2]).then_inc(zeros_stored, 16)
            for t in range(PREP):
                load_tile(0, t)
            sp.wait_ge(zeros_stored, 16)
            with sp.Fori(0, NG) as g:
                load_weights(g, 0, qw_in, w_stage, DIM)
                load_weights(g, 1, kw_in, w_stage, 2 * DIM)
                where_unsafe(sp, g, maxima, no_maxima)
                with sp.Fori(0, GB) as j:
                    load_rank(GB * g + j, 0)
                    for t in range(TILES):
                        load_tile(*ahead(GB * g + j, t + PREP))
                        if t + 1 < TILES:
                            load_rank(GB * g + j, t + 1)
                load_weights(g, 2, vw_in, v_stage, VCOLS)

        @block.tensor
        def _(pe):
            pe.sem_inc(scores_done, CREDIT["scores_done"])
            pe.sem_inc(av_done, CREDIT["av_done"])
            pe.sem_inc(w_used, CREDIT["w_used"])
            pe.sem_inc(v_done, CREDIT["v_done"])
            pe.sem_inc(squares_summed, CREDIT["squares_summed"])
            pe.sem_inc(y_done, CREDIT["y_done"])
            pe.sem_inc(sum_wide, CREDIT["sum_wide"])
            pe.sem_inc(max_scores, CREDIT["max_scores"])

            def three(out, high, low, rhigh, rlow, start, stop):
                nc.tensor.matmul(out, high, rhigh, start=start, stop=False)
                nc.tensor.matmul(out, high, rlow, start=False, stop=False)
                return nc.tensor.matmul(out, low, rhigh, start=False, stop=stop)

            def queries(g):
                def products(h, par, i, nth):
                    pe.wait_ge(w_low_ready, w_index(g, 0, h) + 1 + CREDIT["w_low"])
                    pe.wait_ge(q_copied, H * g + h - 1 + CREDIT["q_copied"])
                    for c in range(NC):
                        cols = slice(c * P, (c + 1) * P)
                        last = three(psum[:, par, 0:GN], w_high[:, par, cols], w_low[:, par, cols],
                                     x_high[:, c, ds(GN * g, GN)], x_low[:, c, ds(GN * g, GN)],
                                     c == 0, c == NC - 1)
                    last.then_inc(w_used, 1)

                def squares(h, par, i, nth):
                    pe.wait_ge(q_copied, H * g + h + 1 + CREDIT["q_copied"])
                    for i in range(2):
                        last = nc.tensor.matmul(psum[0:TOK, 2, ds(3 * H * i + 3 * h, 3)],
                                                q_square[:, par, TOK * i:TOK * i + TOK],
                                                square_w[:, ds(h, 1), :].rearrange("p a n -> p (a n)"),
                                                start=True, stop=True)
                    last.then_inc(squares_summed, 1)
                heads(pe, squares, products)
                pe.wait_ge(q_rms_ready, g + 1)
                for i in range(2):
                    last = nc.tensor.matmul(psum[:, 3, TOK * i:TOK * i + TOK],
                                            q_rms[:, i:i + 1].to_broadcast([TOK, P]), ident[0:TOK, 0:TOK],
                                            start=True, stop=True)
                last.then_inc(q_wide, 1)
                pe.wait_ge(bound_step, BOUND_STEPS * g + 4)
                pe.wait_ge(recip_ready, 4 * GB * g + CREDIT["recip_ready"])
                nc.tensor.matmul(psum[0:1, SUM, 0:TOK], bound_max[:, :], ident[0:TOK, 0:TOK], start=True, stop=True)\
                    .then_inc(bound_flat, 1)

            def absorb(g):
                def products(h, par, i, nth):
                    pe.wait_ge(q_wide_copied, g + 1)
                    pe.wait_ge(w_low_ready, w_index(g, 1, h) + 1 + CREDIT["w_low"])
                    pe.wait_ge(q_split, H * g + h + 1)
                    pe.wait_ge(u_copied, H * g + h - 1 + CREDIT["u_copied"])
                    pe.wait_ge(u_text_copied, H * g + h - 1 + CREDIT["u_text_copied"])
                    for s in range(2):
                        for c in range(NC):
                            cols = slice(s * DIM + c * P, s * DIM + (c + 1) * P)
                            three(psum[:, 2 * par + s, c * GN:(c + 1) * GN], w_high[:, par, cols],
                                  w_low[:, par, cols], r_high[:, par, 0:GN], r_low[:, par, 0:GN], True, True)
                    three(psum[:, 4 + par, 0:GN], bias_wide_high[:, par, :], bias_wide_low[:, par, :],
                          r_high[:, par, 0:GN], r_low[:, par, 0:GN], True, True).then_inc(w_used, 1)
                heads(pe, products)

            def gram(it, t):
                s = int(t >= IMG_TILES)
                k = slot(t, CTX_RING)
                pe.wait_ge(ctx_high, TILES * it + t + 1)
                pe.wait_ge(norm_summed, TILES * it + t + CREDIT["norm_summed"])
                for c in range(NC):
                    for i, part in enumerate((gram_high, gram_low)):
                        last = nc.tensor.matmul(psum[:, GRAM, 0:DIM], c_high[:, k, c * P:(c + 1) * P],
                                                part[:, s, c, :], start=c == 0 and i == 0, stop=c == 1 and i == 1)
                last.then_inc(gram_done, 1)

            def scores(it, bl, u):
                t, half = divmod(u, 2)
                s, k = int(t >= IMG_TILES), slot(t, CTX_RING)
                cols = slice(half * HALF, (half + 1) * HALF)
                if t in (0, IMG_TILES):
                    pe.wait_ge(u_split, 4 * it + 2 * s + half + 1)
                if half == 0:
                    pe.wait_ge(ctx_low, TILES * it + t + 1)
                    i = rank_slot(t)[0]
                    of_slot = [x for x in range(TILES) if rank_slot(x)[0] == i]
                    pe.wait_ge(rank_loaded[i], 16 * (len(of_slot) * it + of_slot.index(t) + 1))
                pe.wait_ge(exp_done, UNITS * it + u - 1 + CREDIT["exp_done"])
                out = psum[:, SC + half, 0:HALF]
                for c in range(NC):
                    w = slice(c * P, (c + 1) * P)
                    three(out, c_high[:, k, w], c_low[:, k, w], u_high[:, 2 * s + c, cols], u_low[:, 2 * s + c, cols],
                          c == 0, False)
                nc.tensor.matmul(out, rank_w[:, rank_slot(t)[0], :], rank_rows[:, ds(bl, 1), cols].rearrange("p a n -> p (a n)"),
                                 start=False, stop=True).then_inc(scores_done, 1)

            def average(it, u):
                t, half = divmod(u, 2)
                s, k, n = int(t >= IMG_TILES), slot(t, CTX_RING), ROWS[t]
                pe.wait_ge(probs_split, UNITS * it + u + 1 + CREDIT["probs_split"])
                first, last_tile = t in (0, IMG_TILES), t in (IMG_TILES - 1, TILES - 1)
                if first:
                    pe.wait_ge(o_copied, 4 * it + 2 * s + half - 1 + CREDIT["o_copied"])
                for c in range(NC):
                    w = slice(DIM + c * P, DIM + (c + 1) * P)
                    last = three(psum[:, O + 2 * half + c, 0:HALF], c_high[0:n, k, w], c_low[0:n, k, w],
                                 p_high[0:n, half, :], p_low[0:n, half, :], first, last_tile)
                last.then_inc(av_done, 1)

            def sums(it, s, half):
                n = 4 * it + 2 * s + half
                pe.wait_ge(sum_split, n + 1 + CREDIT["sum_split"])
                pe.wait_ge(recip_ready, n + CREDIT["recip_ready"])
                nc.tensor.matmul(psum[:, SUM, 0:HALF], ones_r[:, :], p_sum_high[:, :], start=True, stop=False)
                nc.tensor.matmul(psum[:, SUM, 0:HALF], ones_r[:, :], p_sum_low[:, :], start=False, stop=True)\
                    .then_inc(sum_wide, 1)

            def carried(it, step):
                if step < 2:
                    average(it - 1, UNITS - 2 + step)
                if step == 3:
                    sums(it - 1, 1, 0)
                if step == 7:
                    sums(it - 1, 1, 1)

            def body(it, bl, has_prev, has_next):
                for step in range(UNITS):
                    if step % 2 == 0:
                        gram(*ahead(it, step // 2 + 1))
                    scores(it, bl, step)
                    if step >= 2:
                        average(it, step - 2)
                    if has_prev:
                        carried(it, step)
                    if step == 10:
                        sums(it, 0, 0)
                    if step == 14:
                        sums(it, 0, 1)

            def tail(it, bl):
                for step in range(8):
                    carried(it, step)

            def outputs(g):
                def values(h, par, i, nth):
                    pe.wait_ge(w_low_ready, w_index(g, 2, h) + 1 + CREDIT["w_low"])
                    pe.wait_ge(o_split, H * g + h + 1)
                    pe.wait_ge(v_copied, H * g + h - 1 + CREDIT["v_copied"])
                    for k in range(4):
                        cols, r = slice(k * P, (k + 1) * P), slice(k * GN, (k + 1) * GN)
                        last = three(psum[:, par, 0:GN], w_high[:, par, cols], w_low[:, par, cols],
                                     r_high[:, par, r], r_low[:, par, r], k == 0, k == 3)
                    last.then_inc(v_done, 1)

                def project(h, par, i, start, stop):
                    pe.wait_ge(v_split, H * g + h + 1 + CREDIT["v_split"])
                    for c in range(NC):
                        cols = slice(c * P, (c + 1) * P)
                        last = three(psum[:, 4 + c, 0:GN], ow_high[:, i, cols], ow_low[:, i, cols],
                                     v_high[:, par, :], v_low[:, par, :], start, stop)
                    last.then_inc(y_done, 1)

                values(0, 0, 0, 0)
                values(1, 1, 1, 0)
                project(0, 0, 0, True, False)
                with pe.Fori(0, H // WRING - 1) as quad:
                    for n in range(WRING):
                        values(WRING * quad + n + 2, n % 2, (n + 2) % WRING, 0)
                        project(WRING * quad + n + 1, (n + 1) % 2, (n + 1) % WRING, False, False)
                for h in range(H - 2, H):
                    values(h, h % 2, h % WRING, 0)
                    project(h - 1, (h - 1) % 2, (h - 1) % WRING, False, False)
                project(H - 1, 1, WRING - 1, False, True)

            def maxima(it, bl):
                pe.wait_ge(max_u_split, it + 1)
                for t in range(TILES):
                    s = int(t >= IMG_TILES)
                    pe.wait_ge(max_low, TILES * it + t + 1)
                    pe.wait_ge(max_tile_done, TILES * it + t + CREDIT["max_tile_done"])
                    for c in range(NC):
                        for i, part in enumerate((gram_high, gram_low)):
                            nc.tensor.matmul(psum[:, GRAM, 0:DIM], c_high[:, MAX_SLOT, c * P:(c + 1) * P],
                                             part[:, s, c, :], start=c == 0 and i == 0, stop=c == 1 and i == 1)
                    for half in range(2):
                        cols = slice(half * HALF, (half + 1) * HALF)
                        out = psum[:, SC + half, 0:HALF]
                        for c in range(NC):
                            w = slice(c * P, (c + 1) * P)
                            three(out, c_high[:, MAX_SLOT, w], c_low[:, MAX_SLOT, w], u_high[:, 2 * s + c, cols],
                                  u_low[:, 2 * s + c, cols], c == 0, False)
                        last = nc.tensor.matmul(out, rank_w[:, 2 * s, :], rank_rows[:, ds(bl, 1), cols]
                                                .rearrange("p a n -> p (a n)"), start=False, stop=True)
                    last.then_inc(max_scores, 1)
                pe.wait_ge(max_tile_done, TILES * (it + 1) + CREDIT["max_tile_done"])
                run = max_run.rearrange("p s n -> p (s n)")
                for k in range(2 * HS // P):
                    last = nc.tensor.transpose(psum[:, k // 4, (k % 4) * P:(k % 4 + 1) * P], run[:, k * P:(k + 1) * P],
                                               ident[:, :])
                last.then_inc(max_flipped, 1)
                pe.wait_ge(max_stored, 64 * (it + 1))

            def no_maxima():
                pe.sem_inc(max_scores, GB * TILES)
                pe.sem_inc(max_flipped, GB)

            pe.wait_ge(start_ready, START_STEPS)
            for t in range(PREP - 1):
                gram(0, t)
            with pe.Fori(0, NG) as g:
                pe.wait_ge(y_added, g + CREDIT["y_added"])
                queries(g)
                absorb(g)
                pe.wait_ge(u_copied, H * (g + 1) + CREDIT["u_copied"])
                pe.wait_ge(u_text_copied, H * (g + 1) + CREDIT["u_text_copied"])
                where_unsafe(pe, g, maxima, no_maxima)
                batches(pe, g, body, tail)
                pe.wait_ge(o_copied, 4 * GB * (g + 1) + CREDIT["o_copied"])
                outputs(g)

        @block.scalar
        def _(act):
            act.sem_inc(exp_done, CREDIT["exp_done"])
            act.sem_inc(q_copied, CREDIT["q_copied"])
            act.sem_inc(u_copied, CREDIT["u_copied"])
            act.sem_inc(v_copied, CREDIT["v_copied"])
            act.sem_inc(o_copied, CREDIT["o_copied"])

            def copy(out, in_, **kw):
                return nc.scalar.activation(out, in_, ACT.Copy, **kw)

            def loaded(g, phase, i, nth):
                act.wait_ge(w_loaded[i], 16 * (3 * (H // WRING) * g + (H // WRING) * phase + nth + 1))

            def queries(g):
                act.wait_ge(w_low_ready, w_index(g, 0, 0) + CREDIT["w_low"])

                def take(h, par, i, nth):
                    bias = small[:, ds(SMALL["qb"] + h, 1)]
                    act.wait_ge(w_used, 2 * H * g + h + 1 + CREDIT["w_used"])
                    act.wait_ge(squares_summed, H * g + h - 1 + CREDIT["squares_summed"])
                    nc.scalar.activation(q_square[:, par, :], psum[:, par, 0:GN], ACT.Square, bias=bias)
                    nc.scalar.activation(q_raw[:, ds(h, 1), :].rearrange("p a n -> p (a n)"), psum[:, par, 0:GN],
                                         ACT.Identity, bias=bias).then_inc(q_copied, 1)
                heads(act, take)
                act.wait_ge(q_wide, g + 1)
                copy(q_rms_wide[:, :], psum[:, 3, 0:GN]).then_inc(q_wide_copied, 1)

            def absorb(g):
                def ready(h, par, i, nth):
                    loaded(g, 1, i, nth)
                    act.wait_ge(w_used, 2 * H * g + H + h - 1 + CREDIT["w_used"])
                    for s in range(2):
                        last = copy(w_high[:, par, s * DIM:(s + 1) * DIM], w_stage[:, i, s * DIM:(s + 1) * DIM],
                                    scale=key_scale[:, s, ds(h, 1)])
                    last.then_inc(w_high_ready, 1)
                    act.wait_ge(q_scaled, H * g + h + 1 + CREDIT["q_scaled"])
                    copy(r_high[:, par, 0:GN], q_hat[:, par, :]).then_inc(q_high_ready, 1)

                def take(h, par, i, nth):
                    act.wait_ge(w_used, 2 * H * g + H + h + 1 + CREDIT["w_used"])
                    copy(rank_rows[:, :, ds(h * S, S)], psum[:, 4 + par, 0:GN].rearrange("p (b q) -> p b q", b=GB))\
                        .then_inc(rank_copied, 1)
                    uo = rows_uo[:, :, ds(h * S, S)].rearrange("p (b r) q -> p r b q", b=GB)
                    for c in range(NC):
                        last = copy(uo[:, c, :, :],
                                    psum[:, 2 * par, c * GN:(c + 1) * GN].rearrange("p (b q) -> p b q", b=GB))
                    last.then_inc(u_copied, 1)
                heads(act, take, ready)

            def prepare(it, t):
                k, st = slot(t, CTX_RING), slot(t, STAGE_RING)
                per = len([x for x in range(TILES) if slot(x, STAGE_RING) == st])
                nth = len([x for x in range(t) if slot(x, STAGE_RING) == st])
                act.wait_ge(ctx_loaded[st], 16 * (per * it + nth + 1))
                act.wait_ge(av_done, last_unit_of_buffer(it, t))
                copy(c_high[:, k, :], stage[:, st, :]).then_inc(ctx_high, 1)

            def split_u(it, bl, s, half):
                last = UNITS * (it - 1) + (2 * IMG_TILES if s == 0 else UNITS)
                act.wait_ge(scores_done, last + CREDIT["scores_done"])
                cols = slice(half * HALF, (half + 1) * HALF)
                copy(u_high[:, 2 * s:2 * s + 2, cols], rows_uo[:, ds(4 * bl + 2 * s, 2), cols])\
                    .then_inc(u_high_ready, 1)

            def exponentials(it, u):
                t, half = divmod(u, 2)
                act.wait_ge(scores_done, UNITS * it + u + 1 + CREDIT["scores_done"])
                if half == 0:
                    act.wait_ge(key_norm, TILES * it + t + 1)
                act.wait_ge(av_done, UNITS * it + u - 1 + CREDIT["av_done"])
                act.wait_ge(probs_split, UNITS * it + u - 1 + CREDIT["probs_split"])
                act.wait_ge(sum_added, UNITS * it + u - 1 + CREDIT["sum_added"])
                src = psum[:, SC + half, 0:HALF]
                nc.scalar.activation(p_high[:, half, :], src, ACT.Exp, scale=key_rms[:, t:t + 1])
                nc.scalar.activation(probs[:, half, :], src, ACT.Exp, scale=key_rms[:, t:t + 1]).then_inc(exp_done, 1)

            def copy_o(it, bl, s, half):
                last = 2 * (IMG_TILES if s == 0 else TILES) - 2 + half
                act.wait_ge(av_done, UNITS * it + last + 1 + CREDIT["av_done"])
                act.wait_ge(u_split, 4 * it + 2 * s + half + 1)
                cols = slice(half * HALF, (half + 1) * HALF)
                copy(rows_uo[:, ds(4 * bl + 2 * s, 2), cols], psum[:, O + 2 * half:O + 2 * half + 2, 0:HALF])\
                    .then_inc(o_copied, 1)

            def carried(it, bl, step):
                if step == 0:
                    exponentials(it - 1, UNITS - 1)
                if step in (1, 2):
                    copy_o(it - 1, bl - 1, 1, step - 1)

            def body(it, bl, has_prev, has_next):
                if not has_prev:
                    for half in range(2):
                        split_u(it, bl, 0, half)
                for step in range(UNITS):
                    if has_prev:
                        carried(it, bl, step)
                    if step >= 1:
                        exponentials(it, step - 1)
                    if step % 2 == 0:
                        prepare(*ahead(it, step // 2 + PREP))
                    if step in (1, 2):
                        split_u(it, bl, 1, step - 1)
                    if step in (7, 8):
                        copy_o(it, bl, 0, step - 7)
                    if has_next and step in (16, 18):
                        split_u(it + 1, bl + 1, 0, (step - 16) // 2)

            def tail(it, bl):
                for step in range(3):
                    carried(it, bl, step)

            def outputs(g):
                def ready(h, par, i, nth):
                    loaded(g, 2, i, nth)
                    act.wait_ge(v_done, H * g + h - 1 + CREDIT["v_done"])
                    act.wait_ge(y_done, H * g + h - WRING + 1 + CREDIT["y_done"])
                    copy(w_high[:, par, :], v_stage[:, i, 0:2 * DIM])
                    copy(ow_high[:, i, :], v_stage[:, i, 2 * DIM:VCOLS]).then_inc(w_high_ready, 1)
                    act.wait_ge(o_scaled, 4 * GB * (g + 1) + CREDIT["o_scaled"])
                    uo = rows_uo[:, :, ds(h * S, S)].rearrange("p (b r) q -> p r b q", b=GB)
                    copy(r_high[:, par, :].rearrange("p (r b q) -> p r b q", r=4, b=GB), uo).then_inc(o_high_ready, 1)

                def take(h, par, i, nth):
                    act.wait_ge(v_done, H * g + h + 1 + CREDIT["v_done"])
                    act.wait_ge(v_split, H * g + h - 1 + CREDIT["v_split"])
                    nc.scalar.activation(v_out[:, par, :], psum[:, par, 0:GN], ACT.Identity,
                                         bias=v_bias[:, ds(h, 1)]).then_inc(v_copied, 1)
                heads(act, take, ready)

            def maxima(it, bl):
                act.wait_ge(max_scores, TILES * it + CREDIT["max_scores"])
                copy(u_high[:, :, :], rows_uo[:, ds(4 * bl, 4), :]).then_inc(max_u_high, 1)
                for t in range(TILES):
                    act.wait_ge(max_loaded, 16 * (TILES * it + t + 1))
                    act.wait_ge(max_scores, TILES * it + t + CREDIT["max_scores"])
                    copy(c_high[:, MAX_SLOT, :], stage[:, MAX_SLOT, :]).then_inc(max_high, 1)
                act.wait_ge(max_scores, TILES * (it + 1) + CREDIT["max_scores"])
                act.wait_ge(max_stored, 64 * (it + 1))

            def no_maxima():
                act.sem_inc(max_u_high, GB)
                act.sem_inc(max_high, GB * TILES)

            for t in range(PREP):
                prepare(0, t)
            with act.Fori(0, NG) as g:
                queries(g)
                absorb(g)
                act.wait_ge(u_copied, H * (g + 1) + CREDIT["u_copied"])
                act.wait_ge(u_text_copied, H * (g + 1) + CREDIT["u_text_copied"])
                where_unsafe(act, g, maxima, no_maxima)
                batches(act, g, body, tail)
                outputs(g)

        @block.vector
        def _(dve):
            dve.sem_inc(probs_split, CREDIT["probs_split"])
            dve.sem_inc(stage_used, CREDIT["stage_used"])
            dve.sem_inc(u_text_copied, CREDIT["u_text_copied"])
            dve.sem_inc(sum_split, CREDIT["sum_split"])
            dve.sem_inc(w_low_ready, CREDIT["w_low"])
            dve.sem_inc(v_split, CREDIT["v_split"])
            dve.sem_inc(y_added, CREDIT["y_added"])
            dve.sem_inc(recip_ready, CREDIT["recip_ready"])
            dve.sem_inc(o_scaled, CREDIT["o_scaled"])
            dve.sem_inc(norm_summed, CREDIT["norm_summed"])
            dve.sem_inc(max_tile_done, CREDIT["max_tile_done"])
            dve.sem_inc(judgement_read, CREDIT["judgement_read"])

            def sub(out, a, b):
                return nc.vector.tensor_tensor(out, a, b, ALU.subtract)

            def queries(g):
                def ready(h, par, i, nth):
                    k, w = H * g + h, w_index(g, 0, h)
                    dve.wait_ge(w_loaded[i], 16 * (3 * (H // WRING) * g + nth + 1))
                    dve.wait_ge(w_used, 2 * H * g + h - 1 + CREDIT["w_used"])
                    nc.vector.tensor_copy(w_high[:, par, 0:DIM], w_stage[:, i, 0:DIM]).then_inc(q_w_high_ready, 1)
                    dve.wait_ge(q_w_high_ready, k + 1)
                    sub(w_low[:, par, 0:DIM], w_stage[:, i, 0:DIM], w_high[:, par, 0:DIM].bitcast(F32))\
                        .then_inc(w_low_ready, 1)

                heads(dve, ready)
                dve.wait_ge(squares_summed, H * (g + 1) + CREDIT["squares_summed"])
                sums = psum[0:TOK, 2, 0:2 * H * 3].rearrange("p (i h k) -> p i h k", i=2, h=H)
                nc.vector.tensor_reduce(q_sum[:, :], sums[:, :, :, 0], mybir.AxisListType.X, ALU.add)\
                    .then_inc(q_reduced, 1)
                nc.vector.tensor_reduce(bound_sq[:, :], sums[:, :, :, 1:3], mybir.AxisListType.XY, ALU.max)\
                    .then_inc(bound_step, 1)
                dve.wait_ge(q_reduced, g + 1)
                nc.vector.tensor_scalar(q_ms[:, :], q_sum[:, :], 1.0 / INNER, EPS_RMS, ALU.mult, ALU.add)\
                    .then_inc(q_ms_ready, 1)
                dve.wait_ge(q_rms_ready, g + 1)
                dve.wait_ge(bound_step, BOUND_STEPS * g + 1)
                nc.vector.tensor_tensor(bound_sq[:, :], bound_sq[:, :], q_rms[:, :], ALU.mult).then_inc(bound_step, 1)
                dve.wait_ge(bound_step, BOUND_STEPS * g + 2)
                nc.vector.tensor_tensor(bound_sq[:, :], bound_sq[:, :], q_rms[:, :], ALU.mult).then_inc(bound_step, 1)
                dve.wait_ge(bound_step, BOUND_STEPS * g + 3)
                nc.vector.tensor_reduce(bound_max[:, :], bound_sq[:, :], mybir.AxisListType.X, ALU.max)\
                    .then_inc(bound_step, 1)

            def judge(g):
                dve.wait_ge(bound_flat, g + 1)
                nc.vector.tensor_reduce(bound_row[:, :], psum[0:1, SUM, 0:TOK], mybir.AxisListType.X, ALU.max)\
                    .then_inc(bound_step, 1)
                dve.wait_ge(bound_step, BOUND_STEPS * g + 5)
                dve.wait_ge(judgement_read, 10 * g + CREDIT["judgement_read"])
                nc.vector.tensor_scalar(is_safe[:, :], bound_row[:, :], SAFE_SCORE ** 2 / INNER, None, ALU.is_le)\
                    .then_inc(safe_known, 1)

            def absorb(g):
                def ready(h, par, i, nth):
                    k = H * g + h
                    dve.wait_ge(w_high_ready, k + H * g + 1)
                    for s in range(2):
                        c = slice(s * DIM, (s + 1) * DIM)
                        last = nc.vector.scalar_tensor_tensor(w_low[:, par, c], w_stage[:, i, c],
                                                              key_scale[:, s, ds(h, 1)],
                                                              w_high[:, par, c].bitcast(F32), ALU.mult, ALU.subtract)
                    last.then_inc(w_low_ready, 1)
                    for parts, wide in ((bias_high, bias_wide_high), (bias_low, bias_wide_low)):
                        nc.vector.tensor_copy(wide[:, par, :].rearrange("p (a b) -> p a b", a=4)[:, :, 0],
                                              parts[:, ds(h, 1), :].rearrange("p a n -> p (a n)").bitcast(F32))
                    dve.wait_ge(q_high_ready, k + 1)
                    sub(r_low[:, par, 0:GN], q_hat[:, par, :], r_high[:, par, 0:GN].bitcast(F32)).then_inc(q_split, 1)

                def take(h, par, i, nth):
                    k = H * g + h
                    dve.wait_ge(rank_copied, k + 1)
                    rows = slice(64, P)
                    at = rank_rows[rows, :, ds(h * S, S)]
                    sub(at, psum[rows, 4 + par, 0:GN].rearrange("p (b q) -> p b q", b=GB), at.bitcast(F32))
                    uo = rows_uo[:, :, ds(h * S, S)].rearrange("p (b r) q -> p r b q", b=GB)
                    for c in range(NC):
                        last = nc.vector.tensor_copy(
                            uo[:, 2 + c, :, :],
                            psum[:, 2 * par + 1, c * GN:(c + 1) * GN].rearrange("p (b q) -> p b q", b=GB))
                    last.then_inc(u_text_copied, 1)
                heads(dve, take, ready)

            def prepare(it, t):
                k, st, s, T = slot(t, CTX_RING), slot(t, STAGE_RING), int(t >= IMG_TILES), TILES * it + t
                dve.wait_ge(ctx_high, T + 1)
                sub(c_low[:, k, :], stage[:, st, :], c_high[:, k, :].bitcast(F32)).then_inc(ctx_low, 1)
                return T, k, st, s

            def norm_terms(it, t):
                k, st, s, T = slot(t, CTX_RING), slot(t, STAGE_RING), int(t >= IMG_TILES), TILES * it + t
                dve.wait_ge(ctx_low, T + 1)
                nat = slice(DIM, 2 * DIM)
                nc.vector.tensor_tensor_reduce(out=junk[:, 0, :], in0=stage[:, st, nat], in1=twice_wb[:, s, :],
                                               scale=1.0 / INNER, scalar=bb_eps[:, s:s + 1], op0=ALU.mult,
                                               op1=ALU.add, accum_out=key_lin[:, par_of(t):par_of(t) + 1])
                nc.vector.tensor_tensor(c_twice[:, par_of(t), :], stage[:, st, nat], c_low[:, k, nat].bitcast(F32),
                                        ALU.add).then_inc(stage_used, 1)

            def par_of(t):
                return t % 2 if t < TILES - 1 else 0

            def norm(it, t):
                T = TILES * it + t
                dve.wait_ge(gram_done, T + 1)
                dve.wait_ge(stage_used, T + 1 + CREDIT["stage_used"])
                nc.vector.tensor_tensor_reduce(out=junk[:, 1, :], in0=psum[:, GRAM, 0:DIM], in1=c_twice[:, par_of(t), :],
                                               scale=1.0 / INNER, scalar=key_lin[:, par_of(t):par_of(t) + 1],
                                               op0=ALU.mult, op1=ALU.add, accum_out=key_ms[:, t:t + 1])\
                    .then_inc(norm_summed, 1)

            def split_u(it, bl, s, half):
                dve.wait_ge(u_high_ready, 4 * it + 2 * s + half + 1)
                cols = slice(half * HALF, (half + 1) * HALF)
                sub(u_low[:, 2 * s:2 * s + 2, cols], rows_uo[:, ds(4 * bl + 2 * s, 2), cols],
                    u_high[:, 2 * s:2 * s + 2, cols].bitcast(F32)).then_inc(u_split, 1)

            def split_probs(it, u):
                half = u % 2
                dve.wait_ge(exp_done, UNITS * it + u + 1 + CREDIT["exp_done"])
                sub(p_low[:, half, :], probs[:, half, :], p_high[:, half, :].bitcast(F32)).then_inc(probs_split, 1)

            def split_sum(it, s, half):
                last = 2 * (IMG_TILES if s == 0 else TILES) - 2 + half
                n = 4 * it + 2 * s + half
                dve.wait_ge(sum_added, UNITS * it + last + 1 + CREDIT["sum_added"])
                dve.wait_ge(sum_wide, n + CREDIT["sum_wide"])
                nc.vector.tensor_copy(p_sum_high[:, :], p_sum[:, 2 * s + half, :]).then_inc(sum_high_ready, 1)
                dve.wait_ge(sum_high_ready, n + 1)
                sub(p_sum_low[:, :], p_sum[:, 2 * s + half, :], p_sum_high[:, :].bitcast(F32)).then_inc(sum_split, 1)

            def reciprocal(it, s, half, part):
                n = 4 * it + 2 * s + half
                cols = slice(part * (HALF // 2), (part + 1) * (HALF // 2))
                if part == 0:
                    dve.wait_ge(sum_wide, n + 1 + CREDIT["sum_wide"])
                    dve.wait_ge(o_scaled, n + CREDIT["o_scaled"])
                r = nc.vector.reciprocal(recip[:, cols], psum[:, SUM, cols])
                if part == 1:
                    r.then_inc(recip_ready, 1)

            def scale_o(it, bl, s, half):
                n = 4 * it + 2 * s + half
                dve.wait_ge(recip_ready, n + 1 + CREDIT["recip_ready"])
                dve.wait_ge(o_copied, n + 1 + CREDIT["o_copied"])
                cols = slice(half * HALF, (half + 1) * HALF)
                at = rows_uo[:, ds(4 * bl + 2 * s, 2), cols]
                nc.vector.tensor_tensor(at, at, recip[:, :].unsqueeze(1).to_broadcast([P, 2, HALF]), ALU.mult)\
                    .then_inc(o_scaled, 1)

            def set_end(it, bl, s, step):
                for half, at in ((0, 1), (1, 5)):
                    if step == at:
                        split_sum(it, s, half)
                    if step in (at + 2, at + 3):
                        reciprocal(it, s, half, step - at - 2)
                    if step == at + 4:
                        scale_o(it, bl, s, half)

            def body(it, bl, has_prev, has_next):
                if not has_prev:
                    for half in range(2):
                        split_u(it, bl, 0, half)
                for step in range(UNITS):
                    if has_prev and step == 0:
                        split_probs(it - 1, UNITS - 1)
                    if step >= 1:
                        split_probs(it, step - 1)
                    if step in (1, 2):
                        split_u(it, bl, 1, step - 1)
                    if step % 2 == 0:
                        norm(*ahead(it, step // 2 + 1))
                        prepare(*ahead(it, step // 2 + PREP))
                    else:
                        norm_terms(*ahead(it, step // 2 + PREP))
                    if has_prev:
                        set_end(it - 1, bl - 1, 1, step - 1)
                    set_end(it, bl, 0, step - 8)
                    if has_next and step in (16, 18):
                        split_u(it + 1, bl + 1, 0, (step - 16) // 2)

            def tail(it, bl):
                split_probs(it - 1, UNITS - 1)
                for step in range(10):
                    set_end(it - 1, bl - 1, 1, step)

            def outputs(g):
                def ready(h, par, i, nth):
                    k = H * g + h
                    dve.wait_ge(o_high_ready, k + 1)
                    uo = rows_uo[:, :, ds(h * S, S)].rearrange("p (b r) q -> p r b q", b=GB)
                    wide = lambda x: x.rearrange("p (r b q) -> p r b q", r=4, b=GB)
                    sub(wide(r_low[:, par, :]), uo, wide(r_high[:, par, :].bitcast(F32))).then_inc(o_split, 1)

                def take(h, par, i, nth):
                    k = H * g + h
                    dve.wait_ge(v_copied, k + 1 + CREDIT["v_copied"])
                    dve.wait_ge(y_done, k - 1 + CREDIT["y_done"])
                    nc.vector.tensor_copy(v_high[:, par, :], v_out[:, par, :]).then_inc(v_high_ready, 1)
                    dve.wait_ge(v_high_ready, k + 1)
                    sub(v_low[:, par, :], v_out[:, par, :], v_high[:, par, :].bitcast(F32)).then_inc(v_split, 1)
                heads(dve, take, ready)
                dve.wait_ge(y_done, H * (g + 1) + CREDIT["y_done"])
                for c in range(NC):
                    ob = small[:, SMALL["ob"] + c:SMALL["ob"] + c + 1]
                    at = xT[:, c, ds(GN * g, GN)]
                    last = nc.vector.scalar_tensor_tensor(at, psum[:, 4 + c, 0:GN], ob, at, ALU.add, ALU.add)
                last.then_inc(y_added, 1)

            def maxima(it, bl):
                MAX_STEPS = 4
                dve.wait_ge(max_u_high, it + 1)
                sub(u_low[:, :, :], rows_uo[:, ds(4 * bl, 4), :], u_high[:, :, :].bitcast(F32)).then_inc(max_u_split, 1)
                nat = slice(DIM, 2 * DIM)
                for t in range(TILES):
                    T, s, n, one = TILES * it + t, int(t >= IMG_TILES), ROWS[t], slice(t, t + 1)
                    dve.wait_ge(max_high, T + 1)
                    sub(c_low[:, MAX_SLOT, :], stage[:, MAX_SLOT, :], c_high[:, MAX_SLOT, :].bitcast(F32))\
                        .then_inc(max_low, 1)
                    dve.wait_ge(max_low, T + 1)
                    nc.vector.tensor_tensor_reduce(out=junk[:, 0, :], in0=stage[:, MAX_SLOT, nat],
                                                   in1=twice_wb[:, s, :], scale=1.0 / INNER, scalar=bb_eps[:, s:s + 1],
                                                   op0=ALU.mult, op1=ALU.add, accum_out=max_lin[:, one])\
                        .then_inc(max_terms, 1)
                    nc.vector.tensor_tensor(max_twice, stage[:, MAX_SLOT, nat], c_low[:, MAX_SLOT, nat].bitcast(F32),
                                            ALU.add).then_inc(max_terms, 1)
                    dve.wait_ge(max_terms, 2 * T + 2)
                    dve.wait_ge(max_scores, T + 1 + CREDIT["max_scores"])
                    nc.vector.tensor_tensor_reduce(out=junk[:, 1, :], in0=psum[:, GRAM, 0:DIM], in1=max_twice,
                                                   scale=1.0 / INNER, scalar=max_lin[:, one], op0=ALU.mult,
                                                   op1=ALU.add, accum_out=max_ms[:, one]).then_inc(max_summed, 1)
                    dve.wait_ge(max_rooted, T + 1)
                    dve.wait_ge(max_tile_done, T + CREDIT["max_tile_done"])
                    for half in range(2):
                        run, src = max_run[0:n, 2 * s + half, :], psum[0:n, SC + half, 0:HALF]
                        if t in (0, IMG_TILES):
                            last = nc.vector.tensor_scalar(run, src, max_root[0:n, one], None, ALU.mult)
                        else:
                            last = nc.vector.scalar_tensor_tensor(run, src, max_root[0:n, one], run, ALU.mult, ALU.max)
                    last.then_inc(max_tile_done, 1)
                dve.wait_ge(max_summed, TILES * (it + 1))
                nc.vector.tensor_tensor(max_inverse, max_ms, max_root, ALU.mult).then_inc(max_steps, 1)
                dve.wait_ge(max_steps, MAX_STEPS * it + 1)
                nc.vector.tensor_copy(inverse[:, :, 0], max_inverse).then_inc(max_steps, 1)
                dve.wait_ge(max_steps, MAX_STEPS * it + 2)
                sub(inverse[:, :, 1], max_inverse, inverse[:, :, 0].bitcast(F32)).then_inc(max_steps, 1)
                dve.wait_ge(max_flipped, it + 1)
                nc.vector.tensor_reduce(max_cols, psum[:, 0:4, :].rearrange("p a n -> p (a n)")[:, 0:2 * HS]
                                        .rearrange("p (k n) -> p k n", n=P), mybir.AxisListType.X, ALU.max)\
                    .then_inc(max_steps, 1)
                dve.wait_ge(max_steps, MAX_STEPS * it + 4)
                nc.vector.tensor_scalar(negative, max_cols, -1.0, None, ALU.mult).then_inc(max_found, 1)
                dve.wait_ge(max_stored, 64 * (it + 1))

            def no_maxima():
                dve.sem_inc(max_u_split, GB)
                dve.sem_inc(max_low, GB * TILES)
                dve.sem_inc(max_terms, 2 * GB * TILES)
                dve.sem_inc(max_summed, GB * TILES)
                dve.sem_inc(max_tile_done, GB * TILES)
                dve.sem_inc(max_steps, 4 * GB)
                dve.sem_inc(max_found, GB)

            nc.vector.memset(zeros[:, :], 0.0).then_inc(start_ready, 1)
            dve.wait_ge(start_ready, 1)
            for wide in (bias_wide_high, bias_wide_low):
                nc.vector.memset(wide[:, :, :].bitcast(F32), 0.0).then_inc(start_ready, 1)
            nc.vector.memset(p_sum[:, :, :], 0.0).then_inc(start_ready, 1)
            nc.vector.memset(key_ms[:, :], 0.0).then_inc(start_ready, 1)
            nc.vector.memset(key_lin[:, :], 0.0).then_inc(start_ready, 1)
            nc.vector.memset(square_w[:, :, 0], 1.0).then_inc(start_ready, 1)
            for s in range(2):
                nc.vector.tensor_tensor(square_w[:, :, 1 + s], key_scale[:, s, :], key_scale[:, s, :], ALU.mult)\
                    .then_inc(start_ready, 1)
            dve.wait_ge(start_ready, START_STEPS)
            for t in range(PREP):
                prepare(0, t)
                norm_terms(0, t)
                if t == 0:
                    norm(0, 0)
            with dve.Fori(0, NG) as g:
                queries(g)
                absorb(g)
                judge(g)
                where_unsafe(dve, g, maxima, no_maxima)
                batches(dve, g, body, tail)
                outputs(g)

        @block.gpsimd
        def _(gp):
            gp.sem_inc(sum_added, CREDIT["sum_added"])
            gp.sem_inc(q_scaled, CREDIT["q_scaled"])

            def absorb(g):
                def scale(h, par, i, nth):
                    gp.wait_ge(q_wide_copied, g + 1)
                    gp.wait_ge(w_used, 2 * H * g + H + h - 1 + CREDIT["w_used"])
                    nc.gpsimd.tensor_tensor(q_hat[:, par, :], q_raw[:, ds(h, 1), :].rearrange("p a n -> p (a n)"),
                                            q_rms_wide[:, :], ALU.mult).then_inc(q_scaled, 1)
                heads(gp, scale)

            def outputs(g):
                def split(h, par, i, nth):
                    gp.wait_ge(w_high_ready, 2 * H * g + H + h + 1)
                    nc.gpsimd.tensor_tensor(w_low[:, par, :], v_stage[:, i, 0:2 * DIM], w_high[:, par, :].bitcast(F32),
                                            ALU.subtract)
                    nc.gpsimd.tensor_tensor(ow_low[:, i, :], v_stage[:, i, 2 * DIM:VCOLS],
                                            ow_high[:, i, :].bitcast(F32), ALU.subtract).then_inc(w_low_ready, 1)
                heads(gp, split)

            def key_root(it, t):
                gp.wait_ge(norm_summed, TILES * it + t + 1 + CREDIT["norm_summed"])
                nc.gpsimd.tensor_tensor(key_rms[:, t:t + 1], key_ms[:, t:t + 1], minus_half[:, 0:1], ALU.pow)\
                    .then_inc(key_norm, 1)

            def add(it, u):
                t, half = divmod(u, 2)
                s, n = int(t >= IMG_TILES), ROWS[t]
                gp.wait_ge(exp_done, UNITS * it + u + 1 + CREDIT["exp_done"])
                if t in (0, IMG_TILES):
                    gp.wait_ge(sum_split, 4 * (it - 1) + 2 * s + half + 1 + CREDIT["sum_split"])
                    before_it = zeros[0:n, :].to_broadcast([n, HALF])
                else:
                    before_it = p_sum[0:n, 2 * s + half, :]
                gp.wait_ge(sum_added, UNITS * it + u - 1 + CREDIT["sum_added"])
                nc.gpsimd.tensor_tensor(p_sum[0:n, 2 * s + half, :], probs[0:n, half, :], before_it, ALU.add)\
                    .then_inc(sum_added, 1)

            def body(it, bl, has_prev, has_next):
                for step in range(UNITS):
                    if has_prev and step == 0:
                        add(it - 1, UNITS - 1)
                    if step >= 1:
                        add(it, step - 1)
                    if step % 2 == 0:
                        key_root(*ahead(it, step // 2 + 1))

            def tail(it, bl):
                add(it - 1, UNITS - 1)

            def maxima(it, bl):
                for t in range(TILES):
                    gp.wait_ge(max_summed, TILES * it + t + 1)
                    nc.gpsimd.tensor_tensor(max_root[:, t:t + 1], max_ms[:, t:t + 1], minus_half[:, 0:1], ALU.pow)\
                        .then_inc(max_rooted, 1)

            def no_maxima():
                gp.sem_inc(max_rooted, GB * TILES)

            gp.wait_ge(start_ready, START_STEPS)
            gp.wait_ge(zeros_stored, 16)
            key_root(0, 0)
            with gp.Fori(0, NG) as g:
                gp.wait_ge(q_ms_ready, g + 1)
                nc.gpsimd.tensor_tensor(q_rms[:, :], q_ms[:, :], minus_half[0:TOK, 0:2], ALU.pow)\
                    .then_inc(q_rms_ready, 1)
                absorb(g)
                where_unsafe(gp, g, maxima, no_maxima)
                batches(gp, g, body, tail)
                outputs(g)


def experts(nc, router_in, bias_in, ffn_in, out, probs_dram, psum, xT, ident, ones, minus_half):
    ctx = ExitStack()
    with ctx:
        sb = lambda n, s, dt=F32: ctx.enter_context(nc.sbuf_tensor(n, s, dt))
        sem = lambda n: ctx.enter_context(nc.semaphore(n))
        RT = N // P
        RING = 3
        WCOLS = 3 * DIM
        credit = {"w_split": RING, "scaled": 2 * RING, "down_done": 2 * RING, "h_split": 2, "clipped": 2}
        xn = sb("ffn_xn", [P, NC, N])
        x_high, x_low = sb("ffn_x_high", [P, NC, N], F32R), sb("ffn_x_low", [P, NC, N], F32R)
        router = sb("router", [P, NC, E])
        e_bias = sb("e_bias", [P, E])
        logit, absolute, u, w, lnw, big, small, mask, score = [
            sb(n, [P, RT, E]) for n in ("logit", "absolute", "exp_abs", "one_plus", "ln_one_plus", "log1p_big",
                                        "log1p_small", "mask", "score")]
        ranked, picked = sb("ranked", [P, RT, E + 4]), sb("picked", [P, RT, E + 4])
        top = sb("top", [P, RT, 8])
        p_sum, p_rec = sb("chosen_sum", [P, RT]), sb("chosen_rec", [P, RT])
        probs = sb("router_probs", [P, RT, E])
        probs_T = sb("probs_T", [E + 1, N])
        w_stage = sb("e_stage", [P, RING, WCOLS])
        w_high, w_low = sb("e_high", [P, RING, WCOLS], F32R), sb("e_low", [P, RING, WCOLS], F32R)
        p_wide = sb("p_wide", [P, RING, N])
        gate, gated, scaled_gate, up, h = [sb(n, [P, 2, N // 2]) for n in ("gate", "gated", "scaled_gate", "up", "h")]
        h_high, h_low = sb("h_high", [P, 2, N // 2], F32R), sb("h_low", [P, 2, N // 2], F32R)
        HN = N // 2
        DOWN, GATE_UP = 0, 4

        router_loaded, consts, x_high_ready, x_split = (
            sem("router_loaded"), sem("router_consts"), sem("ffn_x_high_ready"), sem("ffn_x_split"))
        logits_done, chain, act_chain = sem("logits_done"), sem("router_chain"), sem("router_act")
        flipped, probs_stored, out_stored = sem("flipped"), sem("probs_stored"), sem("out_stored")
        w_loaded = [sem(f"e_loaded{i}") for i in range(RING)]
        p_loaded = [sem(f"p_loaded{i}") for i in range(RING)]
        w_high_ready, w_split = sem("e_high_ready"), sem("e_split")
        gate_up_done, gate_clipped, up_clipped, silu_done, scaled, h_ready, h_high_ready, h_split, down_done = [
            sem(n) for n in ("gate_up_done", "gate_clipped", "up_clipped", "silu_done", "gate_scaled", "h_ready",
                             "h_high_ready", "h_split", "down_done")]
        out_ready = sem("out_ready")
        ln_pe, ln_dve, ln_pool, ln_done = layer_norm(
            nc, ctx, "ln2", xT, lambda c: xn[:, c, :].rearrange("p (h n) -> p h n", h=2), psum[:, 0:3, :])
        block = ctx.enter_context(nc.Block())

        def triples(eng, body):
            body(0, True)
            with eng.Fori(1, (E + 1) // RING) as k:
                body(k, False)

        @block.sync
        def _(sp):
            def load_weights(e, i):
                sp.wait_ge(w_split, e - RING + 1 + credit["w_split"])
                sp.dma_start(w_stage[:, i, :], ffn_in[ds(e, 1), :, :].rearrange("a p n -> p (a n)"))\
                    .then_inc(w_loaded[i], 16)

            def load_probs(e, i):
                sp.wait_ge(scaled, 2 * (e - RING + 1) + credit["scaled"])
                sp.dma_start(p_wide[:, i, :], probs_dram[ds(e, 1), :].partition_broadcast(P))\
                    .then_inc(p_loaded[i], 16)

            sp.dma_start(router[:, :, :], router_in).then_inc(router_loaded, 16)
            sp.dma_start(e_bias[:, :], bias_in.partition_broadcast(P)).then_inc(router_loaded, 16)
            load_weights(0, 0)
            sp.wait_ge(chain, ROUTER_STEPS)
            sp.dma_start(probs_dram, probs_T[:, :]).then_inc(probs_stored, 16)
            sp.wait_ge(probs_stored, 16)

            def body(k, first):
                for i in range(RING):
                    load_probs(RING * k + i, i)
                    load_weights(RING * k + i + 1, (i + 1) % RING)
            with sp.Fori(0, (E + 1) // RING) as k:
                body(k, False)
            sp.wait_ge(out_ready, NC)
            sp.dma_start(out, xT[:, :, :]).then_inc(out_stored, 16)
            sp.wait_ge(out_stored, 16)

        @block.gpsimd
        def _(gp):
            gp.sem_inc(scaled, credit["scaled"])
            ln_pool(gp, minus_half)

            def body(k, first):
                for j in range(2 * RING):
                    i, half, v = j // 2, j % 2, 2 * RING * k + j
                    gp.wait_ge(p_loaded[i], 16 * (k + 1))
                    gp.wait_ge(silu_done, v + 1)
                    nc.gpsimd.tensor_tensor(scaled_gate[:, half, :], gated[:, half, :],
                                            p_wide[:, i, half * HN:(half + 1) * HN], ALU.mult).then_inc(scaled, 1)
            triples(gp, body)

        @block.tensor
        def _(pe):
            pe.sem_inc(down_done, credit["down_done"])

            def three(out, high, low, rhigh, rlow, start, stop):
                nc.tensor.matmul(out, high, rhigh, start=start, stop=False)
                nc.tensor.matmul(out, high, rlow, start=False, stop=False)
                return nc.tensor.matmul(out, low, rhigh, start=False, stop=stop)

            ln_pe(pe, ones, ident)
            pe.wait_ge(router_loaded, 32)
            pe.wait_ge(ln_done, NC)
            for i in range(RT):
                for c in range(NC):
                    last = nc.tensor.matmul(psum[:, 3, i * E:(i + 1) * E], xn[:, c, i * P:(i + 1) * P],
                                            router[:, c, :], start=c == 0, stop=c == NC - 1)
            last.then_inc(logits_done, 1)
            pe.wait_ge(chain, ROUTER_STEPS - 2)
            for i in range(RT):
                last = nc.tensor.transpose(psum[0:E, 4 + i // 4, (i % 4) * P:(i % 4 + 1) * P], probs[:, i, :],
                                           ident[:, :])
            last.then_inc(flipped, 1)
            pe.wait_ge(chain, ROUTER_STEPS)
            pe.wait_ge(x_split, NC)

            def gate_up(k, j):
                i, half, v = j // 2, j % 2, 2 * RING * k + j
                if half == 0:
                    pe.wait_ge(w_split, RING * k + i + 1 + credit["w_split"])
                pe.wait_ge(up_clipped, v - 1 + credit["clipped"])
                for m in range(2):
                    for c in range(NC):
                        cols = slice(m * DIM + c * P, m * DIM + (c + 1) * P)
                        r = slice(half * HN, (half + 1) * HN)
                        last = three(psum[:, GATE_UP + 2 * half + m, 0:HN], w_high[:, i, cols], w_low[:, i, cols],
                                     x_high[:, c, r], x_low[:, c, r], c == 0, c == NC - 1)
                last.then_inc(gate_up_done, 1)

            def down(k, j, start, stop):
                i, half, v = j // 2, j % 2, 2 * RING * k + j
                pe.wait_ge(h_split, v + 1 + credit["h_split"])
                for c in range(NC):
                    cols = slice(2 * DIM + c * P, 2 * DIM + (c + 1) * P)
                    last = three(psum[:, DOWN + 2 * half + c, 0:HN], w_high[:, i, cols], w_low[:, i, cols],
                                 h_high[:, half, :], h_low[:, half, :], start, stop)
                last.then_inc(down_done, 1)

            def body(k, first):
                for j in range(2 * RING):
                    gate_up(k, j)
                    if j >= 2:
                        down(k, j - 2, first and j < 4, False)
                    elif not first:
                        down(k - 1, 2 * RING - 2 + j, False, False)
            triples(pe, body)
            for j in (4, 5):
                down((E + 1) // RING - 1, j, False, True)

        @block.scalar
        def _(act):
            copy = lambda out, in_: nc.scalar.activation(out, in_, ACT.Copy)
            for c in range(NC):
                act.wait_ge(ln_done, c + 1)
                copy(x_high[:, c, :], xn[:, c, :]).then_inc(x_high_ready, 1)
            act.wait_ge(chain, 2)
            nc.scalar.activation(u[:, :, :], absolute[:, :, :], ACT.Exp, scale=-1.0).then_inc(act_chain, 1)
            act.wait_ge(chain, 3)
            nc.scalar.activation(lnw[:, :, :], w[:, :, :], ACT.Ln).then_inc(act_chain, 1)
            act.wait_ge(chain, SOFTPLUS_STEPS)
            nc.scalar.activation(score[:, :, :], big[:, :, :], ACT.Sqrt).then_inc(act_chain, 1)

            def split(e, i, k_loads):
                act.wait_ge(w_loaded[i], 16 * k_loads)
                act.wait_ge(down_done, 2 * (e - RING + 1) + credit["down_done"])
                copy(w_high[:, i, :], w_stage[:, i, :]).then_inc(w_high_ready, 1)

            def silu(v, half):
                act.wait_ge(gate_clipped, v + 1)
                act.wait_ge(scaled, v - 1 + credit["scaled"])
                nc.scalar.activation(gated[:, half, :], gate[:, half, :], ACT.Silu).then_inc(silu_done, 1)

            def high(v, half):
                act.wait_ge(h_ready, v + 1)
                act.wait_ge(down_done, v - 1 + credit["down_done"])
                copy(h_high[:, half, :], h[:, half, :]).then_inc(h_high_ready, 1)

            def body(k, first):
                for j in range(2 * RING):
                    v = 2 * RING * k + j
                    silu(v, j % 2)
                    if not (first and j == 0):
                        high(v - 1, (j - 1) % 2)
                    if j % 2 == 0:
                        split(RING * k + j // 2 + 1, (j // 2 + 1) % RING, k + 1 + (j // 2 + 1) // RING)
            split(0, 0, 1)
            triples(act, body)
            high(2 * (E + 1) - 1, 1)

        @block.vector
        def _(dve):
            dve.sem_inc(w_split, credit["w_split"])
            dve.sem_inc(h_split, credit["h_split"])
            dve.sem_inc(up_clipped, credit["clipped"])
            V = nc.vector
            ln_dve(dve)
            for c in range(NC):
                dve.wait_ge(x_high_ready, c + 1)
                V.tensor_tensor(x_low[:, c, :], xn[:, c, :], x_high[:, c, :].bitcast(F32), ALU.subtract)\
                    .then_inc(x_split, 1)
            steps = [0]

            def link(ins):
                steps[0] += 1
                ins.then_inc(chain, 1)
                dve.wait_ge(chain, steps[0])

            dve.wait_ge(logits_done, 1)
            link(V.tensor_copy(logit[:, :, :], psum[:, 3, 0:RT * E].rearrange("p (t e) -> p t e", t=RT)))
            link(V.scalar_tensor_tensor(absolute[:, :, :], logit[:, :, :], -1.0, logit[:, :, :], ALU.mult, ALU.max))
            dve.wait_ge(act_chain, 1)
            link(V.tensor_scalar(w[:, :, :], u[:, :, :], 1.0, None, ALU.add))
            link(V.tensor_scalar(big[:, :, :], w[:, :, :], -1.0, 1e-30, ALU.add, ALU.max))
            link(V.reciprocal(mask[:, :, :], big[:, :, :]))
            link(V.tensor_tensor(big[:, :, :], mask[:, :, :], u[:, :, :], ALU.mult))
            dve.wait_ge(act_chain, 2)
            link(V.tensor_tensor(big[:, :, :], big[:, :, :], lnw[:, :, :], ALU.mult))
            link(V.tensor_scalar(small[:, :, :], u[:, :, :], 1 / 5, -1 / 4, ALU.mult, ALU.add))
            for term in (1 / 3, -1 / 2, 1.0):
                link(V.tensor_tensor(small[:, :, :], small[:, :, :], u[:, :, :], ALU.mult))
                link(V.tensor_scalar(small[:, :, :], small[:, :, :], term, None, ALU.add))
            link(V.tensor_tensor(small[:, :, :], small[:, :, :], u[:, :, :], ALU.mult))
            link(V.tensor_scalar(mask[:, :, :], u[:, :, :], 1 / 64, None, ALU.is_lt))
            link(V.tensor_tensor(small[:, :, :], small[:, :, :], big[:, :, :], ALU.subtract))
            link(V.tensor_tensor(small[:, :, :], small[:, :, :], mask[:, :, :], ALU.mult))
            link(V.tensor_tensor(small[:, :, :], small[:, :, :], big[:, :, :], ALU.add))
            link(V.scalar_tensor_tensor(big[:, :, :], logit[:, :, :], 0.0, small[:, :, :], ALU.max, ALU.add))
            assert steps[0] == SOFTPLUS_STEPS, steps
            link(V.memset(ranked[:, :, E:E + 4], -1e30))
            dve.wait_ge(router_loaded, 32)
            dve.wait_ge(act_chain, 3)
            link(V.tensor_tensor(ranked[:, :, 0:E], score[:, :, :], e_bias[:, :].unsqueeze(1).to_broadcast([P, RT, E]),
                                 ALU.add))
            for t in range(RT):
                V.max(top[:, t, :], ranked[:, t, 0:E])
            link(V.memset(small[:, :, :], 0.0))
            link(V.memset(top[:, :, K_TOP:8], -1e30))
            for t in range(RT):
                V.match_replace(picked[:, t, :], top[:, t, :], ranked[:, t, :], -3e38)
            link(V.memset(mask[:, :, :], 0.0))
            link(V.tensor_tensor(mask[:, :, :], picked[:, :, 0:E], ranked[:, :, 0:E], ALU.is_lt))
            link(V.tensor_tensor(score[:, :, :], score[:, :, :], mask[:, :, :], ALU.mult))
            link(V.tensor_reduce(p_sum[:, :], score[:, :, :], mybir.AxisListType.X, ALU.add))
            link(V.tensor_scalar(p_sum[:, :], p_sum[:, :], 1e-20, None, ALU.add))
            link(V.reciprocal(p_rec[:, :], p_sum[:, :]))
            link(V.tensor_tensor(probs[:, :, :], score[:, :, :], p_rec[:, :].unsqueeze(2).to_broadcast([P, RT, E]),
                                 ALU.mult))
            assert steps[0] == ROUTER_STEPS - 2, steps
            dve.wait_ge(flipped, 1)
            V.memset(probs_T[E:E + 1, :], 1.0)
            link(V.tensor_copy(probs_T[0:E, 0:4 * P], psum[0:E, 4, 0:4 * P]))
            link(V.tensor_copy(probs_T[0:E, 4 * P:N], psum[0:E, 5, 0:N - 4 * P]))

            def split(e, i, cols, last):
                dve.wait_ge(w_high_ready, e + 1)
                r = V.tensor_tensor(w_low[:, i, cols], w_stage[:, i, cols], w_high[:, i, cols].bitcast(F32),
                                    ALU.subtract)
                if last:
                    r.then_inc(w_split, 1)

            def clip(v, half):
                dve.wait_ge(gate_up_done, v + 1)
                V.tensor_scalar(gate[:, half, :], psum[:, GATE_UP + 2 * half, 0:HN], ALPHA, -ALPHA, ALU.min, ALU.max)\
                    .then_inc(gate_clipped, 1)
                V.tensor_scalar(up[:, half, :], psum[:, GATE_UP + 2 * half + 1, 0:HN], ALPHA, -ALPHA, ALU.min,
                                ALU.max).then_inc(up_clipped, 1)

            def multiply(v, half):
                dve.wait_ge(scaled, v + 1 + credit["scaled"])
                dve.wait_ge(up_clipped, v + 1 + credit["clipped"])
                dve.wait_ge(h_split, v - 1 + credit["h_split"])
                V.tensor_tensor(h[:, half, :], up[:, half, :], scaled_gate[:, half, :], ALU.mult).then_inc(h_ready, 1)

            def low(v, half):
                dve.wait_ge(h_high_ready, v + 1)
                V.tensor_tensor(h_low[:, half, :], h[:, half, :], h_high[:, half, :].bitcast(F32), ALU.subtract)\
                    .then_inc(h_split, 1)

            def body(k, first):
                for j in range(2 * RING):
                    v = 2 * RING * k + j
                    e, i = RING * k + j // 2 + 1, (j // 2 + 1) % RING
                    clip(v, j % 2)
                    if not (first and j == 0):
                        multiply(v - 1, (j - 1) % 2)
                    cols = slice(0, 2 * DIM) if j % 2 == 0 else slice(2 * DIM, 3 * DIM)
                    if j % 2 == 1:
                        split(e, i, slice(0, WCOLS), True)
                    if not (first and j == 0):
                        low(v - 1, (j - 1) % 2)
            split(0, 0, slice(0, WCOLS), True)
            triples(dve, body)
            v = 2 * (E + 1) - 1
            multiply(v, 1)
            low(v, 1)
            dve.wait_ge(down_done, 2 * (E + 1) + credit["down_done"])
            for c in range(NC):
                at = xT[:, c, :].rearrange("p (h n) -> p h n", h=2)
                acc = psum[:, DOWN:DOWN + 4, 0:HN].rearrange("p (h c) n -> p h c n", h=2)[:, :, c, :]
                V.tensor_tensor(at, at, acc, ALU.add).then_inc(out_ready, 1)


SOFTPLUS_STEPS = 20
ROUTER_STEPS = 33


def _layouts(a):
    import numpy as np
    chunks = lambda w: w.reshape(NC, P, -1).transpose(1, 0, 2)
    x = np.asarray(a["x"]).reshape(N, DIM)
    context = np.asarray(a["ctx_2048"])
    tiles = np.zeros((B, TILES, P, DIM), np.float32)
    start = 0
    for t, n in enumerate(ROWS):
        tiles[:, t, :n] = context[:, start:start + n]
        start += n
    packed = np.zeros((B * TILES + PREP, P, 2 * DIM), np.float32)
    flat = tiles.reshape(B * TILES, P, DIM)
    packed[:B * TILES, :, 0:DIM] = flat.reshape(-1, P, NC, P).transpose(0, 3, 2, 1).reshape(-1, P, DIM)
    packed[:B * TILES, :, DIM:] = flat
    g = {k[len("L0_xattn_"):]: np.asarray(v) for k, v in a.items() if k.startswith("L0_xattn_")}
    f = {k[len("L0_ffn_"):]: np.asarray(v) for k, v in a.items() if k.startswith("L0_ffn_")}
    by_head = lambda w: w.reshape(NC, P, H, D).transpose(2, 1, 0, 3).reshape(H, P, DIM)
    flipped = lambda w: w.reshape(DIM, H, D).transpose(1, 2, 0)
    row = lambda v: v.reshape(H, D).T
    small = np.concatenate([row(g["q_b"]), row(g["nq_s"]), row(g["ki_b"]), row(g["k_b"]), row(g["nki_s"]),
                            row(g["nkt_s"]), row(g["vi_b"]), row(g["v_b"]), g["o_b"].reshape(NC, P).T], axis=1)
    up_T = lambda w: w.reshape(-1, I, NC, P).transpose(0, 3, 2, 1).reshape(-1, P, DIM)
    ffn = np.zeros((E + 2, P, 3 * DIM), np.float32)
    for at, gate, up, down in ((slice(0, E), f["gate_w"], f["up_w"], f["down_w"]),
                               (slice(E, E + 1), f["shared_gate_w"][None], f["shared_up_w"][None],
                                f["shared_down_w"][None])):
        ffn[at] = np.concatenate([up_T(gate), up_T(up), down.transpose(0, 2, 1)], axis=2)
    return {
        "xT": chunks(x.T), "ctx": packed, "qw": by_head(g["q_w"]),
        "kw": np.concatenate([flipped(g["ki_w"]), flipped(g["k_w"])], axis=2),
        "vw": np.concatenate([by_head(g["vi_w"]), by_head(g["v_w"]), g["o_w"].reshape(H, D, DIM)], axis=2),
        "small": small, "router": chunks(f["router_w"].T), "bias": f["expert_bias"][None], "ffn": ffn,
    }


def kernel(**inputs):
    import numpy as np
    from concourse import bacc
    from concourse.bass_utils import run_bass_kernel_spmd

    nc = bacc.Bacc("TRN2", target_bir_lowering=False, num_devices=1, dynamic_dma_scratch_size=1024)
    arrays = {f"in_{k}": np.ascontiguousarray(v) for k, v in _layouts(inputs).items()}
    args = [nc.dram_tensor(k, v.shape, mybir.dt.from_np(v.dtype), kind="ExternalInput").ap()
            for k, v in arrays.items()]
    out = nc.dram_tensor("outT", (P, NC, N), F32, kind="ExternalOutput").ap()
    build(nc, *args, out)
    got = run_bass_kernel_spmd(nc, [arrays], core_ids=[0]).results[0]["outT"]
    return got.transpose(1, 0, 2).reshape(DIM, N).T.reshape(B, S, DIM)
```

```python
import concourse.bass as bass
from concourse import mybir
from contextlib import ExitStack

F32 = mybir.dt.float32
F32R = mybir.dt.float32r
ACT = mybir.ActivationFunctionType
ALU = mybir.AluOpType
ds = bass.ds

P = 128
B, S, DIM = 16, 56, 256
NC = DIM // P
N = B * S
H, D = 16, 128
INNER = H * D
N_IMG, L = 257, 1500
GB = 4
NG = B // GB
GN = GB * S
HS = H * S
HALF = HS // 2
IMG_TILES = -(-N_IMG // P)
TXT_TILES = -(-(L - N_IMG) // P)
TILES = IMG_TILES + TXT_TILES
ROWS = [min(P, N_IMG - P * t) for t in range(IMG_TILES)] + \
       [min(P, L - N_IMG - P * t) for t in range(TXT_TILES)]
PREP = 2
UNITS = 2 * TILES
TOK = 112
NTOK = N // TOK
EPS_RMS, EPS_LN = 1e-6, 1e-5
E, K_TOP, I = 32, 4, 128
ALPHA = 7.0
SMALL = {"qb": 0, "nq": 16, "kb": 32, "nk": 64, "vb": 96, "ob": 128, "end": 130}
STAGE_RING, CTX_RING, WRING = 3, 4, 4
RANK_RING = 4
SAFE_SCORE = 79.0
CREDIT = {"scores_done": UNITS, "av_done": UNITS, "exp_done": 2, "probs_split": 2, "sum_added": 2,
          "sum_split": 4, "stage_used": TILES, "u_text_copied": 2, "o_copied": 2, "w_low": WRING, "w_used": WRING, "y_done": WRING, "v_done": WRING, "q_copied": 2, "squares_summed": WRING,
          "q_scaled": 2, "u_copied": 2, "v_copied": WRING, "v_split": WRING, "q_split": WRING, "y_added": 1, "recip_ready": 1, "o_scaled": 1, "norm_summed": 1, "max_tile_done": 1, "judgement_read": 1, "sum_wide": 1, "max_scores": 1}


def slot(t, ring):
    return t % ring if t < TILES - 1 else ring


def rank_slot(t):
    s = int(t >= IMG_TILES)
    start, end = (0, IMG_TILES) if s == 0 else (IMG_TILES, TILES)
    mine = lambda k: 2 * s + (k - start) % 2
    return mine(t), (0, t - 2) if t - 2 >= start else (1, max(k for k in range(start, end) if mine(k) == mine(t)))


def before(t, ring):
    if t == TILES - 1:
        return 1, t
    if t >= ring:
        return 0, t - ring
    return 1, max(k for k in range(TILES - 1) if k % ring == t)




def layer_norm(nc, ctx, tag, xT, keep, banks):
    sem = lambda n: ctx.enter_context(nc.semaphore(f"{tag}_{n}"))
    sums, centred, squared, var, var_eps, rstd, rstd_wide, done = [
        sem(n) for n in ("sums", "centred", "squared", "var", "var_eps", "rstd", "rstd_wide", "done")]
    var_sb = ctx.enter_context(nc.sbuf_tensor(f"{tag}_var_sb", [TOK, NTOK], F32))
    rstd_sb = ctx.enter_context(nc.sbuf_tensor(f"{tag}_rstd_sb", [TOK, NTOK], F32))
    square = ctx.enter_context(nc.sbuf_tensor(f"{tag}_square", [P, NC, N], F32))
    compact, wide = banks[:, 0, 0:NTOK], banks[:, 1:3, 0:N // 2]

    def tensor(pe, ones, ident, meanwhile=(lambda: None, lambda: None)):
        for half in range(2):
            for c in range(NC):
                last = nc.tensor.matmul(wide[:, half, :], ones[:, :], xT[:, c, half * (N // 2):(half + 1) * (N // 2)],
                                        start=c == 0, stop=c == NC - 1)
        last.then_inc(sums, 1)
        meanwhile[0]()
        for i in range(NTOK):
            for c in range(NC):
                if i == 0:
                    pe.wait_ge(squared, c + 1)
                last = nc.tensor.matmul(compact[0:TOK, i:i + 1], square[:, c, TOK * i:TOK * i + TOK], ones[:, 0:1],
                                        start=c == 0, stop=c == NC - 1)
        last.then_inc(var, 1)
        meanwhile[1]()
        pe.wait_ge(rstd, 1)
        pe.wait_ge(centred, NC)
        for i in range(NTOK):
            half, at = divmod(TOK * i, N // 2)
            last = nc.tensor.matmul(wide[:, half, at:at + TOK], rstd_sb[:, i:i + 1].to_broadcast([TOK, P]),
                                    ident[0:TOK, 0:TOK], start=True, stop=True)
        last.then_inc(rstd_wide, 1)

    def vector(dve, meanwhile=(lambda: None, lambda: None)):
        dve.wait_ge(sums, 1)
        for c in range(NC):
            nc.vector.scalar_tensor_tensor(keep(c), wide, -1.0 / DIM, xT[:, c, :].rearrange("p (h n) -> p h n", h=2),
                                           ALU.mult, ALU.add).then_inc(centred, 1)
        for c in range(NC):
            dve.wait_ge(centred, c + 1)
            nc.vector.tensor_tensor(square[:, c, :].rearrange("p (h n) -> p h n", h=2), keep(c), keep(c),
                                    ALU.mult).then_inc(squared, 1)
        meanwhile[0]()
        dve.wait_ge(var, 1)
        nc.vector.tensor_scalar(var_sb[:, :], compact[0:TOK, :], 1.0 / DIM, EPS_LN, ALU.mult, ALU.add)\
            .then_inc(var_eps, 1)
        meanwhile[1]()
        dve.wait_ge(rstd_wide, 1)
        for c in range(NC):
            nc.vector.tensor_tensor(keep(c), keep(c), wide, ALU.mult).then_inc(done, 1)

    def pool(gp, minus_half):
        gp.wait_ge(var_eps, 1)
        nc.gpsimd.tensor_tensor(rstd_sb[:, :], var_sb[:, :], minus_half[0:TOK, 0:NTOK], ALU.pow).then_inc(rstd, 1)

    return tensor, vector, pool, done


def build(nc, xT_in, ctx_in, qw_in, kw_in, kwb_in, vw_in, small_in, router_in, bias_in, ffn_in, out):
    ctx = ExitStack()
    with ctx:
        def sb(name, shape, dt=F32, stack=ctx):
            return stack.enter_context(nc.sbuf_tensor(name, shape, dt))

        def sem(name, stack=ctx):
            return stack.enter_context(nc.semaphore(name))

        probs_dram = nc.dram_tensor("probs_by_expert", [E + 1, N], F32, kind="Internal").ap()
        psum = ctx.enter_context(nc.psum_tensor("psum", [P, 8, 512], F32))
        xT = sb("xT", [P, NC, N])
        ident = sb("ident", [P, P])
        ones = sb("ones", [P, P])
        minus_half = sb("minus_half", [P, 16])

        attn = ExitStack()
        with attn:
            small = sb("small", [P, SMALL["end"]], stack=attn)
            key_scale = sb("key_scale", [P, 2, H], stack=attn)
            bias_cols = sb("bias_cols", [P, H, 4], stack=attn)
            bias_high = sb("bias_high", [P, H, 4], F32R, attn)
            bias_low = sb("bias_low", [P, H, 4], F32R, attn)
            v_bias = sb("v_bias", [P, H], stack=attn)
            x_high = sb("x_high", [P, NC, N], F32R, attn)
            x_low = sb("x_low", [P, NC, N], F32R, attn)
            gram_high = sb("gram_high", [P, 2, NC, DIM], F32R, attn)
            gram_low = sb("gram_low", [P, 2, NC, DIM], F32R, attn)
            twice_wb = sb("twice_wb", [P, 2, DIM], stack=attn)
            bb_eps = sb("bb_eps", [P, 2], stack=attn)
            ones_r = sb("ones_r", [P, P], F32R, attn)
            rank_w = sb("rank_w", [P, RANK_RING, P], F32R, attn)
            prologue(nc, xT_in, kwb_in, small_in, psum, xT, ident, ones, minus_half, small, key_scale, bias_cols,
                     bias_high, bias_low, v_bias, x_high, x_low, gram_high, gram_low, twice_wb, bb_eps, ones_r,
                     rank_w)
            attention(nc, ctx_in, qw_in, kw_in, vw_in, psum, xT, ident, ones, minus_half, small, key_scale,
                      bias_high, bias_low, v_bias, x_high, x_low, gram_high, gram_low, twice_wb, bb_eps, ones_r,
                      rank_w)
        experts(nc, router_in, bias_in, ffn_in, out, probs_dram, psum, xT, ident, ones, minus_half)


def prologue(nc, xT_in, kwb_in, small_in, psum, xT, ident, ones, minus_half, small, key_scale, bias_cols, bias_high,
             bias_low, v_bias, x_high, x_low, gram_high, gram_low, twice_wb, bb_eps, ones_r, rank_w):
    ctx = ExitStack()
    with ctx:
        sb = lambda n, s, dt=F32: ctx.enter_context(nc.sbuf_tensor(n, s, dt))
        sem = lambda n: ctx.enter_context(nc.semaphore(n))
        KW = 4
        WB = DIM + 2
        kw = sb("kw", [P, KW, 2 * WB])
        kw_high, kw_low = sb("kw_high", [P, 2, 2 * WB], F32R), sb("kw_low", [P, 2, 2 * WB], F32R)
        wb_cols, bb_cols = sb("wb_cols", [P, 2 * NC]), sb("bb_cols", [P, 2])
        bb_products = sb("bb_products", [P, 2, H])
        kw_high_ready, kw_split = sem("kw_high_ready"), sem("kw_split")
        bb_ready, cols_ready, cols_wide = sem("bb_ready"), sem("cols_ready"), sem("cols_wide")
        GRAM = 3
        xn = sb("xn", [P, NC, N])
        x_loaded, small_loaded = sem("x_loaded"), sem("small_loaded")
        kw_loaded = [sem(f"kw_loaded{i}") for i in range(KW)]
        kw_used, const_ready, ident_ready = sem("kw_used"), sem("const_ready"), sem("ident_ready")
        scale_ready, bias_ready, bias_high_ready, bias_split = (
            sem("scale_ready"), sem("bias_ready"), sem("bias_high_ready"), sem("bias_split"))
        gram_high_ready, gram_split = sem("gram_high_ready"), sem("gram_split")
        x_high_ready, x_split = sem("x_high_ready"), sem("x_split")
        ln_pe, ln_dve, ln_pool, ln_done = layer_norm(
            nc, ctx, "ln1", xT, lambda c: xn[:, c, :].rearrange("p (h n) -> p h n", h=2), psum[:, 0:3, :])
        kb = small[:, SMALL["kb"]:SMALL["kb"] + 2 * H].rearrange("p (s h) -> p s h", s=2)
        nk = small[:, SMALL["nk"]:SMALL["nk"] + 2 * H].rearrange("p (s h) -> p s h", s=2)
        nq = small[:, SMALL["nq"]:SMALL["nq"] + H]
        vb = small[:, SMALL["vb"]:SMALL["vb"] + 2 * H].rearrange("p (s h) -> p s h", s=2)
        block = ctx.enter_context(nc.Block())

        @block.sync
        def _(sp):
            sp.dma_start(xT[:, :, :], xT_in).then_inc(x_loaded, 16)
            sp.dma_start(small[:, :], small_in).then_inc(small_loaded, 16)
            for h in range(H):
                if h >= KW:
                    sp.wait_ge(kw_split, h - KW + 1)
                sp.dma_start(kw[:, h % KW, :], kwb_in[h, :, :]).then_inc(kw_loaded[h % KW], 16)

        @block.gpsimd
        def _(gp):
            nc.gpsimd.memset(ident[:, :], 0.0).then_inc(ident_ready, 1)
            nc.gpsimd.memset(ones[:, :], 1.0).then_inc(const_ready, 1)
            nc.gpsimd.memset(minus_half[:, :], -0.5).then_inc(const_ready, 1)
            gp.wait_ge(ident_ready, 1)
            nc.gpsimd.affine_select(out=ident[:, :], in_=ident[:, :], compare_op=ALU.not_equal, fill=1.0, base=0,
                                    pattern=[[-1, P]], channel_multiplier=1).then_inc(const_ready, 1)
            ln_pool(gp, minus_half)

        @block.tensor
        def _(pe):
            def gram(heads):
                for h in heads:
                    pe.wait_ge(kw_split, h + 1)
                    for s in range(2):
                        high, low = [x[:, h % 2, s * WB:(s + 1) * WB] for x in (kw_high, kw_low)]
                        for c in range(NC):
                            out, cols = psum[:, GRAM + s * NC + c, 0:WB], slice(c * P, (c + 1) * P)
                            nc.tensor.matmul(out, high[:, cols], high, start=h == 0, stop=False)
                            nc.tensor.matmul(out, high[:, cols], low, start=False, stop=False)
                            last = nc.tensor.matmul(out, low[:, cols], high, start=False, stop=h == H - 1)
                    last.then_inc(kw_used, 1)

            pe.wait_ge(const_ready, 3)
            pe.wait_ge(x_loaded, 16)
            ln_pe(pe, ones, ident, (lambda: gram(range(0, 4)), lambda: gram(range(4, 7))))
            gram(range(7, H))
            pe.wait_ge(cols_ready, 1)
            pe.wait_ge(ln_done, NC)
            for k in range(2 * NC):
                nc.tensor.matmul(psum[:, 1 + k // 2, (k % 2) * P:(k % 2 + 1) * P],
                                 wb_cols[:, k:k + 1].to_broadcast([P, P]), ident[:, :], start=True, stop=True)
            pe.wait_ge(bb_ready, 2)
            nc.tensor.matmul(psum[:, 0, 0:2], ones[:, :], bb_cols[:, :], start=True, stop=True).then_inc(cols_wide, 1)

        @block.scalar
        def _(act):
            def split(heads):
                for h in heads:
                    act.wait_ge(kw_loaded[h % KW], 16 * (h // KW + 1))
                    if h >= 2:
                        act.wait_ge(kw_used, h - 1)
                    nc.scalar.activation(kw_high[:, h % 2, :], kw[:, h % KW, :], ACT.Copy).then_inc(kw_high_ready, 1)

            split(range(0, 2))
            act.wait_ge(bias_ready, 4)
            nc.scalar.activation(bias_high[:, :, :], bias_cols[:, :, :], ACT.Copy).then_inc(bias_high_ready, 1)
            split(range(2, 9))
            for c in range(NC):
                act.wait_ge(ln_done, c + 1)
                nc.scalar.activation(x_high[:, c, :], xn[:, c, :], ACT.Copy).then_inc(x_high_ready, 1)
            split(range(9, H))
            act.wait_ge(kw_used, H)
            nc.scalar.activation(gram_high[:, :, :, :], psum[:, GRAM:GRAM + 4, 0:DIM]
                                 .rearrange("p (s c) n -> p s c n", s=2), ACT.Copy).then_inc(gram_high_ready, 1)

        @block.vector
        def _(dve):
            dve.wait_ge(const_ready, 1)
            nc.vector.tensor_copy(ones_r[:, :], ones[:, :])
            nc.vector.tensor_scalar(rank_w[:, :, :], ones[:, 0:1].to_broadcast([P, RANK_RING, P]), 0.0, None,
                                    ALU.mult).then_inc(scale_ready, 1)
            dve.wait_ge(scale_ready, 1)
            for s in range(2):
                for row in (32 * s, 64 + 32 * s):
                    nc.vector.tensor_copy(rank_w[row:row + 1, 2 * s:2 * s + 2, :],
                                          ones[row:row + 1, :].unsqueeze(1).to_broadcast([1, 2, P]))\
                        .then_inc(scale_ready, 1)
            dve.wait_ge(small_loaded, 16)
            for s in range(2):
                nc.vector.scalar_tensor_tensor(key_scale[:, s, :], nk[:, s, :], float(D) ** -0.5, nq, ALU.mult,
                                               ALU.mult).then_inc(scale_ready, 1)
            dve.wait_ge(scale_ready, 7)
            for s in range(2):
                for i in range(2):
                    nc.vector.tensor_tensor(bias_cols[:, :, s + 2 * i], kb[:, s, :], key_scale[:, s, :], ALU.mult)\
                        .then_inc(bias_ready, 1)
            nc.vector.tensor_tensor(v_bias[:, :], vb[:, 0, :], vb[:, 1, :], ALU.add).then_inc(scale_ready, 1)
            dve.wait_ge(bias_high_ready, 1)
            dve.wait_ge(bias_ready, 4)
            nc.vector.tensor_tensor(bias_low[:, :, :], bias_cols[:, :, :], bias_high[:, :, :].bitcast(F32),
                                    ALU.subtract).then_inc(bias_split, 1)
            for s in range(2):
                nc.vector.tensor_tensor_reduce(out=bb_products[:, s, :], in0=kb[:, s, :], in1=kb[:, s, :], scale=1.0,
                                               scalar=0.0, op0=ALU.mult, op1=ALU.add, accum_out=bb_cols[:, s:s + 1])\
                    .then_inc(bb_ready, 1)

            def split(heads):
                for h in heads:
                    dve.wait_ge(kw_high_ready, h + 1)
                    nc.vector.tensor_tensor(kw_low[:, h % 2, :], kw[:, h % KW, :], kw_high[:, h % 2, :].bitcast(F32),
                                            ALU.subtract).then_inc(kw_split, 1)
            split(range(0, 2))
            ln_dve(dve, (lambda: split(range(2, 4)), lambda: split(range(4, 7))))
            split(range(7, 9))
            for c in range(NC):
                dve.wait_ge(x_high_ready, c + 1)
                nc.vector.tensor_tensor(x_low[:, c, :], xn[:, c, :], x_high[:, c, :].bitcast(F32), ALU.subtract)\
                    .then_inc(x_split, 1)
            split(range(9, H))
            dve.wait_ge(gram_high_ready, 1)
            nc.vector.tensor_copy(wb_cols[:, :], psum[:, GRAM:GRAM + 4, DIM]).then_inc(cols_ready, 1)
            nc.vector.tensor_tensor(gram_low[:, :, :, :].rearrange("p s c n -> p (s c) n"),
                                    psum[:, GRAM:GRAM + 4, 0:DIM],
                                    gram_high[:, :, :, :].bitcast(F32).rearrange("p s c n -> p (s c) n"),
                                    ALU.subtract).then_inc(gram_split, 1)
            dve.wait_ge(cols_wide, 1)
            nc.vector.tensor_scalar(twice_wb[:, :, :], psum[:, 1:3, 0:DIM], 2.0, None, ALU.mult).then_inc(gram_split, 1)
            nc.vector.tensor_scalar(bb_eps[:, :], psum[:, 0, 0:2], 1.0 / INNER, EPS_RMS, ALU.mult, ALU.add)\
                .then_inc(gram_split, 1)


def attention(nc, ctx_in, qw_in, kw_in, vw_in, psum, xT, ident, ones, minus_half, small, key_scale, bias_high,
              bias_low, v_bias, x_high, x_low, gram_high, gram_low, twice_wb, bb_eps, ones_r, rank_w):
    ctx = ExitStack()
    with ctx:
        sb = lambda n, s, dt=F32: ctx.enter_context(nc.sbuf_tensor(n, s, dt))
        names = {}

        def sem(n):
            names[n] = ctx.enter_context(nc.semaphore(n))
            return names[n]

        rows_uo = sb("rows_uo", [P, GB * 4, HS])
        rank_rows = sb("rank_rows", [P, GB, HS], F32R)
        q_raw = sb("q_raw", [P, H, GN])
        square_w = sb("square_w", [P, H, 1 + 2 * H])
        bound_sq = sb("bound_sq", [TOK, 2])
        bound_max = sb("bound_max", [TOK, 1])
        bound_row = sb("bound_row", [1, 1])
        is_safe = sb("is_safe", [1, 1], mybir.dt.int32)
        q_ms = sb("q_ms", [TOK, 2])
        q_rms = sb("q_rms", [TOK, 2])
        q_rms_wide = sb("q_rms_wide", [P, GN])
        square_sums = q_rms_wide[0:1 + 2 * H, :]
        q_hat = sb("q_hat", [P, WRING, GN])
        v_out = q_hat
        v_high = sb("v_high", [P, 2, GN], F32R)
        v_low = sb("v_low", [P, 2, GN], F32R)
        VCOLS = 3 * DIM
        w_stage = sb("w_stage", [P, WRING, 2 * DIM])
        v_stage = q_raw[:, :, :].rearrange("p h n -> p (h n)")[:, 0:WRING * VCOLS].rearrange("p (r n) -> p r n", r=WRING)
        UCOLS, WCOLS, RCOLS = 2 * NC * HS, 2 * DIM, 4 * GN
        shared = sb("shared", [P, 2, max(UCOLS, 2 * WCOLS + 3 * RCOLS + DIM)], F32R)
        u_high, u_low = [shared[:, i, 0:UCOLS].rearrange("p (r n) -> p r n", r=4) for i in range(2)]
        stage = sb("stage", [P, STAGE_RING + 1, 2 * DIM])
        q_square = stage[:, 2, 0:2 * GN].rearrange("p (a n) -> p a n", a=2)
        square_w_ring = stage[:, 3, 0:WRING * (1 + 2 * H)].rearrange("p (a n) -> p a n", a=WRING)
        c_high = sb("c_high", [P, CTX_RING + 1, 2 * DIM], F32R)
        c_low = sb("c_low", [P, CTX_RING + 1, 2 * DIM], F32R)
        c_twice = sb("c_twice", [P, 2, DIM])
        junk = sb("junk", [P, DIM], mybir.dt.bfloat16)
        key_lin = sb("key_lin", [P, 2])
        key_ms = sb("key_ms", [P, TILES])
        key_rms = sb("key_rms", [P, TILES])
        probs = sb("probs", [P, 2, HALF])
        p_high = sb("p_high", [P, 2, HALF], F32R)
        p_low = sb("p_low", [P, 2, HALF], F32R)
        zeros = sb("zeros", [P, 1])
        p_sum = sb("p_sum", [P, 4, HALF])
        p_sum_high = sb("p_sum_high", [P, HALF], F32R)
        p_sum_low = sb("p_sum_low", [P, HALF], F32R)
        taken = lambda i, col, cols: shared[:, i, col:col + cols]
        flat2 = lambda x: x.rearrange("p a n -> p (a n)")
        w_high, w_low = [[taken(i, 0, WCOLS), taken(i, WCOLS, WCOLS), c[:, 2, :], c[:, 3, :]]
                         for i, c in enumerate((c_high, c_low))]
        r_high, r_low = [[taken(i, 2 * WCOLS, RCOLS), taken(i, 2 * WCOLS + RCOLS, RCOLS), flat2(parts[:, :, :]),
                          taken(i, 2 * WCOLS + 2 * RCOLS, RCOLS)] for i, parts in enumerate((p_high, p_low))]
        ow_high, ow_low = [[taken(i, 2 * WCOLS + 3 * RCOLS, DIM), c[:, CTX_RING, 0:DIM], c[:, CTX_RING, DIM:2 * DIM],
                            sums[:, 0:DIM]] for i, (c, sums) in enumerate(((c_high, p_sum_high), (c_low, p_sum_low)))]
        bias_wide_high, bias_wide_low = [c[:, CTX_RING, :].rearrange("p (r a b) -> p r a b", r=WRING, a=4)
                                         for c in (c_high, c_low)]
        recip = sb("recip", [P, HALF])

        BOUND_STEPS, START_STEPS = 5, 7
        O, SC, GRAM, SUM = 0, 4, 6, 7

        inverse_dram = nc.dram_tensor("inverse_rms", [B * TILES, 2, P], F32, kind="Internal").ap()
        negative_dram = nc.dram_tensor("negative_maxima", [B, 2 * HS // P, P], F32, kind="Internal").ap()
        flat = q_raw[:, :, :].rearrange("p h n -> p (h n)")
        max_run = flat[:, 0:2 * HS].rearrange("p (s n) -> p s n", s=4)
        max_twice = flat[:, 2 * HS:2 * HS + DIM]
        at = 2 * HS + DIM
        max_lin, max_ms, max_root, max_inverse = [flat[:, at + TILES * i:at + TILES * (i + 1)] for i in range(4)]
        max_cols = flat[:, at + 4 * TILES:at + 4 * TILES + 2 * HS // P]
        inverse = p_low[:, 0, 0:2 * TILES].rearrange("p (t r) -> p t r", r=2)
        negative = p_low[:, 1, 0:2 * HS // P]
        MAX_SLOT = 2
        (max_loaded, max_high, max_low, max_terms, max_scores, max_summed, max_rooted, max_tile_done, max_u_high,
         max_u_split, max_flipped, max_steps, max_found, max_listed, max_stored) = [sem(f"max_{n}") for n in (
             "loaded", "high", "low", "terms", "scores", "summed", "rooted", "tile_done", "u_high", "u_split",
             "flipped", "steps", "found", "listed", "stored")]
        start_ready = sem("start_ready")
        ctx_loaded = [sem(f"ctx_loaded{i}") for i in range(STAGE_RING + 1)]
        w_loaded = [sem(f"w_loaded{i}") for i in range(WRING)]
        rank_loaded = [sem(f"rank_loaded{i}") for i in range(RANK_RING)]
        zeros_stored = sem("zeros_stored")
        ctx_high, ctx_low, ctx_twice, stage_used = sem("ctx_high"), sem("ctx_low"), sem("ctx_twice"), sem("stage_used")
        gram_done, norm_summed, key_norm = sem("gram_done"), sem("norm_summed"), sem("key_norm")
        u_high_ready, u_split = sem("u_high_ready"), sem("u_split")
        scores_done, exp_done, probs_split, av_done = (
            sem("scores_done"), sem("exp_done"), sem("probs_split"), sem("av_done"))
        sum_added, sum_high_ready, sum_split = sem("sum_added"), sem("sum_high_ready"), sem("sum_split")
        sum_wide, recip_ready, o_copied, o_scaled = sem("sum_wide"), sem("recip_ready"), sem("o_copied"), sem("o_scaled")
        ow_high_ready, bias_zeroed, square_w_placed = sem("ow_high_ready"), sem("bias_zeroed"), sem("square_w_placed")
        q_w_high_ready, w_high_ready, w_low_ready, w_used = sem("q_w_high_ready"), sem("w_high_ready"), sem("w_low"), sem("w_used")
        q_copied, squares_summed, sums_copied, sums_flipped = (
            sem("q_copied"), sem("squares_summed"), sem("sums_copied"), sem("sums_flipped"))
        bound_step, bound_flat, safe_known, judgement_read = (
            sem("bound_step"), sem("bound_flat"), sem("safe_known"), sem("judgement_read"))
        q_ms_ready, q_rms_ready, q_wide, q_wide_copied = (
            sem("q_ms_ready"), sem("q_rms_ready"), sem("q_wide"), sem("q_wide_copied"))
        q_scaled, q_high_ready, q_split, bias_copied = (
            sem("q_scaled"), sem("q_high_ready"), sem("q_split"), sem("bias_copied"))
        bias_ready, u_copied, rank_copied, u_text_copied = (
            sem("bias_ready"), sem("u_copied"), sem("rank_copied"), sem("u_text_copied"))
        o_high_ready, o_split, v_done, v_copied, v_high_ready, v_split = (
            sem("o_high_ready"), sem("o_split"), sem("v_done"), sem("v_copied"), sem("v_high_ready"), sem("v_split"))
        y_done, y_added = sem("y_done"), sem("y_added")
        block = ctx.enter_context(nc.Block())

        def last_unit_of_buffer(it, t):
            back, k = before(t, CTX_RING)
            return UNITS * (it - back) + 2 * k + 2 + CREDIT["av_done"]

        def w_index(g, phase, h):
            return 3 * H * g + H * phase + h

        def batches(eng, g, body, tail):
            body(GB * g, 0, False, True)
            with eng.Fori(1, GB - 1) as j:
                body(GB * g + j, j, True, True)
            body(GB * g + GB - 1, GB - 1, True, False)
            tail(GB * g + GB, GB)

        def heads(eng, main, prepare=None, lead=2):
            def step(quad, i, last):
                n = i + lead
                if prepare is not None and not (last and n >= WRING):
                    prepare(WRING * quad + n, n % WRING, quad + n // WRING, False)
                main(WRING * quad + i, i, quad, last and i == WRING - 1)
            if prepare is not None:
                for n in range(lead):
                    prepare(n, n, 0, False)
            with eng.Fori(0, H // WRING - 1) as quad:
                for i in range(WRING):
                    step(quad, i, False)
            for i in range(WRING):
                step(H // WRING - 1, i, True)

        def where_unsafe(eng, g, maxima, no_maxima):
            eng.wait_ge(safe_known, g + 1)
            eng.sem_inc(judgement_read, 1)
            safe = eng.value_load(is_safe[0:1, 0:1], min_val=0, max_val=1)
            eng.sem_inc(judgement_read, 1)
            with eng.If(safe == 0):
                with eng.Fori(0, GB) as j:
                    maxima(GB * g + j, j)
            with eng.Else():
                no_maxima()

        def ahead(it, t):
            return (it, t) if t < TILES else (it + 1, t - TILES)

        @block.sync
        def _(sp):
            def load_tile(it, t):
                back, k = before(t, STAGE_RING)
                sp.wait_ge(stage_used, TILES * (it - back) + k + 1 + CREDIT["stage_used"])
                sp.dma_start(stage[:, slot(t, STAGE_RING), :], ctx_in[ds(TILES * it + t, 1), :, :]
                             .rearrange("a p n -> p (a n)")).then_inc(ctx_loaded[slot(t, STAGE_RING)], 16)

            def load_weights(g, phase, src, stage_of, cols):
                def load(h, i, nth, last):
                    sp.wait_ge(w_low_ready, w_index(g, phase, h) - WRING + 1 + CREDIT["w_low"])
                    sp.dma_start(stage_of[:, i, 0:cols], src[ds(h, 1), :, :].rearrange("a p n -> p (a n)"))\
                        .then_inc(w_loaded[i], 16)
                heads(sp, load)

            def load_rank(it, t):
                i, (back, k) = rank_slot(t)
                sp.wait_ge(scores_done, UNITS * (it - back) + 2 * k + 2 + CREDIT["scores_done"])
                row = 32 * (i // 2) + 1
                sp.dma_start(rank_w[row:row + 2, i, :].bitcast(F32), inverse_dram[ds(TILES * it + t, 1), :, :]
                             .rearrange("a r n -> (a r) n")).then_inc(rank_loaded[i], 16)

            def maxima(it, bl):
                for t in range(TILES):
                    sp.wait_ge(max_tile_done, TILES * it + t + CREDIT["max_tile_done"])
                    sp.dma_start(stage[:, MAX_SLOT, :], ctx_in[ds(TILES * it + t, 1), :, :]
                                 .rearrange("a p n -> p (a n)")).then_inc(max_loaded, 16)
                sp.wait_ge(max_found, it + 1)
                sp.dma_start(negative_dram[ds(it, 1), :, :].rearrange("a k n -> n (a k)"), negative.bitcast(F32),
                             allow_slow_non_contiguous=True)\
                    .then_inc(max_listed, 16)
                sp.dma_start(inverse_dram[ds(TILES * it, TILES), :, :].rearrange("t r n -> n t r"), inverse.bitcast(F32),
                             allow_slow_non_contiguous=True)\
                    .then_inc(max_listed, 16)
                sp.wait_ge(max_listed, 32 * (it + 1))
                for s in range(2):
                    for row in (32 * s + 1, 32 * s + 2):
                        sp.dma_start(rank_rows[row:row + 1, ds(bl, 1), :].rearrange("p a n -> p (a n)").bitcast(F32),
                                     negative_dram[ds(it, 1), 7 * s:7 * s + 7, :].rearrange("a k n -> a (k n)"))\
                            .then_inc(max_stored, 16)

            def no_maxima():
                sp.sem_inc(max_loaded, 16 * GB * TILES)
                sp.sem_inc(max_listed, 32 * GB)
                sp.sem_inc(max_stored, 64 * GB)

            sp.wait_ge(start_ready, START_STEPS)
            sp.dma_start(inverse_dram.rearrange("a r n -> (a r n)").rearrange("(p n) -> p n", p=P),
                         p_sum[:, :, :].rearrange("p a n -> p (a n)")[:, 0:B * TILES * 2]).then_inc(zeros_stored, 16)
            for t in range(PREP):
                load_tile(0, t)
            sp.wait_ge(zeros_stored, 16)
            with sp.Fori(0, NG) as g:
                load_weights(g, 0, qw_in, w_stage, DIM)
                load_weights(g, 1, kw_in, w_stage, 2 * DIM)
                where_unsafe(sp, g, maxima, no_maxima)
                with sp.Fori(0, GB) as j:
                    load_rank(GB * g + j, 0)
                    for t in range(TILES):
                        load_tile(*ahead(GB * g + j, t + PREP))
                        if t + 1 < TILES:
                            load_rank(GB * g + j, t + 1)
                load_weights(g, 2, vw_in, v_stage, VCOLS)

        @block.tensor
        def _(pe):
            pe.sem_inc(scores_done, CREDIT["scores_done"])
            pe.sem_inc(av_done, CREDIT["av_done"])
            pe.sem_inc(w_used, CREDIT["w_used"])
            pe.sem_inc(v_done, CREDIT["v_done"])
            pe.sem_inc(squares_summed, CREDIT["squares_summed"])
            pe.sem_inc(y_done, CREDIT["y_done"])
            pe.sem_inc(sum_wide, CREDIT["sum_wide"])
            pe.sem_inc(max_scores, CREDIT["max_scores"])

            def three(out, high, low, rhigh, rlow, start, stop):
                nc.tensor.matmul(out, high, rhigh, start=start, stop=False)
                nc.tensor.matmul(out, high, rlow, start=False, stop=False)
                return nc.tensor.matmul(out, low, rhigh, start=False, stop=stop)

            def queries(g):
                zero = zeros[:, :].to_broadcast([P, 1 + 2 * H])
                nc.tensor.matmul(psum[0:1 + 2 * H, 2, 0:GN], zero, zeros[:, :].to_broadcast([P, GN]), start=True,
                                 stop=False)

                def products(h, i, nth, last):
                    pe.wait_ge(w_low_ready, w_index(g, 0, h) + 1 + CREDIT["w_low"])
                    pe.wait_ge(q_copied, H * g + h - 1 + CREDIT["q_copied"])
                    for c in range(NC):
                        cols = slice(c * P, (c + 1) * P)
                        last = three(psum[:, i % 2, 0:GN], w_high[i][:, cols], w_low[i][:, cols],
                                     x_high[:, c, ds(GN * g, GN)], x_low[:, c, ds(GN * g, GN)],
                                     c == 0, c == NC - 1)
                    last.then_inc(w_used, 1)

                def squares(h, i, nth, last):
                    pe.wait_ge(q_copied, H * g + h + 1 + CREDIT["q_copied"])
                    pe.wait_ge(square_w_placed, H * g + h + 1)
                    nc.tensor.matmul(psum[0:1 + 2 * H, 2, 0:GN], square_w_ring[:, i, :], q_square[:, i % 2, :],
                                     start=False, stop=last)\
                        .then_inc(squares_summed, 1)
                heads(pe, squares, products, lead=1)
                pe.wait_ge(sums_copied, g + 1)
                for i in range(2):
                    last = nc.tensor.matmul(psum[0:TOK, 3, i * P:i * P + 1 + 2 * H],
                                            square_sums[:, TOK * i:TOK * i + TOK],
                                            ident[0:1 + 2 * H, 0:1 + 2 * H], start=True, stop=True)
                last.then_inc(sums_flipped, 1)
                pe.wait_ge(q_rms_ready, g + 1)
                for i in range(2):
                    last = nc.tensor.matmul(psum[:, 2, TOK * i:TOK * i + TOK],
                                            q_rms[:, i:i + 1].to_broadcast([TOK, P]), ident[0:TOK, 0:TOK],
                                            start=True, stop=True)
                last.then_inc(q_wide, 1)
                pe.wait_ge(bound_step, BOUND_STEPS * g + 4)
                pe.wait_ge(recip_ready, 4 * GB * g + CREDIT["recip_ready"])
                nc.tensor.matmul(psum[0:1, SUM, 0:TOK], bound_max[:, :], ident[0:TOK, 0:TOK], start=True, stop=True)\
                    .then_inc(bound_flat, 1)

            def absorb(g):
                def products(h, i, nth, last):
                    pe.wait_ge(q_wide_copied, g + 1)
                    pe.wait_ge(w_low_ready, w_index(g, 1, h) + 1 + CREDIT["w_low"])
                    pe.wait_ge(q_split, H * g + h + 1 + CREDIT["q_split"])
                    pe.wait_ge(bias_ready, H * g + h + 1)
                    pe.wait_ge(u_copied, H * g + h - 1 + CREDIT["u_copied"])
                    pe.wait_ge(u_text_copied, H * g + h - 1 + CREDIT["u_text_copied"])
                    for s in range(2):
                        for c in range(NC):
                            cols = slice(s * DIM + c * P, s * DIM + (c + 1) * P)
                            three(psum[:, 2 * (i % 2) + s, c * GN:(c + 1) * GN], w_high[i][:, cols],
                                  w_low[i][:, cols], r_high[i][:, 0:GN], r_low[i][:, 0:GN], True, True)
                    wide = [x[:, i, :, :].rearrange("p a b -> p (a b)") for x in (bias_wide_high, bias_wide_low)]
                    three(psum[:, 4 + i % 2, 0:GN], *wide, r_high[i][:, 0:GN], r_low[i][:, 0:GN], True, True)\
                        .then_inc(w_used, 1)
                heads(pe, products)

            def gram(it, t):
                s = int(t >= IMG_TILES)
                k = slot(t, CTX_RING)
                pe.wait_ge(ctx_high, TILES * it + t + 1)
                pe.wait_ge(norm_summed, TILES * it + t + CREDIT["norm_summed"])
                for c in range(NC):
                    for i, part in enumerate((gram_high, gram_low)):
                        last = nc.tensor.matmul(psum[:, GRAM, 0:DIM], c_high[:, k, c * P:(c + 1) * P],
                                                part[:, s, c, :], start=c == 0 and i == 0, stop=c == 1 and i == 1)
                last.then_inc(gram_done, 1)

            def scores(it, bl, u):
                t, half = divmod(u, 2)
                s, k = int(t >= IMG_TILES), slot(t, CTX_RING)
                cols = slice(half * HALF, (half + 1) * HALF)
                if t in (0, IMG_TILES):
                    pe.wait_ge(u_split, 4 * it + 2 * s + half + 1)
                if half == 0:
                    pe.wait_ge(ctx_low, TILES * it + t + 1)
                    i = rank_slot(t)[0]
                    of_slot = [x for x in range(TILES) if rank_slot(x)[0] == i]
                    pe.wait_ge(rank_loaded[i], 16 * (len(of_slot) * it + of_slot.index(t) + 1))
                pe.wait_ge(exp_done, UNITS * it + u - 1 + CREDIT["exp_done"])
                out = psum[:, SC + half, 0:HALF]
                for c in range(NC):
                    w = slice(c * P, (c + 1) * P)
                    three(out, c_high[:, k, w], c_low[:, k, w], u_high[:, 2 * s + c, cols], u_low[:, 2 * s + c, cols],
                          c == 0, False)
                nc.tensor.matmul(out, rank_w[:, rank_slot(t)[0], :], rank_rows[:, ds(bl, 1), cols].rearrange("p a n -> p (a n)"),
                                 start=False, stop=True).then_inc(scores_done, 1)

            def average(it, u):
                t, half = divmod(u, 2)
                s, k, n = int(t >= IMG_TILES), slot(t, CTX_RING), ROWS[t]
                pe.wait_ge(probs_split, UNITS * it + u + 1 + CREDIT["probs_split"])
                first, last_tile = t in (0, IMG_TILES), t in (IMG_TILES - 1, TILES - 1)
                if first:
                    pe.wait_ge(o_copied, 4 * it + 2 * s + half - 1 + CREDIT["o_copied"])
                for c in range(NC):
                    w = slice(DIM + c * P, DIM + (c + 1) * P)
                    last = three(psum[:, O + 2 * half + c, 0:HALF], c_high[0:n, k, w], c_low[0:n, k, w],
                                 p_high[0:n, half, :], p_low[0:n, half, :], first, last_tile)
                last.then_inc(av_done, 1)

            def sums(it, s, half):
                n = 4 * it + 2 * s + half
                pe.wait_ge(sum_split, n + 1 + CREDIT["sum_split"])
                pe.wait_ge(recip_ready, n + CREDIT["recip_ready"])
                nc.tensor.matmul(psum[:, SUM, 0:HALF], ones_r[:, :], p_sum_high[:, :], start=True, stop=False)
                nc.tensor.matmul(psum[:, SUM, 0:HALF], ones_r[:, :], p_sum_low[:, :], start=False, stop=True)\
                    .then_inc(sum_wide, 1)

            def carried(it, step):
                if step < 2:
                    average(it - 1, UNITS - 2 + step)
                if step == 3:
                    sums(it - 1, 1, 0)
                if step == 7:
                    sums(it - 1, 1, 1)

            def body(it, bl, has_prev, has_next):
                for step in range(UNITS):
                    if step % 2 == 0:
                        gram(*ahead(it, step // 2 + 1))
                    scores(it, bl, step)
                    if step >= 2:
                        average(it, step - 2)
                    if has_prev:
                        carried(it, step)
                    if step == 10:
                        sums(it, 0, 0)
                    if step == 14:
                        sums(it, 0, 1)

            def tail(it, bl):
                for step in range(8):
                    carried(it, step)

            def outputs(g):
                def values(h, i, nth, last):
                    pe.wait_ge(w_low_ready, w_index(g, 2, h) + 1 + CREDIT["w_low"])
                    pe.wait_ge(o_split, H * g + h + 1)
                    pe.wait_ge(v_copied, H * g + h - WRING + 1 + CREDIT["v_copied"])
                    for k in range(4):
                        cols, r = slice(k * P, (k + 1) * P), slice(k * GN, (k + 1) * GN)
                        last = three(psum[:, i, 0:GN], w_high[i][:, cols], w_low[i][:, cols], r_high[i][:, r],
                                     r_low[i][:, r], k == 0, k == 3)
                    last.then_inc(v_done, 1)

                def project(h, i, nth, last):
                    pe.wait_ge(v_split, H * g + h + 1 + CREDIT["v_split"])
                    for c in range(NC):
                        cols = slice(c * P, (c + 1) * P)
                        done = three(psum[:, 4 + c, 0:GN], ow_high[i][:, cols], ow_low[i][:, cols],
                                     v_high[:, i % 2, :], v_low[:, i % 2, :], False, last)
                    done.then_inc(y_done, 1)

                for c in range(NC):
                    nc.tensor.matmul(psum[:, 4 + c, 0:GN], zeros[:, :].to_broadcast([P, P]),
                                     zeros[:, :].to_broadcast([P, GN]), start=True, stop=False)
                heads(pe, project, values)

            def maxima(it, bl):
                pe.wait_ge(max_u_split, it + 1)
                for t in range(TILES):
                    s = int(t >= IMG_TILES)
                    pe.wait_ge(max_low, TILES * it + t + 1)
                    pe.wait_ge(max_tile_done, TILES * it + t + CREDIT["max_tile_done"])
                    for c in range(NC):
                        for i, part in enumerate((gram_high, gram_low)):
                            nc.tensor.matmul(psum[:, GRAM, 0:DIM], c_high[:, MAX_SLOT, c * P:(c + 1) * P],
                                             part[:, s, c, :], start=c == 0 and i == 0, stop=c == 1 and i == 1)
                    for half in range(2):
                        cols = slice(half * HALF, (half + 1) * HALF)
                        out = psum[:, SC + half, 0:HALF]
                        for c in range(NC):
                            w = slice(c * P, (c + 1) * P)
                            three(out, c_high[:, MAX_SLOT, w], c_low[:, MAX_SLOT, w], u_high[:, 2 * s + c, cols],
                                  u_low[:, 2 * s + c, cols], c == 0, False)
                        last = nc.tensor.matmul(out, rank_w[:, 2 * s, :], rank_rows[:, ds(bl, 1), cols]
                                                .rearrange("p a n -> p (a n)"), start=False, stop=True)
                    last.then_inc(max_scores, 1)
                pe.wait_ge(max_tile_done, TILES * (it + 1) + CREDIT["max_tile_done"])
                run = max_run.rearrange("p s n -> p (s n)")
                for k in range(2 * HS // P):
                    last = nc.tensor.transpose(psum[:, k // 4, (k % 4) * P:(k % 4 + 1) * P], run[:, k * P:(k + 1) * P],
                                               ident[:, :])
                last.then_inc(max_flipped, 1)
                pe.wait_ge(max_stored, 64 * (it + 1))

            def no_maxima():
                pe.sem_inc(max_scores, GB * TILES)
                pe.sem_inc(max_flipped, GB)

            pe.wait_ge(start_ready, START_STEPS)
            for t in range(PREP - 1):
                gram(0, t)
            with pe.Fori(0, NG) as g:
                pe.wait_ge(y_added, g + CREDIT["y_added"])
                queries(g)
                absorb(g)
                pe.wait_ge(u_copied, H * (g + 1) + CREDIT["u_copied"])
                pe.wait_ge(u_text_copied, H * (g + 1) + CREDIT["u_text_copied"])
                where_unsafe(pe, g, maxima, no_maxima)
                batches(pe, g, body, tail)
                pe.wait_ge(o_copied, 4 * GB * (g + 1) + CREDIT["o_copied"])
                outputs(g)

        @block.scalar
        def _(act):
            act.sem_inc(exp_done, CREDIT["exp_done"])
            act.sem_inc(q_copied, CREDIT["q_copied"])
            act.sem_inc(u_copied, CREDIT["u_copied"])
            act.sem_inc(v_copied, CREDIT["v_copied"])
            act.sem_inc(o_copied, CREDIT["o_copied"])

            def copy(out, in_, **kw):
                return nc.scalar.activation(out, in_, ACT.Copy, **kw)

            def loaded(g, phase, i, nth):
                act.wait_ge(w_loaded[i], 16 * (3 * (H // WRING) * g + (H // WRING) * phase + nth + 1))

            def queries(g):
                act.wait_ge(w_low_ready, w_index(g, 0, 0) + CREDIT["w_low"])

                def take(h, i, nth, last):
                    bias = small[:, ds(SMALL["qb"] + h, 1)]
                    act.wait_ge(w_used, 2 * H * g + h + 1 + CREDIT["w_used"])
                    act.wait_ge(squares_summed, H * g + h - 1 + CREDIT["squares_summed"])
                    nc.scalar.activation(q_square[:, i % 2, :], psum[:, i % 2, 0:GN], ACT.Square, bias=bias)
                    nc.scalar.activation(q_raw[:, ds(h, 1), :].rearrange("p a n -> p (a n)"), psum[:, i % 2, 0:GN],
                                         ACT.Identity, bias=bias).then_inc(q_copied, 1)
                heads(act, take)
                act.wait_ge(q_wide, g + 1)
                copy(q_rms_wide[:, :], psum[:, 2, 0:GN]).then_inc(q_wide_copied, 1)

            def absorb(g):
                def ready(h, i, nth, last):
                    loaded(g, 1, i, nth)
                    act.wait_ge(w_used, 2 * H * g + H + h - WRING + 1 + CREDIT["w_used"])
                    for s in range(2):
                        cols = slice(s * DIM, (s + 1) * DIM)
                        done = copy(w_high[i][:, cols], w_stage[:, i, cols], scale=key_scale[:, s, ds(h, 1)])
                    done.then_inc(w_high_ready, 1)
                    act.wait_ge(q_scaled, H * g + h + 1 + CREDIT["q_scaled"])
                    copy(r_high[i][:, 0:GN], q_hat[:, i, :]).then_inc(q_high_ready, 1)

                def take(h, i, nth, last):
                    act.wait_ge(w_used, 2 * H * g + H + h + 1 + CREDIT["w_used"])
                    copy(rank_rows[:, :, ds(h * S, S)], psum[:, 4 + i % 2, 0:GN].rearrange("p (b q) -> p b q", b=GB))\
                        .then_inc(rank_copied, 1)
                    uo = rows_uo[:, :, ds(h * S, S)].rearrange("p (b r) q -> p r b q", b=GB)
                    copy(uo[:, 0:2, :, :], psum[:, 2 * (i % 2), 0:2 * GN].rearrange("p (c b q) -> p c b q", c=NC, b=GB))\
                        .then_inc(u_copied, 1)
                heads(act, take, ready)

            def prepare(it, t):
                k, st = slot(t, CTX_RING), slot(t, STAGE_RING)
                per = len([x for x in range(TILES) if slot(x, STAGE_RING) == st])
                nth = len([x for x in range(t) if slot(x, STAGE_RING) == st])
                act.wait_ge(ctx_loaded[st], 16 * (per * it + nth + 1))
                act.wait_ge(av_done, last_unit_of_buffer(it, t))
                copy(c_high[:, k, :], stage[:, st, :]).then_inc(ctx_high, 1)

            def split_u(it, bl, s, half):
                last = UNITS * (it - 1) + (2 * IMG_TILES if s == 0 else UNITS)
                act.wait_ge(scores_done, last + CREDIT["scores_done"])
                cols = slice(half * HALF, (half + 1) * HALF)
                copy(u_high[:, 2 * s:2 * s + 2, cols], rows_uo[:, ds(4 * bl + 2 * s, 2), cols])\
                    .then_inc(u_high_ready, 1)

            def exponentials(it, u):
                t, half = divmod(u, 2)
                act.wait_ge(scores_done, UNITS * it + u + 1 + CREDIT["scores_done"])
                if half == 0:
                    act.wait_ge(key_norm, TILES * it + t + 1)
                act.wait_ge(av_done, UNITS * it + u - 1 + CREDIT["av_done"])
                act.wait_ge(probs_split, UNITS * it + u - 1 + CREDIT["probs_split"])
                act.wait_ge(sum_added, UNITS * it + u - 1 + CREDIT["sum_added"])
                src = psum[:, SC + half, 0:HALF]
                nc.scalar.activation(p_high[:, half, :], src, ACT.Exp, scale=key_rms[:, t:t + 1])
                nc.scalar.activation(probs[:, half, :], src, ACT.Exp, scale=key_rms[:, t:t + 1]).then_inc(exp_done, 1)

            def copy_o(it, bl, s, half):
                last = 2 * (IMG_TILES if s == 0 else TILES) - 2 + half
                act.wait_ge(av_done, UNITS * it + last + 1 + CREDIT["av_done"])
                act.wait_ge(u_split, 4 * it + 2 * s + half + 1)
                cols = slice(half * HALF, (half + 1) * HALF)
                copy(rows_uo[:, ds(4 * bl + 2 * s, 2), cols], psum[:, O + 2 * half:O + 2 * half + 2, 0:HALF])\
                    .then_inc(o_copied, 1)

            def carried(it, bl, step):
                if step == 0:
                    exponentials(it - 1, UNITS - 1)
                if step in (1, 2):
                    copy_o(it - 1, bl - 1, 1, step - 1)

            def body(it, bl, has_prev, has_next):
                if not has_prev:
                    for half in range(2):
                        split_u(it, bl, 0, half)
                for step in range(UNITS):
                    if has_prev:
                        carried(it, bl, step)
                    if step >= 1:
                        exponentials(it, step - 1)
                    if step % 2 == 0:
                        prepare(*ahead(it, step // 2 + PREP))
                    if step in (1, 2):
                        split_u(it, bl, 1, step - 1)
                    if step in (7, 8):
                        copy_o(it, bl, 0, step - 7)
                    if has_next and step in (16, 18):
                        split_u(it + 1, bl + 1, 0, (step - 16) // 2)

            def tail(it, bl):
                for step in range(3):
                    carried(it, bl, step)

            def outputs(g):
                def ready(h, i, nth, last):
                    loaded(g, 2, i, nth)
                    act.wait_ge(v_done, H * g + h - WRING + 1 + CREDIT["v_done"])
                    copy(w_high[i], v_stage[:, i, 0:WCOLS]).then_inc(w_high_ready, 1)
                    act.wait_ge(o_scaled, 4 * GB * (g + 1) + CREDIT["o_scaled"])
                    uo = rows_uo[:, :, ds(h * S, S)].rearrange("p (b r) q -> p r b q", b=GB)
                    copy(r_high[i].rearrange("p (r b q) -> p r b q", r=4, b=GB), uo).then_inc(o_high_ready, 1)

                def take(h, i, nth, last):
                    act.wait_ge(v_done, H * g + h + 1 + CREDIT["v_done"])
                    act.wait_ge(v_split, H * g + h - WRING + 1 + CREDIT["v_split"])
                    nc.scalar.activation(v_out[:, i, :], psum[:, i, 0:GN], ACT.Identity,
                                         bias=v_bias[:, ds(h, 1)]).then_inc(v_copied, 1)
                heads(act, take, ready)

            def maxima(it, bl):
                act.wait_ge(max_scores, TILES * it + CREDIT["max_scores"])
                copy(u_high[:, :, :], rows_uo[:, ds(4 * bl, 4), :]).then_inc(max_u_high, 1)
                for t in range(TILES):
                    act.wait_ge(max_loaded, 16 * (TILES * it + t + 1))
                    act.wait_ge(max_scores, TILES * it + t + CREDIT["max_scores"])
                    copy(c_high[:, MAX_SLOT, :], stage[:, MAX_SLOT, :]).then_inc(max_high, 1)
                act.wait_ge(max_scores, TILES * (it + 1) + CREDIT["max_scores"])
                act.wait_ge(max_stored, 64 * (it + 1))

            def no_maxima():
                act.sem_inc(max_u_high, GB)
                act.sem_inc(max_high, GB * TILES)

            for t in range(PREP):
                prepare(0, t)
            with act.Fori(0, NG) as g:
                queries(g)
                absorb(g)
                act.wait_ge(u_copied, H * (g + 1) + CREDIT["u_copied"])
                act.wait_ge(u_text_copied, H * (g + 1) + CREDIT["u_text_copied"])
                where_unsafe(act, g, maxima, no_maxima)
                batches(act, g, body, tail)
                outputs(g)

        @block.vector
        def _(dve):
            dve.sem_inc(probs_split, CREDIT["probs_split"])
            dve.sem_inc(stage_used, CREDIT["stage_used"])
            dve.sem_inc(u_text_copied, CREDIT["u_text_copied"])
            dve.sem_inc(sum_split, CREDIT["sum_split"])
            dve.sem_inc(w_low_ready, CREDIT["w_low"])
            dve.sem_inc(v_split, CREDIT["v_split"])
            dve.sem_inc(y_added, CREDIT["y_added"])
            dve.sem_inc(recip_ready, CREDIT["recip_ready"])
            dve.sem_inc(o_scaled, CREDIT["o_scaled"])
            dve.sem_inc(norm_summed, CREDIT["norm_summed"])
            dve.sem_inc(max_tile_done, CREDIT["max_tile_done"])
            dve.sem_inc(judgement_read, CREDIT["judgement_read"])

            def sub(out, a, b):
                return nc.vector.tensor_tensor(out, a, b, ALU.subtract)

            def queries(g):
                def ready(h, i, nth, last):
                    dve.wait_ge(w_loaded[i], 16 * (3 * (H // WRING) * g + nth + 1))
                    dve.wait_ge(w_used, 2 * H * g + h - WRING + 1 + CREDIT["w_used"])
                    nc.vector.tensor_copy(w_high[i][:, 0:DIM], w_stage[:, i, 0:DIM]).then_inc(q_w_high_ready, 1)
                    dve.wait_ge(squares_summed, H * g + h - WRING + 1 + CREDIT["squares_summed"])
                    nc.vector.tensor_copy(square_w_ring[:, i, :], square_w[:, ds(h, 1), :]
                                          .rearrange("p a n -> p (a n)")).then_inc(square_w_placed, 1)
                    dve.wait_ge(q_w_high_ready, H * g + h + 1)
                    sub(w_low[i][:, 0:DIM], w_stage[:, i, 0:DIM], w_high[i][:, 0:DIM].bitcast(F32))\
                        .then_inc(w_low_ready, 1)
                heads(dve, ready)
                dve.wait_ge(squares_summed, H * (g + 1) + CREDIT["squares_summed"])
                nc.vector.tensor_copy(square_sums[:, :], psum[0:1 + 2 * H, 2, 0:GN]).then_inc(sums_copied, 1)
                for wide in (bias_wide_high, bias_wide_low):
                    nc.vector.memset(wide.rearrange("p r a b -> p (r a b)").bitcast(F32), 0.0).then_inc(bias_zeroed, 1)
                dve.wait_ge(sums_flipped, g + 1)
                sums = psum[0:TOK, 3, 0:2 * P].rearrange("p (i k) -> p i k", i=2)
                nc.vector.tensor_scalar(q_ms[:, :], sums[:, :, 0], 1.0 / INNER, EPS_RMS, ALU.mult, ALU.add)\
                    .then_inc(q_ms_ready, 1)
                nc.vector.tensor_reduce(bound_sq[:, :], sums[:, :, 1:1 + 2 * H], mybir.AxisListType.X, ALU.max)\
                    .then_inc(bound_step, 1)
                dve.wait_ge(q_rms_ready, g + 1)
                dve.wait_ge(bound_step, BOUND_STEPS * g + 1)
                nc.vector.tensor_tensor(bound_sq[:, :], bound_sq[:, :], q_rms[:, :], ALU.mult).then_inc(bound_step, 1)
                dve.wait_ge(bound_step, BOUND_STEPS * g + 2)
                nc.vector.tensor_tensor(bound_sq[:, :], bound_sq[:, :], q_rms[:, :], ALU.mult).then_inc(bound_step, 1)
                dve.wait_ge(bound_step, BOUND_STEPS * g + 3)
                nc.vector.tensor_reduce(bound_max[:, :], bound_sq[:, :], mybir.AxisListType.X, ALU.max)\
                    .then_inc(bound_step, 1)

            def judge(g):
                dve.wait_ge(bound_flat, g + 1)
                nc.vector.tensor_reduce(bound_row[:, :], psum[0:1, SUM, 0:TOK], mybir.AxisListType.X, ALU.max)\
                    .then_inc(bound_step, 1)
                dve.wait_ge(bound_step, BOUND_STEPS * g + 5)
                dve.wait_ge(judgement_read, 10 * g + CREDIT["judgement_read"])
                nc.vector.tensor_scalar(is_safe[:, :], bound_row[:, :], SAFE_SCORE ** 2 / INNER, None, ALU.is_le)\
                    .then_inc(safe_known, 1)

            def absorb(g):
                def ready(h, i, nth, last):
                    dve.wait_ge(w_high_ready, 2 * H * g + h + 1)
                    for s in range(2):
                        c = slice(s * DIM, (s + 1) * DIM)
                        done = nc.vector.scalar_tensor_tensor(w_low[i][:, c], w_stage[:, i, c],
                                                              key_scale[:, s, ds(h, 1)],
                                                              w_high[i][:, c].bitcast(F32), ALU.mult, ALU.subtract)
                    done.then_inc(w_low_ready, 1)
                    dve.wait_ge(bias_zeroed, 2 * (g + 1))
                    for parts, wide in ((bias_high, bias_wide_high), (bias_low, bias_wide_low)):
                        done = nc.vector.tensor_copy(wide[:, i, :, 0], parts[:, ds(h, 1), :]
                                                     .rearrange("p a n -> p (a n)").bitcast(F32))
                    done.then_inc(bias_ready, 1)

                def take(h, i, nth, last):
                    dve.wait_ge(rank_copied, H * g + h + 1)
                    rows = slice(64, P)
                    at = rank_rows[rows, :, ds(h * S, S)]
                    sub(at, psum[rows, 4 + i % 2, 0:GN].rearrange("p (b q) -> p b q", b=GB), at.bitcast(F32))
                    uo = rows_uo[:, :, ds(h * S, S)].rearrange("p (b r) q -> p r b q", b=GB)
                    nc.vector.tensor_copy(uo[:, 2:4, :, :], psum[:, 2 * (i % 2) + 1, 0:2 * GN]
                                          .rearrange("p (c b q) -> p c b q", c=NC, b=GB)).then_inc(u_text_copied, 1)
                heads(dve, take, ready)

            def prepare(it, t):
                k, st, s, T = slot(t, CTX_RING), slot(t, STAGE_RING), int(t >= IMG_TILES), TILES * it + t
                dve.wait_ge(ctx_high, T + 1)
                sub(c_low[:, k, :], stage[:, st, :], c_high[:, k, :].bitcast(F32)).then_inc(ctx_low, 1)
                return T, k, st, s

            def norm_terms(it, t):
                k, st, s, T = slot(t, CTX_RING), slot(t, STAGE_RING), int(t >= IMG_TILES), TILES * it + t
                dve.wait_ge(ctx_low, T + 1)
                nat = slice(DIM, 2 * DIM)
                nc.vector.tensor_tensor_reduce(out=junk[:, :], in0=stage[:, st, nat], in1=twice_wb[:, s, :],
                                               scale=1.0 / INNER, scalar=bb_eps[:, s:s + 1], op0=ALU.mult,
                                               op1=ALU.add, accum_out=key_lin[:, par_of(t):par_of(t) + 1])
                nc.vector.tensor_tensor(c_twice[:, par_of(t), :], stage[:, st, nat], c_low[:, k, nat].bitcast(F32),
                                        ALU.add).then_inc(stage_used, 1)

            def par_of(t):
                return t % 2 if t < TILES - 1 else 0

            def norm(it, t):
                T = TILES * it + t
                dve.wait_ge(gram_done, T + 1)
                dve.wait_ge(stage_used, T + 1 + CREDIT["stage_used"])
                twice = c_twice[:, par_of(t), :]
                nc.vector.tensor_tensor_reduce(out=twice, in0=psum[:, GRAM, 0:DIM], in1=twice,
                                               scale=1.0 / INNER, scalar=key_lin[:, par_of(t):par_of(t) + 1],
                                               op0=ALU.mult, op1=ALU.add, accum_out=key_ms[:, t:t + 1])\
                    .then_inc(norm_summed, 1)

            def split_u(it, bl, s, half):
                dve.wait_ge(u_high_ready, 4 * it + 2 * s + half + 1)
                cols = slice(half * HALF, (half + 1) * HALF)
                sub(u_low[:, 2 * s:2 * s + 2, cols], rows_uo[:, ds(4 * bl + 2 * s, 2), cols],
                    u_high[:, 2 * s:2 * s + 2, cols].bitcast(F32)).then_inc(u_split, 1)

            def split_probs(it, u):
                half = u % 2
                dve.wait_ge(exp_done, UNITS * it + u + 1 + CREDIT["exp_done"])
                sub(p_low[:, half, :], probs[:, half, :], p_high[:, half, :].bitcast(F32)).then_inc(probs_split, 1)

            def split_sum(it, s, half):
                last = 2 * (IMG_TILES if s == 0 else TILES) - 2 + half
                n = 4 * it + 2 * s + half
                dve.wait_ge(sum_added, UNITS * it + last + 1 + CREDIT["sum_added"])
                dve.wait_ge(sum_wide, n + CREDIT["sum_wide"])
                nc.vector.tensor_copy(p_sum_high[:, :], p_sum[:, 2 * s + half, :]).then_inc(sum_high_ready, 1)
                dve.wait_ge(sum_high_ready, n + 1)
                sub(p_sum_low[:, :], p_sum[:, 2 * s + half, :], p_sum_high[:, :].bitcast(F32)).then_inc(sum_split, 1)

            def reciprocal(it, s, half, part):
                n = 4 * it + 2 * s + half
                cols = slice(part * (HALF // 2), (part + 1) * (HALF // 2))
                if part == 0:
                    dve.wait_ge(sum_wide, n + 1 + CREDIT["sum_wide"])
                    dve.wait_ge(o_scaled, n + CREDIT["o_scaled"])
                r = nc.vector.reciprocal(recip[:, cols], psum[:, SUM, cols])
                if part == 1:
                    r.then_inc(recip_ready, 1)

            def scale_o(it, bl, s, half):
                n = 4 * it + 2 * s + half
                dve.wait_ge(recip_ready, n + 1 + CREDIT["recip_ready"])
                dve.wait_ge(o_copied, n + 1 + CREDIT["o_copied"])
                cols = slice(half * HALF, (half + 1) * HALF)
                at = rows_uo[:, ds(4 * bl + 2 * s, 2), cols]
                nc.vector.tensor_tensor(at, at, recip[:, :].unsqueeze(1).to_broadcast([P, 2, HALF]), ALU.mult)\
                    .then_inc(o_scaled, 1)

            def set_end(it, bl, s, step):
                for half, at in ((0, 1), (1, 5)):
                    if step == at:
                        split_sum(it, s, half)
                    if step in (at + 2, at + 3):
                        reciprocal(it, s, half, step - at - 2)
                    if step == at + 4:
                        scale_o(it, bl, s, half)

            def body(it, bl, has_prev, has_next):
                if not has_prev:
                    for half in range(2):
                        split_u(it, bl, 0, half)
                for step in range(UNITS):
                    if has_prev and step == 0:
                        split_probs(it - 1, UNITS - 1)
                    if step >= 1:
                        split_probs(it, step - 1)
                    if step in (1, 2):
                        split_u(it, bl, 1, step - 1)
                    if step % 2 == 0:
                        norm(*ahead(it, step // 2 + 1))
                        prepare(*ahead(it, step // 2 + PREP))
                    else:
                        norm_terms(*ahead(it, step // 2 + PREP))
                    if has_prev:
                        set_end(it - 1, bl - 1, 1, step - 1)
                    set_end(it, bl, 0, step - 8)
                    if has_next and step in (16, 18):
                        split_u(it + 1, bl + 1, 0, (step - 16) // 2)

            def tail(it, bl):
                split_probs(it - 1, UNITS - 1)
                for step in range(10):
                    set_end(it - 1, bl - 1, 1, step)

            def outputs(g):
                def ready(h, i, nth, last):
                    dve.wait_ge(w_loaded[i], 16 * (3 * (H // WRING) * g + 2 * (H // WRING) + nth + 1))
                    dve.wait_ge(y_done, H * g + h - WRING + 1 + CREDIT["y_done"])
                    nc.vector.tensor_copy(ow_high[i], v_stage[:, i, WCOLS:VCOLS]).then_inc(ow_high_ready, 1)
                    dve.wait_ge(o_high_ready, H * g + h + 1)
                    uo = rows_uo[:, :, ds(h * S, S)].rearrange("p (b r) q -> p r b q", b=GB)
                    wide = lambda x: x.rearrange("p (r b q) -> p r b q", r=4, b=GB)
                    sub(wide(r_low[i]), uo, wide(r_high[i].bitcast(F32))).then_inc(o_split, 1)

                def take(h, i, nth, last):
                    k = H * g + h
                    dve.wait_ge(v_copied, k + 1 + CREDIT["v_copied"])
                    dve.wait_ge(y_done, k - 1 + CREDIT["y_done"])
                    nc.vector.tensor_copy(v_high[:, i % 2, :], v_out[:, i, :]).then_inc(v_high_ready, 1)
                    dve.wait_ge(v_high_ready, k + 1)
                    sub(v_low[:, i % 2, :], v_out[:, i, :], v_high[:, i % 2, :].bitcast(F32)).then_inc(v_split, 1)
                heads(dve, take, ready)
                dve.wait_ge(y_done, H * (g + 1) + CREDIT["y_done"])
                for c in range(NC):
                    ob = small[:, SMALL["ob"] + c:SMALL["ob"] + c + 1]
                    at = xT[:, c, ds(GN * g, GN)]
                    last = nc.vector.scalar_tensor_tensor(at, psum[:, 4 + c, 0:GN], ob, at, ALU.add, ALU.add)
                last.then_inc(y_added, 1)

            def maxima(it, bl):
                MAX_STEPS = 4
                dve.wait_ge(max_u_high, it + 1)
                sub(u_low[:, :, :], rows_uo[:, ds(4 * bl, 4), :], u_high[:, :, :].bitcast(F32)).then_inc(max_u_split, 1)
                nat = slice(DIM, 2 * DIM)
                for t in range(TILES):
                    T, s, n, one = TILES * it + t, int(t >= IMG_TILES), ROWS[t], slice(t, t + 1)
                    dve.wait_ge(max_high, T + 1)
                    sub(c_low[:, MAX_SLOT, :], stage[:, MAX_SLOT, :], c_high[:, MAX_SLOT, :].bitcast(F32))\
                        .then_inc(max_low, 1)
                    dve.wait_ge(max_low, T + 1)
                    nc.vector.tensor_tensor_reduce(out=junk[:, :], in0=stage[:, MAX_SLOT, nat],
                                                   in1=twice_wb[:, s, :], scale=1.0 / INNER, scalar=bb_eps[:, s:s + 1],
                                                   op0=ALU.mult, op1=ALU.add, accum_out=max_lin[:, one])\
                        .then_inc(max_terms, 1)
                    nc.vector.tensor_tensor(max_twice, stage[:, MAX_SLOT, nat], c_low[:, MAX_SLOT, nat].bitcast(F32),
                                            ALU.add).then_inc(max_terms, 1)
                    dve.wait_ge(max_terms, 2 * T + 2)
                    dve.wait_ge(max_scores, T + 1 + CREDIT["max_scores"])
                    nc.vector.tensor_tensor_reduce(out=max_twice, in0=psum[:, GRAM, 0:DIM], in1=max_twice,
                                                   scale=1.0 / INNER, scalar=max_lin[:, one], op0=ALU.mult,
                                                   op1=ALU.add, accum_out=max_ms[:, one]).then_inc(max_summed, 1)
                    dve.wait_ge(max_rooted, T + 1)
                    dve.wait_ge(max_tile_done, T + CREDIT["max_tile_done"])
                    for half in range(2):
                        run, src = max_run[0:n, 2 * s + half, :], psum[0:n, SC + half, 0:HALF]
                        if t in (0, IMG_TILES):
                            last = nc.vector.tensor_scalar(run, src, max_root[0:n, one], None, ALU.mult)
                        else:
                            last = nc.vector.scalar_tensor_tensor(run, src, max_root[0:n, one], run, ALU.mult, ALU.max)
                    last.then_inc(max_tile_done, 1)
                dve.wait_ge(max_summed, TILES * (it + 1))
                nc.vector.tensor_tensor(max_inverse, max_ms, max_root, ALU.mult).then_inc(max_steps, 1)
                dve.wait_ge(max_steps, MAX_STEPS * it + 1)
                nc.vector.tensor_copy(inverse[:, :, 0], max_inverse).then_inc(max_steps, 1)
                dve.wait_ge(max_steps, MAX_STEPS * it + 2)
                sub(inverse[:, :, 1], max_inverse, inverse[:, :, 0].bitcast(F32)).then_inc(max_steps, 1)
                dve.wait_ge(max_flipped, it + 1)
                nc.vector.tensor_reduce(max_cols, psum[:, 0:4, :].rearrange("p a n -> p (a n)")[:, 0:2 * HS]
                                        .rearrange("p (k n) -> p k n", n=P), mybir.AxisListType.X, ALU.max)\
                    .then_inc(max_steps, 1)
                dve.wait_ge(max_steps, MAX_STEPS * it + 4)
                nc.vector.tensor_scalar(negative, max_cols, -1.0, None, ALU.mult).then_inc(max_found, 1)
                dve.wait_ge(max_stored, 64 * (it + 1))

            def no_maxima():
                dve.sem_inc(max_u_split, GB)
                dve.sem_inc(max_low, GB * TILES)
                dve.sem_inc(max_terms, 2 * GB * TILES)
                dve.sem_inc(max_summed, GB * TILES)
                dve.sem_inc(max_tile_done, GB * TILES)
                dve.sem_inc(max_steps, 4 * GB)
                dve.sem_inc(max_found, GB)

            nc.vector.memset(zeros[:, :], 0.0).then_inc(start_ready, 1)
            dve.wait_ge(start_ready, 1)
            nc.vector.memset(p_sum[:, :, :], 0.0).then_inc(start_ready, 1)
            nc.vector.memset(key_ms[:, :], 0.0).then_inc(start_ready, 1)
            nc.vector.memset(key_lin[:, :], 0.0).then_inc(start_ready, 1)
            nc.vector.memset(square_w[:, :, :], 0.0).then_inc(start_ready, 1)
            dve.wait_ge(start_ready, 5)
            nc.vector.memset(square_w[:, :, 0], 1.0).then_inc(start_ready, 1)
            for h in range(H):
                for s in range(2):
                    last = nc.vector.tensor_tensor(square_w[:, h, 1 + 2 * h + s:2 + 2 * h + s], key_scale[:, s, h:h + 1],
                                                   key_scale[:, s, h:h + 1], ALU.mult)
            last.then_inc(start_ready, 1)
            dve.wait_ge(start_ready, START_STEPS)
            for t in range(PREP):
                prepare(0, t)
                norm_terms(0, t)
                if t == 0:
                    norm(0, 0)
            with dve.Fori(0, NG) as g:
                queries(g)
                absorb(g)
                judge(g)
                where_unsafe(dve, g, maxima, no_maxima)
                batches(dve, g, body, tail)
                outputs(g)

        @block.gpsimd
        def _(gp):
            gp.sem_inc(sum_added, CREDIT["sum_added"])
            gp.sem_inc(q_scaled, CREDIT["q_scaled"])
            gp.sem_inc(q_split, CREDIT["q_split"])

            def absorb(g):
                def scale(h, i, nth, last):
                    gp.wait_ge(q_wide_copied, g + 1)
                    gp.wait_ge(q_split, H * g + h - WRING + 1 + CREDIT["q_split"])
                    nc.gpsimd.tensor_tensor(q_hat[:, i, :], q_raw[:, ds(h, 1), :].rearrange("p a n -> p (a n)"),
                                            q_rms_wide[:, :], ALU.mult).then_inc(q_scaled, 1)

                def split(h, i, nth, last):
                    gp.wait_ge(q_high_ready, H * g + h + 1)
                    nc.gpsimd.tensor_tensor(r_low[i][:, 0:GN], q_hat[:, i, :], r_high[i][:, 0:GN].bitcast(F32),
                                            ALU.subtract).then_inc(q_split, 1)
                heads(gp, split, scale)

            def outputs(g):
                def split(h, i, nth, last):
                    gp.wait_ge(w_high_ready, 2 * H * g + H + h + 1)
                    nc.gpsimd.tensor_tensor(w_low[i], v_stage[:, i, 0:WCOLS], w_high[i].bitcast(F32), ALU.subtract)
                    gp.wait_ge(ow_high_ready, H * g + h + 1)
                    nc.gpsimd.tensor_tensor(ow_low[i], v_stage[:, i, WCOLS:VCOLS], ow_high[i].bitcast(F32),
                                            ALU.subtract).then_inc(w_low_ready, 1)
                heads(gp, split)

            def key_root(it, t):
                gp.wait_ge(norm_summed, TILES * it + t + 1 + CREDIT["norm_summed"])
                nc.gpsimd.tensor_tensor(key_rms[:, t:t + 1], key_ms[:, t:t + 1], minus_half[:, 0:1], ALU.pow)\
                    .then_inc(key_norm, 1)

            def add(it, u):
                t, half = divmod(u, 2)
                s, n = int(t >= IMG_TILES), ROWS[t]
                gp.wait_ge(exp_done, UNITS * it + u + 1 + CREDIT["exp_done"])
                if t in (0, IMG_TILES):
                    gp.wait_ge(sum_split, 4 * (it - 1) + 2 * s + half + 1 + CREDIT["sum_split"])
                    before_it = zeros[0:n, :].to_broadcast([n, HALF])
                else:
                    before_it = p_sum[0:n, 2 * s + half, :]
                gp.wait_ge(sum_added, UNITS * it + u - 1 + CREDIT["sum_added"])
                nc.gpsimd.tensor_tensor(p_sum[0:n, 2 * s + half, :], probs[0:n, half, :], before_it, ALU.add)\
                    .then_inc(sum_added, 1)

            def body(it, bl, has_prev, has_next):
                for step in range(UNITS):
                    if has_prev and step == 0:
                        add(it - 1, UNITS - 1)
                    if step >= 1:
                        add(it, step - 1)
                    if step % 2 == 0:
                        key_root(*ahead(it, step // 2 + 1))

            def tail(it, bl):
                add(it - 1, UNITS - 1)

            def maxima(it, bl):
                for t in range(TILES):
                    gp.wait_ge(max_summed, TILES * it + t + 1)
                    nc.gpsimd.tensor_tensor(max_root[:, t:t + 1], max_ms[:, t:t + 1], minus_half[:, 0:1], ALU.pow)\
                        .then_inc(max_rooted, 1)

            def no_maxima():
                gp.sem_inc(max_rooted, GB * TILES)

            gp.wait_ge(start_ready, START_STEPS)
            gp.wait_ge(zeros_stored, 16)
            key_root(0, 0)
            with gp.Fori(0, NG) as g:
                gp.wait_ge(q_ms_ready, g + 1)
                nc.gpsimd.tensor_tensor(q_rms[:, :], q_ms[:, :], minus_half[0:TOK, 0:2], ALU.pow)\
                    .then_inc(q_rms_ready, 1)
                absorb(g)
                where_unsafe(gp, g, maxima, no_maxima)
                batches(gp, g, body, tail)
                outputs(g)


def experts(nc, router_in, bias_in, ffn_in, out, probs_dram, psum, xT, ident, ones, minus_half):
    ctx = ExitStack()
    with ctx:
        sb = lambda n, s, dt=F32: ctx.enter_context(nc.sbuf_tensor(n, s, dt))
        sem = lambda n: ctx.enter_context(nc.semaphore(n))
        RT = N // P
        RING = 3
        WCOLS = 3 * DIM
        credit = {"w_split": RING, "scaled": 2 * RING, "down_done": 2 * RING, "h_split": 2, "clipped": 2}
        xn = sb("ffn_xn", [P, NC, N])
        x_high, x_low = sb("ffn_x_high", [P, NC, N], F32R), sb("ffn_x_low", [P, NC, N], F32R)
        router = sb("router", [P, NC, E])
        e_bias = sb("e_bias", [P, E])
        logit, absolute, u, w, lnw, big, small, mask, score = [
            sb(n, [P, RT, E]) for n in ("logit", "absolute", "exp_abs", "one_plus", "ln_one_plus", "log1p_big",
                                        "log1p_small", "mask", "score")]
        ranked, picked = sb("ranked", [P, RT, E + 4]), sb("picked", [P, RT, E + 4])
        top = sb("top", [P, RT, 8])
        p_sum, p_rec = sb("chosen_sum", [P, RT]), sb("chosen_rec", [P, RT])
        probs = sb("router_probs", [P, RT, E])
        probs_T = sb("probs_T", [E + 1, N])
        w_stage = sb("e_stage", [P, RING, WCOLS])
        w_high, w_low = sb("e_high", [P, RING, WCOLS], F32R), sb("e_low", [P, RING, WCOLS], F32R)
        p_wide = sb("p_wide", [P, RING, N])
        gate, gated, scaled_gate, up, h = [sb(n, [P, 2, N // 2]) for n in ("gate", "gated", "scaled_gate", "up", "h")]
        h_high, h_low = sb("h_high", [P, 2, N // 2], F32R), sb("h_low", [P, 2, N // 2], F32R)
        HN = N // 2
        DOWN, GATE_UP = 0, 4

        router_loaded, consts, x_high_ready, x_split = (
            sem("router_loaded"), sem("router_consts"), sem("ffn_x_high_ready"), sem("ffn_x_split"))
        logits_done, chain, act_chain = sem("logits_done"), sem("router_chain"), sem("router_act")
        flipped, probs_stored, out_stored = sem("flipped"), sem("probs_stored"), sem("out_stored")
        w_loaded = [sem(f"e_loaded{i}") for i in range(RING)]
        p_loaded = [sem(f"p_loaded{i}") for i in range(RING)]
        w_high_ready, w_split = sem("e_high_ready"), sem("e_split")
        gate_up_done, gate_clipped, up_clipped, silu_done, scaled, h_ready, h_high_ready, h_split, down_done = [
            sem(n) for n in ("gate_up_done", "gate_clipped", "up_clipped", "silu_done", "gate_scaled", "h_ready",
                             "h_high_ready", "h_split", "down_done")]
        out_ready = sem("out_ready")
        ln_pe, ln_dve, ln_pool, ln_done = layer_norm(
            nc, ctx, "ln2", xT, lambda c: xn[:, c, :].rearrange("p (h n) -> p h n", h=2), psum[:, 0:3, :])
        block = ctx.enter_context(nc.Block())

        def triples(eng, body):
            body(0, True)
            with eng.Fori(1, (E + 1) // RING) as k:
                body(k, False)

        @block.sync
        def _(sp):
            def load_weights(e, i):
                sp.wait_ge(w_split, e - RING + 1 + credit["w_split"])
                sp.dma_start(w_stage[:, i, :], ffn_in[ds(e, 1), :, :].rearrange("a p n -> p (a n)"))\
                    .then_inc(w_loaded[i], 16)

            def load_probs(e, i):
                sp.wait_ge(scaled, 2 * (e - RING + 1) + credit["scaled"])
                sp.dma_start(p_wide[:, i, :], probs_dram[ds(e, 1), :].partition_broadcast(P))\
                    .then_inc(p_loaded[i], 16)

            sp.dma_start(router[:, :, :], router_in).then_inc(router_loaded, 16)
            sp.dma_start(e_bias[:, :], bias_in.partition_broadcast(P)).then_inc(router_loaded, 16)
            load_weights(0, 0)
            sp.wait_ge(chain, ROUTER_STEPS)
            sp.dma_start(probs_dram, probs_T[:, :]).then_inc(probs_stored, 16)
            sp.wait_ge(probs_stored, 16)

            def body(k, first):
                for i in range(RING):
                    load_probs(RING * k + i, i)
                    load_weights(RING * k + i + 1, (i + 1) % RING)
            with sp.Fori(0, (E + 1) // RING) as k:
                body(k, False)
            sp.wait_ge(out_ready, NC)
            sp.dma_start(out, xT[:, :, :]).then_inc(out_stored, 16)
            sp.wait_ge(out_stored, 16)

        @block.gpsimd
        def _(gp):
            gp.sem_inc(scaled, credit["scaled"])
            ln_pool(gp, minus_half)

            def body(k, first):
                for j in range(2 * RING):
                    i, half, v = j // 2, j % 2, 2 * RING * k + j
                    gp.wait_ge(p_loaded[i], 16 * (k + 1))
                    gp.wait_ge(silu_done, v + 1)
                    nc.gpsimd.tensor_tensor(scaled_gate[:, half, :], gated[:, half, :],
                                            p_wide[:, i, half * HN:(half + 1) * HN], ALU.mult).then_inc(scaled, 1)
            triples(gp, body)

        @block.tensor
        def _(pe):
            pe.sem_inc(down_done, credit["down_done"])

            def three(out, high, low, rhigh, rlow, start, stop):
                nc.tensor.matmul(out, high, rhigh, start=start, stop=False)
                nc.tensor.matmul(out, high, rlow, start=False, stop=False)
                return nc.tensor.matmul(out, low, rhigh, start=False, stop=stop)

            ln_pe(pe, ones, ident)
            pe.wait_ge(router_loaded, 32)
            pe.wait_ge(ln_done, NC)
            for i in range(RT):
                for c in range(NC):
                    last = nc.tensor.matmul(psum[:, 3, i * E:(i + 1) * E], xn[:, c, i * P:(i + 1) * P],
                                            router[:, c, :], start=c == 0, stop=c == NC - 1)
            last.then_inc(logits_done, 1)
            pe.wait_ge(chain, ROUTER_STEPS - 2)
            for i in range(RT):
                last = nc.tensor.transpose(psum[0:E, 4 + i // 4, (i % 4) * P:(i % 4 + 1) * P], probs[:, i, :],
                                           ident[:, :])
            last.then_inc(flipped, 1)
            pe.wait_ge(chain, ROUTER_STEPS)
            pe.wait_ge(x_split, NC)

            def gate_up(k, j):
                i, half, v = j // 2, j % 2, 2 * RING * k + j
                if half == 0:
                    pe.wait_ge(w_split, RING * k + i + 1 + credit["w_split"])
                pe.wait_ge(up_clipped, v - 1 + credit["clipped"])
                for m in range(2):
                    for c in range(NC):
                        cols = slice(m * DIM + c * P, m * DIM + (c + 1) * P)
                        r = slice(half * HN, (half + 1) * HN)
                        last = three(psum[:, GATE_UP + 2 * half + m, 0:HN], w_high[:, i, cols], w_low[:, i, cols],
                                     x_high[:, c, r], x_low[:, c, r], c == 0, c == NC - 1)
                last.then_inc(gate_up_done, 1)

            def down(k, j, start, stop):
                i, half, v = j // 2, j % 2, 2 * RING * k + j
                pe.wait_ge(h_split, v + 1 + credit["h_split"])
                for c in range(NC):
                    cols = slice(2 * DIM + c * P, 2 * DIM + (c + 1) * P)
                    last = three(psum[:, DOWN + 2 * half + c, 0:HN], w_high[:, i, cols], w_low[:, i, cols],
                                 h_high[:, half, :], h_low[:, half, :], start, stop)
                last.then_inc(down_done, 1)

            def body(k, first):
                for j in range(2 * RING):
                    gate_up(k, j)
                    if j >= 2:
                        down(k, j - 2, first and j < 4, False)
                    elif not first:
                        down(k - 1, 2 * RING - 2 + j, False, False)
            triples(pe, body)
            for j in (4, 5):
                down((E + 1) // RING - 1, j, False, True)

        @block.scalar
        def _(act):
            copy = lambda out, in_: nc.scalar.activation(out, in_, ACT.Copy)
            for c in range(NC):
                act.wait_ge(ln_done, c + 1)
                copy(x_high[:, c, :], xn[:, c, :]).then_inc(x_high_ready, 1)
            act.wait_ge(chain, 2)
            nc.scalar.activation(u[:, :, :], absolute[:, :, :], ACT.Exp, scale=-1.0).then_inc(act_chain, 1)
            act.wait_ge(chain, 3)
            nc.scalar.activation(lnw[:, :, :], w[:, :, :], ACT.Ln).then_inc(act_chain, 1)
            act.wait_ge(chain, SOFTPLUS_STEPS)
            nc.scalar.activation(score[:, :, :], big[:, :, :], ACT.Sqrt).then_inc(act_chain, 1)

            def split(e, i, k_loads):
                act.wait_ge(w_loaded[i], 16 * k_loads)
                act.wait_ge(down_done, 2 * (e - RING + 1) + credit["down_done"])
                copy(w_high[:, i, :], w_stage[:, i, :]).then_inc(w_high_ready, 1)

            def silu(v, half):
                act.wait_ge(gate_clipped, v + 1)
                act.wait_ge(scaled, v - 1 + credit["scaled"])
                nc.scalar.activation(gated[:, half, :], gate[:, half, :], ACT.Silu).then_inc(silu_done, 1)

            def high(v, half):
                act.wait_ge(h_ready, v + 1)
                act.wait_ge(down_done, v - 1 + credit["down_done"])
                copy(h_high[:, half, :], h[:, half, :]).then_inc(h_high_ready, 1)

            def body(k, first):
                for j in range(2 * RING):
                    v = 2 * RING * k + j
                    silu(v, j % 2)
                    if not (first and j == 0):
                        high(v - 1, (j - 1) % 2)
                    if j % 2 == 0:
                        split(RING * k + j // 2 + 1, (j // 2 + 1) % RING, k + 1 + (j // 2 + 1) // RING)
            split(0, 0, 1)
            triples(act, body)
            high(2 * (E + 1) - 1, 1)

        @block.vector
        def _(dve):
            dve.sem_inc(w_split, credit["w_split"])
            dve.sem_inc(h_split, credit["h_split"])
            dve.sem_inc(up_clipped, credit["clipped"])
            V = nc.vector
            ln_dve(dve)
            for c in range(NC):
                dve.wait_ge(x_high_ready, c + 1)
                V.tensor_tensor(x_low[:, c, :], xn[:, c, :], x_high[:, c, :].bitcast(F32), ALU.subtract)\
                    .then_inc(x_split, 1)
            steps = [0]

            def link(ins):
                steps[0] += 1
                ins.then_inc(chain, 1)
                dve.wait_ge(chain, steps[0])

            dve.wait_ge(logits_done, 1)
            link(V.tensor_copy(logit[:, :, :], psum[:, 3, 0:RT * E].rearrange("p (t e) -> p t e", t=RT)))
            link(V.scalar_tensor_tensor(absolute[:, :, :], logit[:, :, :], -1.0, logit[:, :, :], ALU.mult, ALU.max))
            dve.wait_ge(act_chain, 1)
            link(V.tensor_scalar(w[:, :, :], u[:, :, :], 1.0, None, ALU.add))
            link(V.tensor_scalar(big[:, :, :], w[:, :, :], -1.0, 1e-30, ALU.add, ALU.max))
            link(V.reciprocal(mask[:, :, :], big[:, :, :]))
            link(V.tensor_tensor(big[:, :, :], mask[:, :, :], u[:, :, :], ALU.mult))
            dve.wait_ge(act_chain, 2)
            link(V.tensor_tensor(big[:, :, :], big[:, :, :], lnw[:, :, :], ALU.mult))
            link(V.tensor_scalar(small[:, :, :], u[:, :, :], 1 / 5, -1 / 4, ALU.mult, ALU.add))
            for term in (1 / 3, -1 / 2, 1.0):
                link(V.tensor_tensor(small[:, :, :], small[:, :, :], u[:, :, :], ALU.mult))
                link(V.tensor_scalar(small[:, :, :], small[:, :, :], term, None, ALU.add))
            link(V.tensor_tensor(small[:, :, :], small[:, :, :], u[:, :, :], ALU.mult))
            link(V.tensor_scalar(mask[:, :, :], u[:, :, :], 1 / 64, None, ALU.is_lt))
            link(V.tensor_tensor(small[:, :, :], small[:, :, :], big[:, :, :], ALU.subtract))
            link(V.tensor_tensor(small[:, :, :], small[:, :, :], mask[:, :, :], ALU.mult))
            link(V.tensor_tensor(small[:, :, :], small[:, :, :], big[:, :, :], ALU.add))
            link(V.scalar_tensor_tensor(big[:, :, :], logit[:, :, :], 0.0, small[:, :, :], ALU.max, ALU.add))
            assert steps[0] == SOFTPLUS_STEPS, steps
            link(V.memset(ranked[:, :, E:E + 4], -1e30))
            dve.wait_ge(router_loaded, 32)
            dve.wait_ge(act_chain, 3)
            link(V.tensor_tensor(ranked[:, :, 0:E], score[:, :, :], e_bias[:, :].unsqueeze(1).to_broadcast([P, RT, E]),
                                 ALU.add))
            for t in range(RT):
                V.max(top[:, t, :], ranked[:, t, 0:E])
            link(V.memset(small[:, :, :], 0.0))
            link(V.memset(top[:, :, K_TOP:8], -1e30))
            for t in range(RT):
                V.match_replace(picked[:, t, :], top[:, t, :], ranked[:, t, :], -3e38)
            link(V.memset(mask[:, :, :], 0.0))
            link(V.tensor_tensor(mask[:, :, :], picked[:, :, 0:E], ranked[:, :, 0:E], ALU.is_lt))
            link(V.tensor_tensor(score[:, :, :], score[:, :, :], mask[:, :, :], ALU.mult))
            link(V.tensor_reduce(p_sum[:, :], score[:, :, :], mybir.AxisListType.X, ALU.add))
            link(V.tensor_scalar(p_sum[:, :], p_sum[:, :], 1e-20, None, ALU.add))
            link(V.reciprocal(p_rec[:, :], p_sum[:, :]))
            link(V.tensor_tensor(probs[:, :, :], score[:, :, :], p_rec[:, :].unsqueeze(2).to_broadcast([P, RT, E]),
                                 ALU.mult))
            assert steps[0] == ROUTER_STEPS - 2, steps
            dve.wait_ge(flipped, 1)
            V.memset(probs_T[E:E + 1, :], 1.0)
            link(V.tensor_copy(probs_T[0:E, 0:4 * P], psum[0:E, 4, 0:4 * P]))
            link(V.tensor_copy(probs_T[0:E, 4 * P:N], psum[0:E, 5, 0:N - 4 * P]))

            def split(e, i):
                dve.wait_ge(w_high_ready, e + 1)
                V.tensor_tensor(w_low[:, i, :], w_stage[:, i, :], w_high[:, i, :].bitcast(F32), ALU.subtract)\
                    .then_inc(w_split, 1)

            def clip(v, half):
                dve.wait_ge(gate_up_done, v + 1)
                V.tensor_scalar(gate[:, half, :], psum[:, GATE_UP + 2 * half, 0:HN], ALPHA, -ALPHA, ALU.min, ALU.max)\
                    .then_inc(gate_clipped, 1)
                V.tensor_scalar(up[:, half, :], psum[:, GATE_UP + 2 * half + 1, 0:HN], ALPHA, -ALPHA, ALU.min,
                                ALU.max).then_inc(up_clipped, 1)

            def multiply(v, half):
                dve.wait_ge(scaled, v + 1 + credit["scaled"])
                dve.wait_ge(up_clipped, v + 1 + credit["clipped"])
                dve.wait_ge(h_split, v - 1 + credit["h_split"])
                V.tensor_tensor(h[:, half, :], up[:, half, :], scaled_gate[:, half, :], ALU.mult).then_inc(h_ready, 1)

            def low(v, half):
                dve.wait_ge(h_high_ready, v + 1)
                V.tensor_tensor(h_low[:, half, :], h[:, half, :], h_high[:, half, :].bitcast(F32), ALU.subtract)\
                    .then_inc(h_split, 1)

            def body(k, first):
                for j in range(2 * RING):
                    v = 2 * RING * k + j
                    if j % 2 == 1:
                        split(RING * k + j // 2 + 1, (j // 2 + 1) % RING)
                    clip(v, j % 2)
                    if not (first and j == 0):
                        multiply(v - 1, (j - 1) % 2)
                    if not (first and j == 0):
                        low(v - 1, (j - 1) % 2)
            split(0, 0)
            triples(dve, body)
            v = 2 * (E + 1) - 1
            multiply(v, 1)
            low(v, 1)
            dve.wait_ge(down_done, 2 * (E + 1) + credit["down_done"])
            for c in range(NC):
                at = xT[:, c, :].rearrange("p (h n) -> p h n", h=2)
                acc = psum[:, DOWN:DOWN + 4, 0:HN].rearrange("p (h c) n -> p h c n", h=2)[:, :, c, :]
                V.tensor_tensor(at, at, acc, ALU.add).then_inc(out_ready, 1)


SOFTPLUS_STEPS = 20
ROUTER_STEPS = 33


def _layouts(a):
    import numpy as np
    chunks = lambda w: w.reshape(NC, P, -1).transpose(1, 0, 2)
    x = np.asarray(a["x"]).reshape(N, DIM)
    context = np.asarray(a["ctx_2048"])
    tiles = np.zeros((B, TILES, P, DIM), np.float32)
    start = 0
    for t, n in enumerate(ROWS):
        tiles[:, t, :n] = context[:, start:start + n]
        start += n
    packed = np.zeros((B * TILES + PREP, P, 2 * DIM), np.float32)
    flat = tiles.reshape(B * TILES, P, DIM)
    packed[:B * TILES, :, 0:DIM] = flat.reshape(-1, P, NC, P).transpose(0, 3, 2, 1).reshape(-1, P, DIM)
    packed[:B * TILES, :, DIM:] = flat
    g = {k[len("L0_xattn_"):]: np.asarray(v) for k, v in a.items() if k.startswith("L0_xattn_")}
    f = {k[len("L0_ffn_"):]: np.asarray(v) for k, v in a.items() if k.startswith("L0_ffn_")}
    by_head = lambda w: w.reshape(NC, P, H, D).transpose(2, 1, 0, 3).reshape(H, P, DIM)
    flipped = lambda w: w.reshape(DIM, H, D).transpose(1, 2, 0)
    row = lambda v: v.reshape(H, D).T
    small = np.concatenate([row(g["q_b"]), row(g["nq_s"]), row(g["ki_b"]), row(g["k_b"]), row(g["nki_s"]),
                            row(g["nkt_s"]), row(g["vi_b"]), row(g["v_b"]), g["o_b"].reshape(NC, P).T], axis=1)
    up_T = lambda w: w.reshape(-1, I, NC, P).transpose(0, 3, 2, 1).reshape(-1, P, DIM)
    ffn = np.zeros((E + 2, P, 3 * DIM), np.float32)
    for at, gate, up, down in ((slice(0, E), f["gate_w"], f["up_w"], f["down_w"]),
                               (slice(E, E + 1), f["shared_gate_w"][None], f["shared_up_w"][None],
                                f["shared_down_w"][None])):
        ffn[at] = np.concatenate([up_T(gate), up_T(up), down.transpose(0, 2, 1)], axis=2)
    return {
        "xT": chunks(x.T), "ctx": packed, "qw": by_head(g["q_w"]),
        "kw": np.concatenate([flipped(g["ki_w"]), flipped(g["k_w"])], axis=2),
        "kwb": np.concatenate([x for w, b in (("ki_w", "ki_b"), ("k_w", "k_b"))
                               for x in (flipped(g[w]), g[b].reshape(H, D, 1), g[b].reshape(H, D, 1))], axis=2),
        "vw": np.concatenate([by_head(g["vi_w"]), by_head(g["v_w"]), g["o_w"].reshape(H, D, DIM)], axis=2),
        "small": small, "router": chunks(f["router_w"].T), "bias": f["expert_bias"][None], "ffn": ffn,
    }


def kernel(**inputs):
    import numpy as np
    from concourse import bacc
    from concourse.bass_utils import run_bass_kernel_spmd

    nc = bacc.Bacc("TRN2", target_bir_lowering=False, num_devices=1, dynamic_dma_scratch_size=1024)
    arrays = {f"in_{k}": np.ascontiguousarray(v) for k, v in _layouts(inputs).items()}
    args = [nc.dram_tensor(k, v.shape, mybir.dt.from_np(v.dtype), kind="ExternalInput").ap()
            for k, v in arrays.items()]
    out = nc.dram_tensor("outT", (P, NC, N), F32, kind="ExternalOutput").ap()
    build(nc, *args, out)
    got = run_bass_kernel_spmd(nc, [arrays], core_ids=[0]).results[0]["outT"]
    return got.transpose(1, 0, 2).reshape(DIM, N).T.reshape(B, S, DIM)
```

```python
import concourse.bass as bass
from concourse import mybir
from contextlib import ExitStack

F32 = mybir.dt.float32
F32R = mybir.dt.float32r
ACT = mybir.ActivationFunctionType
ALU = mybir.AluOpType
ds = bass.ds

P = 128
B, S, DIM = 16, 56, 256
NC = DIM // P
N = B * S
H, D = 16, 128
INNER = H * D
N_IMG, L = 257, 1500
GB = 4
NG = B // GB
GN = GB * S
HS = H * S
HALF = HS // 2
IMG_TILES = -(-N_IMG // P)
TXT_TILES = -(-(L - N_IMG) // P)
TILES = IMG_TILES + TXT_TILES
ROWS = [min(P, N_IMG - P * t) for t in range(IMG_TILES)] + \
       [min(P, L - N_IMG - P * t) for t in range(TXT_TILES)]
LONE = IMG_TILES - 1
assert ROWS[LONE] == 1
PREP = 2
UNITS = 2 * TILES
AVERAGES = UNITS - 2
TOK = 112
NTOK = N // TOK
EPS_RMS, EPS_LN = 1e-6, 1e-5
E, K_TOP, I = 32, 4, 128
ALPHA = 7.0
SMALL = {"qb": 0, "nq": 16, "kb": 32, "nk": 64, "vb": 96, "ob": 128, "end": 130}
STAGE_RING, CTX_RING, WRING = 3, 4, 4
RANK_RING = 4
SAFE_SCORE = 74.0
CREDIT = {"scores_done": UNITS, "av_done": AVERAGES, "exp_done": 2, "probs_split": 2, "sum_added": 2,
          "sum_split": 4, "stage_used": TILES, "u_text_copied": 2, "o_copied": 2, "w_low": WRING,
          "w_used": WRING, "y_done": WRING, "v_done": WRING, "q_copied": 2, "squares_summed": WRING,
          "q_scaled": 2, "u_copied": 2, "v_copied": WRING, "v_split": WRING, "q_split": WRING, "y_added": 1,
          "recip_ready": 1, "o_scaled": 1, "norm_summed": 1, "max_tile_done": 1, "judgement_read": 1,
          "sum_wide": 1, "max_scores": 1}


def slot(t, ring):
    return t % ring if t < TILES - 1 else ring


def rank_slot(t):
    s = int(t >= IMG_TILES)
    start, end = (0, IMG_TILES) if s == 0 else (IMG_TILES, TILES)
    mine = lambda k: 2 * s + (k - start) % 2
    return mine(t), (0, t - 2) if t - 2 >= start else (1, max(k for k in range(start, end) if mine(k) == mine(t)))


def averaged(u):
    return u + 1 - min(max(u + 1 - 2 * LONE, 0), 2)


def before(t, ring):
    if t == TILES - 1:
        return 1, t
    if t >= ring:
        return 0, t - ring
    return 1, max(k for k in range(TILES - 1) if k % ring == t)




def layer_norm(nc, ctx, tag, xT, keep, banks):
    sem = lambda n: ctx.enter_context(nc.semaphore(f"{tag}_{n}"))
    sums, centred, squared, var, var_eps, rstd, rstd_wide, done = [
        sem(n) for n in ("sums", "centred", "squared", "var", "var_eps", "rstd", "rstd_wide", "done")]
    var_sb = ctx.enter_context(nc.sbuf_tensor(f"{tag}_var_sb", [TOK, NTOK], F32))
    rstd_sb = ctx.enter_context(nc.sbuf_tensor(f"{tag}_rstd_sb", [TOK, NTOK], F32))
    square = ctx.enter_context(nc.sbuf_tensor(f"{tag}_square", [P, NC, N], F32))
    compact, wide = banks[:, 0, 0:NTOK], banks[:, 1:3, 0:N // 2]

    def tensor(pe, ones, ident, meanwhile=(lambda: None, lambda: None)):
        for half in range(2):
            for c in range(NC):
                last = nc.tensor.matmul(wide[:, half, :], ones[:, :], xT[:, c, half * (N // 2):(half + 1) * (N // 2)],
                                        start=c == 0, stop=c == NC - 1)
        last.then_inc(sums, 1)
        meanwhile[0]()
        for i in range(NTOK):
            for c in range(NC):
                if i == 0:
                    pe.wait_ge(squared, c + 1)
                last = nc.tensor.matmul(compact[0:TOK, i:i + 1], square[:, c, TOK * i:TOK * i + TOK], ones[:, 0:1],
                                        start=c == 0, stop=c == NC - 1)
        last.then_inc(var, 1)
        meanwhile[1]()
        pe.wait_ge(rstd, 1)
        pe.wait_ge(centred, NC)
        for i in range(NTOK):
            half, at = divmod(TOK * i, N // 2)
            last = nc.tensor.matmul(wide[:, half, at:at + TOK], rstd_sb[:, i:i + 1].to_broadcast([TOK, P]),
                                    ident[0:TOK, 0:TOK], start=True, stop=True)
        last.then_inc(rstd_wide, 1)

    def vector(dve, meanwhile=(lambda: None, lambda: None)):
        dve.wait_ge(sums, 1)
        for c in range(NC):
            nc.vector.scalar_tensor_tensor(keep(c), wide, -1.0 / DIM, xT[:, c, :].rearrange("p (h n) -> p h n", h=2),
                                           ALU.mult, ALU.add).then_inc(centred, 1)
        meanwhile[0]()
        dve.wait_ge(var, 1)
        nc.vector.tensor_scalar(var_sb[:, :], compact[0:TOK, :], 1.0 / DIM, EPS_LN, ALU.mult, ALU.add)\
            .then_inc(var_eps, 1)
        meanwhile[1]()
        dve.wait_ge(rstd_wide, 1)
        for c in range(NC):
            nc.vector.tensor_tensor(keep(c), keep(c), wide, ALU.mult).then_inc(done, 1)

    def scalar(act):
        for c in range(NC):
            act.wait_ge(centred, c + 1)
            nc.scalar.activation(square[:, c, :].rearrange("p (h n) -> p h n", h=2), keep(c), ACT.Square)\
                .then_inc(squared, 1)

    def pool(gp, minus_half):
        gp.wait_ge(var_eps, 1)
        nc.gpsimd.tensor_tensor(rstd_sb[:, :], var_sb[:, :], minus_half[0:TOK, 0:NTOK], ALU.pow).then_inc(rstd, 1)

    return tensor, scalar, vector, pool, done


def build(nc, xT_in, ctx_in, qw_in, kw_in, kwb_in, vw_in, small_in, router_in, bias_in, ffn_in, out):
    ctx = ExitStack()
    with ctx:
        def sb(name, shape, dt=F32, stack=ctx):
            return stack.enter_context(nc.sbuf_tensor(name, shape, dt))

        def sem(name, stack=ctx):
            return stack.enter_context(nc.semaphore(name))

        probs_dram = nc.dram_tensor("probs_by_expert", [E + 1, N], F32, kind="Internal").ap()
        psum = ctx.enter_context(nc.psum_tensor("psum", [P, 8, 512], F32))
        xT = sb("xT", [P, NC, N])
        ident = sb("ident", [P, P])
        ones = sb("ones", [P, P])
        minus_half = sb("minus_half", [P, 16])

        attn = ExitStack()
        with attn:
            small = sb("small", [P, SMALL["end"]], stack=attn)
            key_scale = sb("key_scale", [P, 2, H], stack=attn)
            bias_cols = sb("bias_cols", [P, H, 4], stack=attn)
            bias_high = sb("bias_high", [P, H, 4], F32R, attn)
            bias_low = sb("bias_low", [P, H, 4], F32R, attn)
            v_bias = sb("v_bias", [P, H], stack=attn)
            x_high = sb("x_high", [P, NC, N], F32R, attn)
            x_low = sb("x_low", [P, NC, N], F32R, attn)
            gram_high = sb("gram_high", [P, 2, NC, DIM], F32R, attn)
            gram_low = sb("gram_low", [P, 2, NC, DIM], F32R, attn)
            twice_wb = sb("twice_wb", [P, 2, DIM], stack=attn)
            bb_eps = sb("bb_eps", [P, 2], stack=attn)
            ones_r = sb("ones_r", [P, P], F32R, attn)
            rank_w = sb("rank_w", [P, RANK_RING, P], F32R, attn)
            square_w = sb("square_w", [P, H, 1 + 2 * H], stack=attn)
            prologue(nc, xT_in, kwb_in, small_in, psum, xT, ident, ones, minus_half, small, key_scale, bias_cols,
                     bias_high, bias_low, v_bias, x_high, x_low, gram_high, gram_low, twice_wb, bb_eps, ones_r,
                     rank_w, square_w)
            attention(nc, ctx_in, qw_in, kw_in, vw_in, psum, xT, ident, ones, minus_half, small, key_scale,
                      bias_high, bias_low, v_bias, x_high, x_low, gram_high, gram_low, twice_wb, bb_eps, ones_r,
                      rank_w, square_w)
        experts(nc, router_in, bias_in, ffn_in, out, probs_dram, psum, xT, ident, ones, minus_half)


def prologue(nc, xT_in, kwb_in, small_in, psum, xT, ident, ones, minus_half, small, key_scale, bias_cols, bias_high,
             bias_low, v_bias, x_high, x_low, gram_high, gram_low, twice_wb, bb_eps, ones_r, rank_w, square_w):
    ctx = ExitStack()
    with ctx:
        sb = lambda n, s, dt=F32: ctx.enter_context(nc.sbuf_tensor(n, s, dt))
        sem = lambda n: ctx.enter_context(nc.semaphore(n))
        KW = 4
        WB = DIM + 2
        kw = sb("kw", [P, KW, 2 * WB])
        kw_high, kw_low = sb("kw_high", [P, 2, 2 * WB], F32R), sb("kw_low", [P, 2, 2 * WB], F32R)
        wb_cols, bb_cols = sb("wb_cols", [P, 2 * NC]), sb("bb_cols", [P, 2])
        bb_products = sb("bb_products", [P, 2, H])
        kw_high_ready, kw_split = sem("kw_high_ready"), sem("kw_split")
        bb_ready, cols_ready, cols_wide = sem("bb_ready"), sem("cols_ready"), sem("cols_wide")
        GRAM = 3
        xn = sb("xn", [P, NC, N])
        x_loaded, small_loaded = sem("x_loaded"), sem("small_loaded")
        kw_loaded = [sem(f"kw_loaded{i}") for i in range(KW)]
        square_w_zero, square_w_ready = sem("square_w_zero"), sem("square_w_ready")
        kw_used, const_ready, ident_ready = sem("kw_used"), sem("const_ready"), sem("ident_ready")
        scale_ready, bias_ready, bias_high_ready, bias_split = (
            sem("scale_ready"), sem("bias_ready"), sem("bias_high_ready"), sem("bias_split"))
        gram_high_ready, gram_split = sem("gram_high_ready"), sem("gram_split")
        x_high_ready, x_split = sem("x_high_ready"), sem("x_split")
        ln_pe, ln_act, ln_dve, ln_pool, ln_done = layer_norm(
            nc, ctx, "ln1", xT, lambda c: xn[:, c, :].rearrange("p (h n) -> p h n", h=2), psum[:, 0:3, :])
        kb = small[:, SMALL["kb"]:SMALL["kb"] + 2 * H].rearrange("p (s h) -> p s h", s=2)
        nk = small[:, SMALL["nk"]:SMALL["nk"] + 2 * H].rearrange("p (s h) -> p s h", s=2)
        nq = small[:, SMALL["nq"]:SMALL["nq"] + H]
        vb = small[:, SMALL["vb"]:SMALL["vb"] + 2 * H].rearrange("p (s h) -> p s h", s=2)
        block = ctx.enter_context(nc.Block())

        @block.sync
        def _(sp):
            sp.dma_start(xT[:, :, :], xT_in).then_inc(x_loaded, 16)
            sp.dma_start(small[:, :], small_in).then_inc(small_loaded, 16)
            for h in range(H):
                if h >= KW:
                    sp.wait_ge(kw_split, h - KW + 1)
                sp.dma_start(kw[:, h % KW, :], kwb_in[h, :, :]).then_inc(kw_loaded[h % KW], 16)

        @block.gpsimd
        def _(gp):
            nc.gpsimd.memset(ident[:, :], 0.0).then_inc(ident_ready, 1)
            nc.gpsimd.memset(ones[:, :], 1.0).then_inc(const_ready, 1)
            nc.gpsimd.memset(minus_half[:, :], -0.5).then_inc(const_ready, 1)
            nc.gpsimd.memset(square_w[:, :, :], 0.0).then_inc(square_w_zero, 1)
            gp.wait_ge(ident_ready, 1)
            nc.gpsimd.affine_select(out=ident[:, :], in_=ident[:, :], compare_op=ALU.not_equal, fill=1.0, base=0,
                                    pattern=[[-1, P]], channel_multiplier=1).then_inc(const_ready, 1)
            ln_pool(gp, minus_half)

        @block.tensor
        def _(pe):
            def gram(heads):
                for h in heads:
                    pe.wait_ge(kw_split, h + 1)
                    for s in range(2):
                        high, low = [x[:, h % 2, s * WB:(s + 1) * WB] for x in (kw_high, kw_low)]
                        for c in range(NC):
                            out, cols = psum[:, GRAM + s * NC + c, 0:WB], slice(c * P, (c + 1) * P)
                            nc.tensor.matmul(out, high[:, cols], high, start=h == 0, stop=False)
                            nc.tensor.matmul(out, high[:, cols], low, start=False, stop=False)
                            last = nc.tensor.matmul(out, low[:, cols], high, start=False, stop=h == H - 1)
                    last.then_inc(kw_used, 1)

            pe.wait_ge(const_ready, 3)
            pe.wait_ge(x_loaded, 16)
            ln_pe(pe, ones, ident, (lambda: gram(range(0, 4)), lambda: gram(range(4, 7))))
            gram(range(7, H))
            pe.wait_ge(cols_ready, 1)
            pe.wait_ge(ln_done, NC)
            for k in range(2 * NC):
                nc.tensor.matmul(psum[:, 1 + k // 2, (k % 2) * P:(k % 2 + 1) * P],
                                 wb_cols[:, k:k + 1].to_broadcast([P, P]), ident[:, :], start=True, stop=True)
            pe.wait_ge(bb_ready, 2)
            nc.tensor.matmul(psum[:, 0, 0:2], ones[:, :], bb_cols[:, :], start=True, stop=True).then_inc(cols_wide, 1)

        @block.scalar
        def _(act):
            def split(heads):
                for h in heads:
                    act.wait_ge(kw_loaded[h % KW], 16 * (h // KW + 1))
                    if h >= 2:
                        act.wait_ge(kw_used, h - 1)
                    nc.scalar.activation(kw_high[:, h % 2, :], kw[:, h % KW, :], ACT.Copy).then_inc(kw_high_ready, 1)

            split(range(0, 2))
            act.wait_ge(bias_ready, 4)
            nc.scalar.activation(bias_high[:, :, :], bias_cols[:, :, :], ACT.Copy).then_inc(bias_high_ready, 1)
            ln_act(act)
            split(range(2, 9))
            for c in range(NC):
                act.wait_ge(ln_done, c + 1)
                nc.scalar.activation(x_high[:, c, :], xn[:, c, :], ACT.Copy).then_inc(x_high_ready, 1)
            split(range(9, H))
            act.wait_ge(kw_used, H)
            nc.scalar.activation(gram_high[:, :, :, :], psum[:, GRAM:GRAM + 4, 0:DIM]
                                 .rearrange("p (s c) n -> p s c n", s=2), ACT.Copy).then_inc(gram_high_ready, 1)

        @block.vector
        def _(dve):
            dve.wait_ge(const_ready, 1)
            nc.vector.tensor_copy(ones_r[:, :], ones[:, :])
            nc.vector.tensor_scalar(rank_w[:, :, :], ones[:, 0:1].to_broadcast([P, RANK_RING, P]), 0.0, None,
                                    ALU.mult).then_inc(scale_ready, 1)
            dve.wait_ge(scale_ready, 1)
            for s in range(2):
                for row in (32 * s, 64 + 32 * s):
                    nc.vector.tensor_copy(rank_w[row:row + 1, 2 * s:2 * s + 2, :],
                                          ones[row:row + 1, :].unsqueeze(1).to_broadcast([1, 2, P]))\
                        .then_inc(scale_ready, 1)
            dve.wait_ge(small_loaded, 16)
            for s in range(2):
                nc.vector.scalar_tensor_tensor(key_scale[:, s, :], nk[:, s, :], float(D) ** -0.5, nq, ALU.mult,
                                               ALU.mult).then_inc(scale_ready, 1)
            dve.wait_ge(scale_ready, 7)
            for s in range(2):
                for i in range(2):
                    nc.vector.tensor_tensor(bias_cols[:, :, s + 2 * i], kb[:, s, :], key_scale[:, s, :], ALU.mult)\
                        .then_inc(bias_ready, 1)
            nc.vector.tensor_tensor(v_bias[:, :], vb[:, 0, :], vb[:, 1, :], ALU.add).then_inc(scale_ready, 1)
            dve.wait_ge(bias_high_ready, 1)
            dve.wait_ge(bias_ready, 4)
            nc.vector.tensor_tensor(bias_low[:, :, :], bias_cols[:, :, :], bias_high[:, :, :].bitcast(F32),
                                    ALU.subtract).then_inc(bias_split, 1)
            for s in range(2):
                nc.vector.tensor_tensor_reduce(out=bb_products[:, s, :], in0=kb[:, s, :], in1=kb[:, s, :], scale=1.0,
                                               scalar=0.0, op0=ALU.mult, op1=ALU.add, accum_out=bb_cols[:, s:s + 1])\
                    .then_inc(bb_ready, 1)

            def square_weights():
                dve.wait_ge(square_w_zero, 1)
                dve.wait_ge(scale_ready, 7)
                nc.vector.tensor_copy(square_w[:, :, 0], ones[:, 0:H]).then_inc(square_w_ready, 1)
                for h in range(H):
                    nc.vector.tensor_tensor(square_w[:, h, 1 + 2 * h:3 + 2 * h], key_scale[:, :, h], key_scale[:, :, h],
                                            ALU.mult).then_inc(square_w_ready, 1)

            def split(heads):
                for h in heads:
                    dve.wait_ge(kw_high_ready, h + 1)
                    nc.vector.tensor_tensor(kw_low[:, h % 2, :], kw[:, h % KW, :], kw_high[:, h % 2, :].bitcast(F32),
                                            ALU.subtract).then_inc(kw_split, 1)
            split(range(0, 2))
            ln_dve(dve, (lambda: split(range(2, 4)), lambda: (split(range(4, 7)), square_weights())))
            split(range(7, 9))
            for c in range(NC):
                dve.wait_ge(x_high_ready, c + 1)
                nc.vector.tensor_tensor(x_low[:, c, :], xn[:, c, :], x_high[:, c, :].bitcast(F32), ALU.subtract)\
                    .then_inc(x_split, 1)
            split(range(9, H))
            dve.wait_ge(gram_high_ready, 1)
            nc.vector.tensor_copy(wb_cols[:, :], psum[:, GRAM:GRAM + 4, DIM]).then_inc(cols_ready, 1)
            nc.vector.tensor_tensor(gram_low[:, :, :, :].rearrange("p s c n -> p (s c) n"),
                                    psum[:, GRAM:GRAM + 4, 0:DIM],
                                    gram_high[:, :, :, :].bitcast(F32).rearrange("p s c n -> p (s c) n"),
                                    ALU.subtract).then_inc(gram_split, 1)
            dve.wait_ge(cols_wide, 1)
            nc.vector.tensor_scalar(twice_wb[:, :, :], psum[:, 1:3, 0:DIM], 2.0, None, ALU.mult).then_inc(gram_split, 1)
            nc.vector.tensor_scalar(bb_eps[:, :], psum[:, 0, 0:2], 1.0 / INNER, EPS_RMS, ALU.mult, ALU.add)\
                .then_inc(gram_split, 1)


def attention(nc, ctx_in, qw_in, kw_in, vw_in, psum, xT, ident, ones, minus_half, small, key_scale, bias_high,
              bias_low, v_bias, x_high, x_low, gram_high, gram_low, twice_wb, bb_eps, ones_r, rank_w, square_w):
    ctx = ExitStack()
    with ctx:
        sb = lambda n, s, dt=F32: ctx.enter_context(nc.sbuf_tensor(n, s, dt))
        names = {}

        def sem(n):
            names[n] = ctx.enter_context(nc.semaphore(n))
            return names[n]

        rows_uo = sb("rows_uo", [P, GB * 4, HS])
        rank_rows = sb("rank_rows", [P, GB, HS], F32R)
        q_raw = sb("q_raw", [P, H, GN])
        bound_sq = sb("bound_sq", [TOK, 2])
        bound_max = sb("bound_max", [TOK, 1])
        bound_row = sb("bound_row", [1, 1])
        is_safe = sb("is_safe", [1, 1], mybir.dt.int32)
        q_ms = sb("q_ms", [TOK, 2])
        q_rms = sb("q_rms", [TOK, 2])
        q_rms_wide = sb("q_rms_wide", [P, GN])
        square_sums = q_rms_wide[0:1 + 2 * H, :]
        q_hat = sb("q_hat", [P, WRING, GN])
        v_out = q_hat
        v_high = sb("v_high", [P, 2, GN], F32R)
        v_low = sb("v_low", [P, 2, GN], F32R)
        VCOLS = 3 * DIM
        w_stage = sb("w_stage", [P, WRING, 2 * DIM])
        v_stage = q_raw[:, :, :].rearrange("p h n -> p (h n)")[:, 0:WRING * VCOLS]\
            .rearrange("p (r n) -> p r n", r=WRING)
        UCOLS, WCOLS, RCOLS = 2 * NC * HS, 2 * DIM, 4 * GN
        shared = sb("shared", [P, 2, max(UCOLS, 2 * WCOLS + 3 * RCOLS + DIM)], F32R)
        u_high, u_low = [shared[:, i, 0:UCOLS].rearrange("p (r n) -> p r n", r=4) for i in range(2)]
        stage = sb("stage", [P, STAGE_RING + 1, 2 * DIM])
        q_square = stage[:, 2, 0:2 * GN].rearrange("p (a n) -> p a n", a=2)
        square_w_ring = stage[:, 3, 0:WRING * (1 + 2 * H)].rearrange("p (a n) -> p a n", a=WRING)
        c_high = sb("c_high", [P, CTX_RING + 1, 2 * DIM], F32R)
        c_low = sb("c_low", [P, CTX_RING + 1, 2 * DIM], F32R)
        c_twice = sb("c_twice", [P, 2, DIM])
        junk = sb("junk", [P, DIM], mybir.dt.bfloat16)
        key_lin = sb("key_lin", [P, 2])
        lone_row = sb("lone_row", [P, NC])
        key_ms = sb("key_ms", [P, TILES])
        key_rms = sb("key_rms", [P, TILES])
        probs = sb("probs", [P, 2, HALF])
        p_high = sb("p_high", [P, 2, HALF], F32R)
        p_low = sb("p_low", [P, 2, HALF], F32R)
        zeros = sb("zeros", [P, 1])
        p_sum = sb("p_sum", [P, 4, HALF])
        p_sum_high = sb("p_sum_high", [P, HALF], F32R)
        p_sum_low = sb("p_sum_low", [P, HALF], F32R)
        taken = lambda i, col, cols: shared[:, i, col:col + cols]
        flat2 = lambda x: x.rearrange("p a n -> p (a n)")
        w_high, w_low = [[taken(i, 0, WCOLS), taken(i, WCOLS, WCOLS), c[:, 2, :], c[:, 3, :]]
                         for i, c in enumerate((c_high, c_low))]
        r_high, r_low = [[taken(i, 2 * WCOLS, RCOLS), taken(i, 2 * WCOLS + RCOLS, RCOLS), flat2(parts[:, :, :]),
                          taken(i, 2 * WCOLS + 2 * RCOLS, RCOLS)] for i, parts in enumerate((p_high, p_low))]
        ow_high, ow_low = [[taken(i, 2 * WCOLS + 3 * RCOLS, DIM), c[:, CTX_RING, 0:DIM], c[:, CTX_RING, DIM:2 * DIM],
                            sums[:, 0:DIM]] for i, (c, sums) in enumerate(((c_high, p_sum_high), (c_low, p_sum_low)))]
        bias_wide_high, bias_wide_low = [c[:, CTX_RING, :].rearrange("p (r a b) -> p r a b", r=WRING, a=4)
                                         for c in (c_high, c_low)]
        recip = sb("recip", [P, HALF])

        inverted = lambda half, *parts: tuple(("invert", half, part) for part in parts)
        TEXT_END = {1: (("split", 0),), 3: (("split", 1),), 7: inverted(0, 0, 1), 8: inverted(0, 2),
                    9: inverted(0, 3) + (("scale", 0),), 11: inverted(1, 0, 1), 12: inverted(1, 2),
                    13: inverted(1, 3) + (("scale", 1),)}
        IMAGE_END = {14: (("split", 0),), 16: (("split", 1),), 17: inverted(0, 0), 19: inverted(0, 1, 2),
                     20: inverted(0, 3), 21: (("scale", 0),), 23: inverted(1, 0, 1), 24: inverted(1, 2),
                     25: inverted(1, 3) + (("scale", 1),)}
        TEXT_SUMS, IMAGE_SUMS = (2, 10), (15, 22)
        LAST_END = [(("split", 0),) + inverted(0, *range(4)) + (("scale", 0), ("split", 1)),
                    inverted(1, *range(4)) + (("scale", 1),)]
        BOUND_STEPS, START_STEPS = 5, 4
        O, SC, GRAM, SUM = 0, 4, 6, 7

        inverse_dram = nc.dram_tensor("inverse_rms", [B * TILES, 2, P], F32, kind="Internal").ap()
        negative_dram = nc.dram_tensor("negative_maxima", [B, 2 * HS // P, P], F32, kind="Internal").ap()
        flat = q_raw[:, :, :].rearrange("p h n -> p (h n)")
        max_run = flat[:, 0:2 * HS].rearrange("p (s n) -> p s n", s=4)
        max_twice = flat[:, 2 * HS:2 * HS + DIM]
        at = 2 * HS + DIM
        max_lin, max_ms, max_root, max_inverse = [flat[:, at + TILES * i:at + TILES * (i + 1)] for i in range(4)]
        max_cols = flat[:, at + 4 * TILES:at + 4 * TILES + 2 * HS // P]
        inverse = p_low[:, 0, 0:2 * TILES].rearrange("p (t r) -> p t r", r=2)
        negative = p_low[:, 1, 0:2 * HS // P]
        MAX_SLOT = 2
        (max_loaded, max_high, max_low, max_terms, max_scores, max_summed, max_rooted, max_tile_done, max_u_high,
         max_u_split, max_flipped, max_steps, max_found, max_listed, max_stored) = [sem(f"max_{n}") for n in (
             "loaded", "high", "low", "terms", "scores", "summed", "rooted", "tile_done", "u_high", "u_split",
             "flipped", "steps", "found", "listed", "stored")]
        start_ready = sem("start_ready")
        ctx_loaded = [sem(f"ctx_loaded{i}") for i in range(STAGE_RING + 1)]
        w_loaded = [sem(f"w_loaded{i}") for i in range(WRING)]
        rank_loaded = [sem(f"rank_loaded{i}") for i in range(RANK_RING)]
        zeros_stored = sem("zeros_stored")
        ctx_high, ctx_low, stage_used = sem("ctx_high"), sem("ctx_low"), sem("stage_used")
        gram_done, norm_summed, key_norm = sem("gram_done"), sem("norm_summed"), sem("key_norm")
        u_high_ready, u_split = sem("u_high_ready"), sem("u_split")
        scores_done, exp_done, probs_split, av_done = (
            sem("scores_done"), sem("exp_done"), sem("probs_split"), sem("av_done"))
        sum_added, sum_high_ready, sum_split = sem("sum_added"), sem("sum_high_ready"), sem("sum_split")
        sum_wide, recip_ready, o_copied, o_scaled = (
            sem("sum_wide"), sem("recip_ready"), sem("o_copied"), sem("o_scaled"))
        ow_high_ready, bias_zeroed, square_w_placed = sem("ow_high_ready"), sem("bias_zeroed"), sem("square_w_placed")
        q_w_high_ready, w_high_ready, w_low_ready, w_used = (
            sem("q_w_high_ready"), sem("w_high_ready"), sem("w_low"), sem("w_used"))
        q_copied, squares_summed, sums_copied, sums_flipped = (
            sem("q_copied"), sem("squares_summed"), sem("sums_copied"), sem("sums_flipped"))
        bound_step, bound_flat, safe_known, judgement_read = (
            sem("bound_step"), sem("bound_flat"), sem("safe_known"), sem("judgement_read"))
        q_ms_ready, q_rms_ready, q_wide, q_wide_copied = (
            sem("q_ms_ready"), sem("q_rms_ready"), sem("q_wide"), sem("q_wide_copied"))
        q_scaled, q_high_ready, q_split = (
            sem("q_scaled"), sem("q_high_ready"), sem("q_split"))
        bias_ready, u_copied, rank_copied, u_text_copied = (
            sem("bias_ready"), sem("u_copied"), sem("rank_copied"), sem("u_text_copied"))
        o_high_ready, o_split, v_done, v_copied, v_high_ready, v_split = (
            sem("o_high_ready"), sem("o_split"), sem("v_done"), sem("v_copied"), sem("v_high_ready"), sem("v_split"))
        y_done, y_added = sem("y_done"), sem("y_added")
        block = ctx.enter_context(nc.Block())

        def last_unit_of_buffer(it, t):
            back, k = before(t, CTX_RING)
            return AVERAGES * (it - back) + averaged(2 * k + 1) + CREDIT["av_done"]

        def w_index(g, phase, h):
            return 3 * H * g + H * phase + h

        def batches(eng, g, body, tail):
            body(GB * g, 0, False, True)
            with eng.Fori(1, GB - 1) as j:
                body(GB * g + j, j, True, True)
            body(GB * g + GB - 1, GB - 1, True, False)
            tail(GB * g + GB, GB)

        def heads(eng, main, prepare=None, lead=2, lead_in=None):
            def step(quad, i, last):
                n = i + lead
                if prepare is not None and not (last and n >= WRING):
                    prepare(WRING * quad + n, n % WRING, quad + n // WRING, False)
                main(WRING * quad + i, i, quad, last and i == WRING - 1)
            if lead_in is not None:
                lead_in()
            elif prepare is not None:
                for n in range(lead):
                    prepare(n, n, 0, False)
            with eng.Fori(0, H // WRING - 1) as quad:
                for i in range(WRING):
                    step(quad, i, False)
            for i in range(WRING):
                step(H // WRING - 1, i, True)

        def where_unsafe(eng, g, maxima, no_maxima, before=lambda: None):
            eng.wait_ge(safe_known, g + 1)
            eng.sem_inc(judgement_read, 1)
            safe = eng.value_load(is_safe[0:1, 0:1], min_val=0, max_val=1)
            eng.sem_inc(judgement_read, 1)
            with eng.If(safe == 0):
                before()
                with eng.Fori(0, GB) as j:
                    maxima(GB * g + j, j)
            with eng.Else():
                no_maxima()

        def ahead(it, t):
            return (it, t) if t < TILES else (it + 1, t - TILES)

        @block.sync
        def _(sp):
            def load_tile(it, t):
                back, k = before(t, STAGE_RING)
                sp.wait_ge(stage_used, TILES * (it - back) + k + 1 + CREDIT["stage_used"])
                sp.dma_start(stage[:, slot(t, STAGE_RING), :], ctx_in[ds(TILES * it + t, 1), :, :]
                             .rearrange("a p n -> p (a n)")).then_inc(ctx_loaded[slot(t, STAGE_RING)], 16)

            def load_weights(g, phase, src, stage_of, cols):
                def load(h, i, nth, last):
                    sp.wait_ge(w_low_ready, w_index(g, phase, h) - WRING + 1 + CREDIT["w_low"])
                    sp.dma_start(stage_of[:, i, 0:cols], src[ds(h, 1), :, :].rearrange("a p n -> p (a n)"))\
                        .then_inc(w_loaded[i], 16)
                heads(sp, load)

            def load_rank(it, t):
                i, (back, k) = rank_slot(t)
                sp.wait_ge(scores_done, UNITS * (it - back) + 2 * k + 2 + CREDIT["scores_done"])
                row = 32 * (i // 2) + 1
                sp.dma_start(rank_w[row:row + 2, i, :].bitcast(F32), inverse_dram[ds(TILES * it + t, 1), :, :]
                             .rearrange("a r n -> (a r) n")).then_inc(rank_loaded[i], 16)

            def maxima(it, bl):
                for t in range(TILES):
                    sp.wait_ge(max_tile_done, TILES * it + t + CREDIT["max_tile_done"])
                    sp.dma_start(stage[:, MAX_SLOT, :], ctx_in[ds(TILES * it + t, 1), :, :]
                                 .rearrange("a p n -> p (a n)")).then_inc(max_loaded, 16)
                sp.wait_ge(max_found, it + 1)
                sp.dma_start(negative_dram[ds(it, 1), :, :].rearrange("a k n -> n (a k)"), negative.bitcast(F32),
                             allow_slow_non_contiguous=True)\
                    .then_inc(max_listed, 16)
                sp.dma_start(inverse_dram[ds(TILES * it, TILES), :, :].rearrange("t r n -> n t r"),
                             inverse.bitcast(F32),
                             allow_slow_non_contiguous=True)\
                    .then_inc(max_listed, 16)
                sp.wait_ge(max_listed, 32 * (it + 1))
                for s in range(2):
                    for row in (32 * s + 1, 32 * s + 2):
                        sp.dma_start(rank_rows[row:row + 1, ds(bl, 1), :].rearrange("p a n -> p (a n)").bitcast(F32),
                                     negative_dram[ds(it, 1), 7 * s:7 * s + 7, :].rearrange("a k n -> a (k n)"))\
                            .then_inc(max_stored, 16)

            def no_maxima():
                sp.sem_inc(max_loaded, 16 * GB * TILES)
                sp.sem_inc(max_listed, 32 * GB)
                sp.sem_inc(max_stored, 64 * GB)

            for t in range(PREP):
                load_tile(0, t)
            sp.wait_ge(start_ready, START_STEPS)
            sp.dma_start(inverse_dram.rearrange("a r n -> (a r n)").rearrange("(p n) -> p n", p=P),
                         p_sum[:, 0, 0:B * TILES * 2]).then_inc(zeros_stored, 16)
            with sp.Fori(0, NG) as g:
                load_weights(g, 0, qw_in, w_stage, DIM)
                load_weights(g, 1, kw_in, w_stage, 2 * DIM)
                sp.wait_ge(zeros_stored, 16)
                where_unsafe(sp, g, maxima, no_maxima)
                with sp.Fori(0, GB) as j:
                    load_rank(GB * g + j, 0)
                    for t in range(TILES):
                        load_tile(*ahead(GB * g + j, t + PREP))
                        if t + 1 < TILES:
                            load_rank(GB * g + j, t + 1)
                load_weights(g, 2, vw_in, v_stage, VCOLS)

        @block.tensor
        def _(pe):
            pe.sem_inc(scores_done, CREDIT["scores_done"])
            pe.sem_inc(av_done, CREDIT["av_done"])
            pe.sem_inc(w_used, CREDIT["w_used"])
            pe.sem_inc(v_done, CREDIT["v_done"])
            pe.sem_inc(squares_summed, CREDIT["squares_summed"])
            pe.sem_inc(y_done, CREDIT["y_done"])
            pe.sem_inc(sum_wide, CREDIT["sum_wide"])
            pe.sem_inc(max_scores, CREDIT["max_scores"])

            def three(out, high, low, rhigh, rlow, start, stop):
                nc.tensor.matmul(out, high, rhigh, start=start, stop=False)
                nc.tensor.matmul(out, high, rlow, start=False, stop=False)
                return nc.tensor.matmul(out, low, rhigh, start=False, stop=stop)

            def queries(g):
                zero = zeros[:, :].to_broadcast([P, 1 + 2 * H])
                nc.tensor.matmul(psum[0:1 + 2 * H, 2, 0:GN], zero, zeros[:, :].to_broadcast([P, GN]), start=True,
                                 stop=False)

                def products(h, i, nth, last):
                    pe.wait_ge(w_low_ready, w_index(g, 0, h) + 1 + CREDIT["w_low"])
                    pe.wait_ge(q_copied, H * g + h - 1 + CREDIT["q_copied"])
                    for c in range(NC):
                        cols = slice(c * P, (c + 1) * P)
                        last = three(psum[:, i % 2, 0:GN], w_high[i][:, cols], w_low[i][:, cols],
                                     x_high[:, c, ds(GN * g, GN)], x_low[:, c, ds(GN * g, GN)],
                                     c == 0, c == NC - 1)
                    last.then_inc(w_used, 1)

                def squares(h, i, nth, last):
                    pe.wait_ge(q_copied, H * g + h + 1 + CREDIT["q_copied"])
                    pe.wait_ge(square_w_placed, H * g + h + 1)
                    nc.tensor.matmul(psum[0:1 + 2 * H, 2, 0:GN], square_w_ring[:, i, :], q_square[:, i % 2, :],
                                     start=False, stop=last)\
                        .then_inc(squares_summed, 1)
                heads(pe, squares, products, lead=1)
                pe.wait_ge(sums_copied, g + 1)
                for i in range(2):
                    last = nc.tensor.matmul(psum[0:TOK, 3, i * P:i * P + 1 + 2 * H],
                                            square_sums[:, TOK * i:TOK * i + TOK],
                                            ident[0:1 + 2 * H, 0:1 + 2 * H], start=True, stop=True)
                last.then_inc(sums_flipped, 1)
                pe.wait_ge(q_rms_ready, g + 1)
                for i in range(2):
                    last = nc.tensor.matmul(psum[:, 2, TOK * i:TOK * i + TOK],
                                            q_rms[:, i:i + 1].to_broadcast([TOK, P]), ident[0:TOK, 0:TOK],
                                            start=True, stop=True)
                last.then_inc(q_wide, 1)
                pe.wait_ge(bound_step, BOUND_STEPS * g + 4)
                pe.wait_ge(recip_ready, 4 * GB * g + CREDIT["recip_ready"])
                nc.tensor.matmul(psum[0:1, SUM, 0:TOK], bound_max[:, :], ident[0:TOK, 0:TOK], start=True, stop=True)\
                    .then_inc(bound_flat, 1)

            def absorb(g):
                def products(h, i, nth, last):
                    pe.wait_ge(q_wide_copied, g + 1)
                    pe.wait_ge(w_low_ready, w_index(g, 1, h) + 1 + CREDIT["w_low"])
                    pe.wait_ge(q_split, H * g + h + 1 + CREDIT["q_split"])
                    pe.wait_ge(bias_ready, H * g + h + 1)
                    pe.wait_ge(u_copied, H * g + h - 1 + CREDIT["u_copied"])
                    pe.wait_ge(u_text_copied, H * g + h - 1 + CREDIT["u_text_copied"])
                    for s in range(2):
                        for c in range(NC):
                            cols = slice(s * DIM + c * P, s * DIM + (c + 1) * P)
                            three(psum[:, 2 * (i % 2) + s, c * GN:(c + 1) * GN], w_high[i][:, cols],
                                  w_low[i][:, cols], r_high[i][:, 0:GN], r_low[i][:, 0:GN], True, True)
                    wide = [x[:, i, :, :].rearrange("p a b -> p (a b)") for x in (bias_wide_high, bias_wide_low)]
                    three(psum[:, 4 + i % 2, 0:GN], *wide, r_high[i][:, 0:GN], r_low[i][:, 0:GN], True, True)\
                        .then_inc(w_used, 1)
                heads(pe, products)

            def gram(it, t):
                s = int(t >= IMG_TILES)
                k = slot(t, CTX_RING)
                pe.wait_ge(ctx_high, TILES * it + t + 1)
                pe.wait_ge(norm_summed, TILES * it + t + CREDIT["norm_summed"])
                for c in range(NC):
                    for i, part in enumerate((gram_high, gram_low)):
                        last = nc.tensor.matmul(psum[:, GRAM, 0:DIM], c_high[:, k, c * P:(c + 1) * P],
                                                part[:, s, c, :], start=c == 0 and i == 0, stop=c == 1 and i == 1)
                last.then_inc(gram_done, 1)

            def scores(it, bl, u):
                t, half = divmod(u, 2)
                s, k = int(t >= IMG_TILES), slot(t, CTX_RING)
                cols = slice(half * HALF, (half + 1) * HALF)
                if t in (0, IMG_TILES):
                    pe.wait_ge(u_split, 4 * it + 2 * s + half + 1)
                if half == 0:
                    pe.wait_ge(ctx_low, TILES * it + t + 1)
                    i = rank_slot(t)[0]
                    of_slot = [x for x in range(TILES) if rank_slot(x)[0] == i]
                    pe.wait_ge(rank_loaded[i], 16 * (len(of_slot) * it + of_slot.index(t) + 1))
                pe.wait_ge(exp_done, UNITS * it + u - 1 + CREDIT["exp_done"])
                out = psum[:, SC + half, 0:HALF]
                for c in range(NC):
                    w = slice(c * P, (c + 1) * P)
                    three(out, c_high[:, k, w], c_low[:, k, w], u_high[:, 2 * s + c, cols], u_low[:, 2 * s + c, cols],
                          c == 0, False)
                nc.tensor.matmul(out, rank_w[:, rank_slot(t)[0], :],
                                 rank_rows[:, ds(bl, 1), cols].rearrange("p a n -> p (a n)"),
                                 start=False, stop=True).then_inc(scores_done, 1)

            def average(it, u):
                t, half = divmod(u, 2)
                s, k, n = int(t >= IMG_TILES), slot(t, CTX_RING), ROWS[t]
                if t == LONE:
                    return
                pe.wait_ge(probs_split, UNITS * it + u + 1 + CREDIT["probs_split"])
                first, last_tile = t in (0, IMG_TILES), t in (LONE - 1, TILES - 1)
                if t == 0:
                    pe.wait_ge(o_copied, 2 * it + half - 1 + CREDIT["o_copied"])
                for c in range(NC):
                    w = slice(DIM + c * P, DIM + (c + 1) * P)
                    last = three(psum[:, O + 2 * half + c, 0:HALF], c_high[0:n, k, w], c_low[0:n, k, w],
                                 p_high[0:n, half, :], p_low[0:n, half, :], first, last_tile)
                last.then_inc(av_done, 1)

            def sums(it, s, half):
                n = 4 * it + 2 * s + half
                pe.wait_ge(sum_split, n + 1 + CREDIT["sum_split"])
                pe.wait_ge(recip_ready, n + CREDIT["recip_ready"])
                nc.tensor.matmul(psum[:, SUM, 0:HALF], ones_r[:, :], p_sum_high[:, :], start=True, stop=False)
                nc.tensor.matmul(psum[:, SUM, 0:HALF], ones_r[:, :], p_sum_low[:, :], start=False, stop=True)\
                    .then_inc(sum_wide, 1)

            def carried(it, step):
                if step < 2:
                    average(it - 1, UNITS - 2 + step)
                if step in TEXT_SUMS:
                    sums(it - 1, 1, TEXT_SUMS.index(step))

            def body(it, bl, has_prev, has_next):
                for step in range(UNITS):
                    if step % 2 == 0:
                        gram(*ahead(it, step // 2 + 1))
                    scores(it, bl, step)
                    if step >= 2:
                        average(it, step - 2)
                    if has_prev:
                        carried(it, step)
                    if step in IMAGE_SUMS:
                        sums(it, 0, IMAGE_SUMS.index(step))

            def tail(it, bl):
                for step in range(TEXT_SUMS[1] + 1):
                    carried(it, step)

            def outputs(g):
                def values(h, i, nth, last):
                    pe.wait_ge(w_low_ready, w_index(g, 2, h) + 1 + CREDIT["w_low"])
                    pe.wait_ge(o_split, H * g + h + 1)
                    pe.wait_ge(v_copied, H * g + h - WRING + 1 + CREDIT["v_copied"])
                    for k in range(4):
                        cols, r = slice(k * P, (k + 1) * P), slice(k * GN, (k + 1) * GN)
                        last = three(psum[:, i, 0:GN], w_high[i][:, cols], w_low[i][:, cols], r_high[i][:, r],
                                     r_low[i][:, r], k == 0, k == 3)
                    last.then_inc(v_done, 1)

                def project(h, i, nth, last):
                    pe.wait_ge(v_split, H * g + h + 1 + CREDIT["v_split"])
                    for c in range(NC):
                        cols = slice(c * P, (c + 1) * P)
                        done = three(psum[:, 4 + c, 0:GN], ow_high[i][:, cols], ow_low[i][:, cols],
                                     v_high[:, i % 2, :], v_low[:, i % 2, :], False, last)
                    done.then_inc(y_done, 1)

                for c in range(NC):
                    nc.tensor.matmul(psum[:, 4 + c, 0:GN], zeros[:, :].to_broadcast([P, P]),
                                     zeros[:, :].to_broadcast([P, GN]), start=True, stop=False)
                heads(pe, project, values)

            def maxima(it, bl):
                pe.wait_ge(max_u_split, it + 1)
                for t in range(TILES):
                    s = int(t >= IMG_TILES)
                    pe.wait_ge(max_low, TILES * it + t + 1)
                    pe.wait_ge(max_tile_done, TILES * it + t + CREDIT["max_tile_done"])
                    for c in range(NC):
                        for i, part in enumerate((gram_high, gram_low)):
                            nc.tensor.matmul(psum[:, GRAM, 0:DIM], c_high[:, MAX_SLOT, c * P:(c + 1) * P],
                                             part[:, s, c, :], start=c == 0 and i == 0, stop=c == 1 and i == 1)
                    for half in range(2):
                        cols = slice(half * HALF, (half + 1) * HALF)
                        out = psum[:, SC + half, 0:HALF]
                        for c in range(NC):
                            w = slice(c * P, (c + 1) * P)
                            three(out, c_high[:, MAX_SLOT, w], c_low[:, MAX_SLOT, w], u_high[:, 2 * s + c, cols],
                                  u_low[:, 2 * s + c, cols], c == 0, False)
                        last = nc.tensor.matmul(out, rank_w[:, 2 * s, :], rank_rows[:, ds(bl, 1), cols]
                                                .rearrange("p a n -> p (a n)"), start=False, stop=True)
                    last.then_inc(max_scores, 1)
                pe.wait_ge(max_tile_done, TILES * (it + 1) + CREDIT["max_tile_done"])
                run = max_run.rearrange("p s n -> p (s n)")
                for k in range(2 * HS // P):
                    last = nc.tensor.transpose(psum[:, k // 4, (k % 4) * P:(k % 4 + 1) * P], run[:, k * P:(k + 1) * P],
                                               ident[:, :])
                last.then_inc(max_flipped, 1)
                pe.wait_ge(max_stored, 64 * (it + 1))

            def no_maxima():
                pe.sem_inc(max_scores, GB * TILES)
                pe.sem_inc(max_flipped, GB)

            pe.wait_ge(start_ready, START_STEPS)
            for t in range(PREP - 1):
                gram(0, t)
            with pe.Fori(0, NG) as g:
                pe.wait_ge(y_added, g + CREDIT["y_added"])
                queries(g)
                absorb(g)
                pe.wait_ge(u_copied, H * (g + 1) + CREDIT["u_copied"])
                pe.wait_ge(u_text_copied, H * (g + 1) + CREDIT["u_text_copied"])
                where_unsafe(pe, g, maxima, no_maxima)
                batches(pe, g, body, tail)
                pe.wait_ge(o_copied, 2 * GB * (g + 1) + CREDIT["o_copied"])
                outputs(g)

        @block.scalar
        def _(act):
            act.sem_inc(exp_done, CREDIT["exp_done"])
            act.sem_inc(q_copied, CREDIT["q_copied"])
            act.sem_inc(u_copied, CREDIT["u_copied"])
            act.sem_inc(v_copied, CREDIT["v_copied"])
            act.sem_inc(o_copied, CREDIT["o_copied"])

            def copy(out, in_, **kw):
                return nc.scalar.activation(out, in_, ACT.Copy, **kw)

            def loaded(g, phase, i, nth):
                act.wait_ge(w_loaded[i], 16 * (3 * (H // WRING) * g + (H // WRING) * phase + nth + 1))

            def queries(g):
                act.wait_ge(w_low_ready, w_index(g, 0, 0) + CREDIT["w_low"])

                def take(h, i, nth, last):
                    bias = small[:, ds(SMALL["qb"] + h, 1)]
                    act.wait_ge(w_used, 2 * H * g + h + 1 + CREDIT["w_used"])
                    act.wait_ge(squares_summed, H * g + h - 1 + CREDIT["squares_summed"])
                    nc.scalar.activation(q_square[:, i % 2, :], psum[:, i % 2, 0:GN], ACT.Square, bias=bias)
                    nc.scalar.activation(q_raw[:, ds(h, 1), :].rearrange("p a n -> p (a n)"), psum[:, i % 2, 0:GN],
                                         ACT.Identity, bias=bias).then_inc(q_copied, 1)
                heads(act, take)

            def absorb(g):
                def weights_high(h, i, nth):
                    loaded(g, 1, i, nth)
                    act.wait_ge(w_used, 2 * H * g + H + h - WRING + 1 + CREDIT["w_used"])
                    for s in range(2):
                        cols = slice(s * DIM, (s + 1) * DIM)
                        done = copy(w_high[i][:, cols], w_stage[:, i, cols], scale=key_scale[:, s, ds(h, 1)])
                    done.then_inc(w_high_ready, 1)

                def query_high(h, i):
                    act.wait_ge(q_scaled, H * g + h + 1 + CREDIT["q_scaled"])
                    copy(r_high[i][:, 0:GN], q_hat[:, i, :]).then_inc(q_high_ready, 1)

                def ready(h, i, nth, last):
                    weights_high(h, i, nth)
                    query_high(h, i)

                def lead_in():
                    for h in range(2):
                        weights_high(h, h, 0)
                    act.wait_ge(q_wide, g + 1)
                    copy(q_rms_wide[:, :], psum[:, 2, 0:GN]).then_inc(q_wide_copied, 1)
                    for h in range(2):
                        query_high(h, h)

                def take(h, i, nth, last):
                    act.wait_ge(w_used, 2 * H * g + H + h + 1 + CREDIT["w_used"])
                    copy(rank_rows[:, :, ds(h * S, S)], psum[:, 4 + i % 2, 0:GN].rearrange("p (b q) -> p b q", b=GB))\
                        .then_inc(rank_copied, 1)
                    uo = rows_uo[:, :, ds(h * S, S)].rearrange("p (b r) q -> p r b q", b=GB)
                    copy(uo[:, 0:2, :, :], psum[:, 2 * (i % 2), 0:2 * GN]
                         .rearrange("p (c b q) -> p c b q", c=NC, b=GB))\
                        .then_inc(u_copied, 1)
                heads(act, take, ready, lead_in=lead_in)

            def prepare(it, t):
                k, st = slot(t, CTX_RING), slot(t, STAGE_RING)
                per = len([x for x in range(TILES) if slot(x, STAGE_RING) == st])
                nth = len([x for x in range(t) if slot(x, STAGE_RING) == st])
                act.wait_ge(ctx_loaded[st], 16 * (per * it + nth + 1))
                act.wait_ge(av_done, last_unit_of_buffer(it, t))
                copy(c_high[:, k, :], stage[:, st, :]).then_inc(ctx_high, 1)

            def split_u(it, bl, s, half):
                last = UNITS * (it - 1) + (2 * IMG_TILES if s == 0 else UNITS)
                act.wait_ge(scores_done, last + CREDIT["scores_done"])
                cols = slice(half * HALF, (half + 1) * HALF)
                copy(u_high[:, 2 * s:2 * s + 2, cols], rows_uo[:, ds(4 * bl + 2 * s, 2), cols])\
                    .then_inc(u_high_ready, 1)

            def exponentials(it, u):
                t, half = divmod(u, 2)
                act.wait_ge(scores_done, UNITS * it + u + 1 + CREDIT["scores_done"])
                if half == 0:
                    act.wait_ge(key_norm, TILES * it + t + 1)
                act.wait_ge(av_done, AVERAGES * it + averaged(u - 2) + CREDIT["av_done"])
                act.wait_ge(probs_split, UNITS * it + u - 1 + CREDIT["probs_split"])
                act.wait_ge(sum_added, UNITS * it + u - 1 + CREDIT["sum_added"])
                src = psum[:, SC + half, 0:HALF]
                if t != LONE:
                    nc.scalar.activation(p_high[:, half, :], src, ACT.Exp, scale=key_rms[:, t:t + 1])
                nc.scalar.activation(probs[:, half, :], src, ACT.Exp, scale=key_rms[:, t:t + 1]).then_inc(exp_done, 1)

            def copy_o(it, bl, half):
                act.wait_ge(av_done, AVERAGES * it + averaged(UNITS - 2 + half) + CREDIT["av_done"])
                act.wait_ge(u_split, 4 * it + 2 + half + 1)
                cols = slice(half * HALF, (half + 1) * HALF)
                copy(rows_uo[:, ds(4 * bl + 2, 2), cols], psum[:, O + 2 * half:O + 2 * half + 2, 0:HALF])\
                    .then_inc(o_copied, 1)

            def carried(it, bl, step):
                if step == 0:
                    exponentials(it - 1, UNITS - 1)
                if step in (1, 2):
                    copy_o(it - 1, bl - 1, step - 1)

            def body(it, bl, has_prev, has_next):
                if not has_prev:
                    for half in range(2):
                        split_u(it, bl, 0, half)
                for step in range(UNITS):
                    if has_prev:
                        carried(it, bl, step)
                    if step >= 1:
                        exponentials(it, step - 1)
                    if step % 2 == 0:
                        prepare(*ahead(it, step // 2 + PREP))
                    if step in (3, 5):
                        split_u(it, bl, 1, (step - 3) // 2)
                    if has_next and step in (15, 17):
                        split_u(it + 1, bl + 1, 0, (step - 15) // 2)

            def tail(it, bl):
                for step in range(3):
                    carried(it, bl, step)

            def outputs(g):
                def ready(h, i, nth, last):
                    loaded(g, 2, i, nth)
                    act.wait_ge(v_done, H * g + h - WRING + 1 + CREDIT["v_done"])
                    copy(w_high[i], v_stage[:, i, 0:WCOLS]).then_inc(w_high_ready, 1)
                    early = 1 if isinstance(h, int) and h < 2 else 0
                    act.wait_ge(o_scaled, 4 * GB * (g + 1) - early + CREDIT["o_scaled"])
                    uo = rows_uo[:, :, ds(h * S, S)].rearrange("p (b r) q -> p r b q", b=GB)
                    copy(r_high[i].rearrange("p (r b q) -> p r b q", r=4, b=GB), uo).then_inc(o_high_ready, 1)

                def take(h, i, nth, last):
                    act.wait_ge(v_done, H * g + h + 1 + CREDIT["v_done"])
                    act.wait_ge(v_split, H * g + h - WRING + 1 + CREDIT["v_split"])
                    nc.scalar.activation(v_out[:, i, :], psum[:, i, 0:GN], ACT.Identity,
                                         bias=v_bias[:, ds(h, 1)]).then_inc(v_copied, 1)
                heads(act, take, ready)

            def maxima(it, bl):
                act.wait_ge(max_scores, TILES * it + CREDIT["max_scores"])
                copy(u_high[:, :, :], rows_uo[:, ds(4 * bl, 4), :]).then_inc(max_u_high, 1)
                for t in range(TILES):
                    act.wait_ge(max_loaded, 16 * (TILES * it + t + 1))
                    act.wait_ge(max_scores, TILES * it + t + CREDIT["max_scores"])
                    copy(c_high[:, MAX_SLOT, :], stage[:, MAX_SLOT, :]).then_inc(max_high, 1)
                act.wait_ge(max_scores, TILES * (it + 1) + CREDIT["max_scores"])
                act.wait_ge(max_stored, 64 * (it + 1))

            def no_maxima():
                act.sem_inc(max_u_high, GB)
                act.sem_inc(max_high, GB * TILES)

            for t in range(PREP):
                prepare(0, t)
            with act.Fori(0, NG) as g:
                queries(g)
                absorb(g)

                def u_complete():
                    act.wait_ge(u_copied, H * (g + 1) + CREDIT["u_copied"])
                    act.wait_ge(u_text_copied, H * (g + 1) + CREDIT["u_text_copied"])
                where_unsafe(act, g, maxima, no_maxima, u_complete)
                u_complete()
                batches(act, g, body, tail)
                outputs(g)

        @block.vector
        def _(dve):
            dve.sem_inc(probs_split, CREDIT["probs_split"])
            dve.sem_inc(stage_used, CREDIT["stage_used"])
            dve.sem_inc(u_text_copied, CREDIT["u_text_copied"])
            dve.sem_inc(sum_split, CREDIT["sum_split"])
            dve.sem_inc(w_low_ready, CREDIT["w_low"])
            dve.sem_inc(v_split, CREDIT["v_split"])
            dve.sem_inc(y_added, CREDIT["y_added"])
            dve.sem_inc(recip_ready, CREDIT["recip_ready"])
            dve.sem_inc(o_scaled, CREDIT["o_scaled"])
            dve.sem_inc(norm_summed, CREDIT["norm_summed"])
            dve.sem_inc(max_tile_done, CREDIT["max_tile_done"])
            dve.sem_inc(judgement_read, CREDIT["judgement_read"])

            def sub(out, a, b):
                return nc.vector.tensor_tensor(out, a, b, ALU.subtract)

            def queries(g):
                def ready(h, i, nth, last):
                    dve.wait_ge(w_loaded[i], 16 * (3 * (H // WRING) * g + nth + 1))
                    dve.wait_ge(w_used, 2 * H * g + h - WRING + 1 + CREDIT["w_used"])
                    nc.vector.tensor_copy(w_high[i][:, 0:DIM], w_stage[:, i, 0:DIM]).then_inc(q_w_high_ready, 1)
                    dve.wait_ge(squares_summed, H * g + h - WRING + 1 + CREDIT["squares_summed"])
                    nc.vector.tensor_copy(square_w_ring[:, i, :], square_w[:, ds(h, 1), :]
                                          .rearrange("p a n -> p (a n)")).then_inc(square_w_placed, 1)
                    dve.wait_ge(q_w_high_ready, H * g + h + 1)
                    sub(w_low[i][:, 0:DIM], w_stage[:, i, 0:DIM], w_high[i][:, 0:DIM].bitcast(F32))\
                        .then_inc(w_low_ready, 1)
                heads(dve, ready)
                for wide in (bias_wide_high, bias_wide_low):
                    nc.vector.memset(wide.rearrange("p r a b -> p (r a b)").bitcast(F32), 0.0).then_inc(bias_zeroed, 1)
                dve.wait_ge(squares_summed, H * (g + 1) + CREDIT["squares_summed"])
                nc.vector.tensor_copy(square_sums[:, :], psum[0:1 + 2 * H, 2, 0:GN]).then_inc(sums_copied, 1)
                dve.wait_ge(sums_flipped, g + 1)
                sums = psum[0:TOK, 3, 0:2 * P].rearrange("p (i k) -> p i k", i=2)
                nc.vector.tensor_scalar(q_ms[:, :], sums[:, :, 0], 1.0 / INNER, EPS_RMS, ALU.mult, ALU.add)\
                    .then_inc(q_ms_ready, 1)
                nc.vector.tensor_reduce(bound_sq[:, :], sums[:, :, 1:1 + 2 * H], mybir.AxisListType.X, ALU.max)\
                    .then_inc(bound_step, 1)
            def bound(g):
                dve.wait_ge(q_rms_ready, g + 1)
                dve.wait_ge(bound_step, BOUND_STEPS * g + 1)
                nc.vector.tensor_tensor(bound_sq[:, :], bound_sq[:, :], q_rms[:, :], ALU.mult).then_inc(bound_step, 1)
                dve.wait_ge(bound_step, BOUND_STEPS * g + 2)
                nc.vector.tensor_tensor(bound_sq[:, :], bound_sq[:, :], q_rms[:, :], ALU.mult).then_inc(bound_step, 1)
                dve.wait_ge(bound_step, BOUND_STEPS * g + 3)
                nc.vector.tensor_reduce(bound_max[:, :], bound_sq[:, :], mybir.AxisListType.X, ALU.max)\
                    .then_inc(bound_step, 1)

            def judge(g):
                dve.wait_ge(bound_flat, g + 1)
                nc.vector.tensor_reduce(bound_row[:, :], psum[0:1, SUM, 0:TOK], mybir.AxisListType.X, ALU.max)\
                    .then_inc(bound_step, 1)
                dve.wait_ge(bound_step, BOUND_STEPS * g + 5)
                dve.wait_ge(judgement_read, 10 * g + CREDIT["judgement_read"])
                nc.vector.tensor_scalar(is_safe[:, :], bound_row[:, :], SAFE_SCORE ** 2 / INNER, None, ALU.is_le)\
                    .then_inc(safe_known, 1)

            def absorb(g):
                def ready(h, i, nth, last):
                    dve.wait_ge(w_high_ready, 2 * H * g + h + 1)
                    for s in range(2):
                        c = slice(s * DIM, (s + 1) * DIM)
                        done = nc.vector.scalar_tensor_tensor(w_low[i][:, c], w_stage[:, i, c],
                                                              key_scale[:, s, ds(h, 1)],
                                                              w_high[i][:, c].bitcast(F32), ALU.mult, ALU.subtract)
                    done.then_inc(w_low_ready, 1)
                    dve.wait_ge(bias_zeroed, 2 * (g + 1))
                    for parts, wide in ((bias_high, bias_wide_high), (bias_low, bias_wide_low)):
                        done = nc.vector.tensor_copy(wide[:, i, :, 0], parts[:, ds(h, 1), :]
                                                     .rearrange("p a n -> p (a n)").bitcast(F32))
                    done.then_inc(bias_ready, 1)

                def take(h, i, nth, last):
                    dve.wait_ge(rank_copied, H * g + h + 1)
                    rows = slice(64, P)
                    at = rank_rows[rows, :, ds(h * S, S)]
                    sub(at, psum[rows, 4 + i % 2, 0:GN].rearrange("p (b q) -> p b q", b=GB), at.bitcast(F32))
                    uo = rows_uo[:, :, ds(h * S, S)].rearrange("p (b r) q -> p r b q", b=GB)
                    nc.vector.tensor_copy(uo[:, 2:4, :, :], psum[:, 2 * (i % 2) + 1, 0:2 * GN]
                                          .rearrange("p (c b q) -> p c b q", c=NC, b=GB)).then_inc(u_text_copied, 1)
                def lead_in():
                    for h in range(2):
                        ready(h, h, 0, False)
                    bound(g)
                    judge(g)
                heads(dve, take, ready, lead_in=lead_in)

            def norm_terms(it, t):
                k, st, s, T = slot(t, CTX_RING), slot(t, STAGE_RING), int(t >= IMG_TILES), TILES * it + t
                dve.wait_ge(ctx_low, T + 1)
                nat = slice(DIM, 2 * DIM)
                nc.vector.tensor_tensor_reduce(out=junk[:, :], in0=stage[:, st, nat], in1=twice_wb[:, s, :],
                                               scale=1.0 / INNER, scalar=bb_eps[:, s:s + 1], op0=ALU.mult,
                                               op1=ALU.add, accum_out=key_lin[:, par_of(t):par_of(t) + 1])
                if t == LONE:
                    nc.vector.tensor_copy(lone_row[:, :], stage[:, st, 0:DIM]
                                          .rearrange("p (c n) -> p c n", c=NC)[:, :, 0])
                nc.vector.tensor_tensor(c_twice[:, par_of(t), :], stage[:, st, nat], c_low[:, k, nat].bitcast(F32),
                                        ALU.add).then_inc(stage_used, 1)

            def par_of(t):
                return t % 2 if t < TILES - 1 else 0

            def norm(it, t):
                T = TILES * it + t
                dve.wait_ge(gram_done, T + 1)
                dve.wait_ge(stage_used, T + 1 + CREDIT["stage_used"])
                twice = c_twice[:, par_of(t), :]
                nc.vector.tensor_tensor_reduce(out=twice, in0=psum[:, GRAM, 0:DIM], in1=twice,
                                               scale=1.0 / INNER, scalar=key_lin[:, par_of(t):par_of(t) + 1],
                                               op0=ALU.mult, op1=ALU.add, accum_out=key_ms[:, t:t + 1])\
                    .then_inc(norm_summed, 1)

            def split_u(it, bl, s, half):
                dve.wait_ge(u_high_ready, 4 * it + 2 * s + half + 1)
                cols = slice(half * HALF, (half + 1) * HALF)
                sub(u_low[:, 2 * s:2 * s + 2, cols], rows_uo[:, ds(4 * bl + 2 * s, 2), cols],
                    u_high[:, 2 * s:2 * s + 2, cols].bitcast(F32)).then_inc(u_split, 1)

            def split_probs(it, bl, u):
                t, half = divmod(u, 2)
                dve.wait_ge(exp_done, UNITS * it + u + 1 + CREDIT["exp_done"])
                if t != LONE:
                    sub(p_low[:, half, :], probs[:, half, :], p_high[:, half, :].bitcast(F32)).then_inc(probs_split, 1)
                    return
                dve.wait_ge(stage_used, TILES * it + t + 1 + CREDIT["stage_used"])
                dve.wait_ge(av_done, AVERAGES * it + averaged(u - 2) + CREDIT["av_done"])
                dve.wait_ge(u_split, 4 * it + half + 1)
                for c in range(NC):
                    last = nc.vector.scalar_tensor_tensor(
                        rows_uo[:, ds(4 * bl + c, 1), half * HALF:(half + 1) * HALF].rearrange("p a n -> p (a n)"),
                        probs[:, half, :], lone_row[:, c:c + 1], psum[:, O + 2 * half + c, 0:HALF], ALU.mult, ALU.add)
                last.then_inc(probs_split, 1)

            def split_sum(it, s, half):
                last = 2 * (IMG_TILES if s == 0 else TILES) - 2 + half
                n = 4 * it + 2 * s + half
                dve.wait_ge(sum_added, UNITS * it + last + 1 + CREDIT["sum_added"])
                dve.wait_ge(sum_wide, n + CREDIT["sum_wide"])
                nc.vector.tensor_copy(p_sum_high[:, :], p_sum[:, 2 * s + half, :]).then_inc(sum_high_ready, 1)
                dve.wait_ge(sum_high_ready, n + 1)
                sub(p_sum_low[:, :], p_sum[:, 2 * s + half, :], p_sum_high[:, :].bitcast(F32)).then_inc(sum_split, 1)

            def reciprocal(it, s, half, part):
                n = 4 * it + 2 * s + half
                cols = slice(part * (HALF // 4), (part + 1) * (HALF // 4))
                if part == 0:
                    dve.wait_ge(sum_wide, n + 1 + CREDIT["sum_wide"])
                    dve.wait_ge(o_scaled, n + CREDIT["o_scaled"])
                r = nc.vector.reciprocal(recip[:, cols], psum[:, SUM, cols])
                if part == 3:
                    r.then_inc(recip_ready, 1)

            def scale_o(it, bl, s, half):
                n = 4 * it + 2 * s + half
                dve.wait_ge(recip_ready, n + 1 + CREDIT["recip_ready"])
                if s == 0:
                    dve.wait_ge(probs_split, UNITS * it + 2 * LONE + half + 1 + CREDIT["probs_split"])
                else:
                    dve.wait_ge(o_copied, 2 * it + half + 1 + CREDIT["o_copied"])
                cols = slice(half * HALF, (half + 1) * HALF)
                at = rows_uo[:, ds(4 * bl + 2 * s, 2), cols]
                nc.vector.tensor_tensor(at, at, recip[:, :].unsqueeze(1).to_broadcast([P, 2, HALF]), ALU.mult)\
                    .then_inc(o_scaled, 1)

            def set_end(it, bl, s, parts):
                for what, half, *part in parts:
                    if what == "split":
                        split_sum(it, s, half)
                    if what == "invert":
                        reciprocal(it, s, half, *part)
                    if what == "scale":
                        scale_o(it, bl, s, half)

            def body(it, bl, has_prev, has_next):
                if not has_prev:
                    for half in range(2):
                        split_u(it, bl, 0, half)
                for step in range(UNITS):
                    if has_prev and step == 0:
                        split_probs(it - 1, bl - 1, UNITS - 1)
                    norms_first = step == 2 * LONE + 2
                    if step >= 1 and not norms_first:
                        split_probs(it, bl, step - 1)
                    if step in (3, 5):
                        split_u(it, bl, 1, (step - 3) // 2)
                    if step % 2 == 0:
                        norm_terms(*ahead(it, step // 2 + 1))
                        norm(*ahead(it, step // 2 + 1))
                    if norms_first:
                        split_probs(it, bl, step - 1)
                    if has_prev:
                        set_end(it - 1, bl - 1, 1, TEXT_END.get(step, ()))
                    set_end(it, bl, 0, IMAGE_END.get(step, ()))
                    if has_next and step in (15, 17):
                        split_u(it + 1, bl + 1, 0, (step - 15) // 2)

            def tail(it, bl):
                split_probs(it - 1, bl - 1, UNITS - 1)
                set_end(it - 1, bl - 1, 1, LAST_END[0])

            def outputs(g):
                def ready(h, i, nth, last):
                    dve.wait_ge(w_loaded[i], 16 * (3 * (H // WRING) * g + 2 * (H // WRING) + nth + 1))
                    dve.wait_ge(y_done, H * g + h - WRING + 1 + CREDIT["y_done"])
                    nc.vector.tensor_copy(ow_high[i], v_stage[:, i, WCOLS:VCOLS]).then_inc(ow_high_ready, 1)
                    dve.wait_ge(o_high_ready, H * g + h + 1)
                    uo = rows_uo[:, :, ds(h * S, S)].rearrange("p (b r) q -> p r b q", b=GB)
                    wide = lambda x: x.rearrange("p (r b q) -> p r b q", r=4, b=GB)
                    sub(wide(r_low[i]), uo, wide(r_high[i].bitcast(F32))).then_inc(o_split, 1)

                def take(h, i, nth, last):
                    k = H * g + h
                    dve.wait_ge(v_copied, k + 1 + CREDIT["v_copied"])
                    dve.wait_ge(y_done, k - 1 + CREDIT["y_done"])
                    nc.vector.tensor_copy(v_high[:, i % 2, :], v_out[:, i, :]).then_inc(v_high_ready, 1)
                    dve.wait_ge(v_high_ready, k + 1)
                    sub(v_low[:, i % 2, :], v_out[:, i, :], v_high[:, i % 2, :].bitcast(F32)).then_inc(v_split, 1)
                def lead_in():
                    ready(0, 0, 0, False)
                    ready(1, 1, 0, False)
                    set_end(GB * g + GB - 1, GB - 1, 1, LAST_END[1])
                heads(dve, take, ready, lead_in=lead_in)
                dve.wait_ge(y_done, H * (g + 1) + CREDIT["y_done"])
                for c in range(NC):
                    ob = small[:, SMALL["ob"] + c:SMALL["ob"] + c + 1]
                    at = xT[:, c, ds(GN * g, GN)]
                    last = nc.vector.scalar_tensor_tensor(at, psum[:, 4 + c, 0:GN], ob, at, ALU.add, ALU.add)
                last.then_inc(y_added, 1)

            def maxima(it, bl):
                MAX_STEPS = 4
                dve.wait_ge(max_u_high, it + 1)
                sub(u_low[:, :, :], rows_uo[:, ds(4 * bl, 4), :], u_high[:, :, :].bitcast(F32)).then_inc(max_u_split, 1)
                nat = slice(DIM, 2 * DIM)
                for t in range(TILES):
                    T, s, n, one = TILES * it + t, int(t >= IMG_TILES), ROWS[t], slice(t, t + 1)
                    dve.wait_ge(max_high, T + 1)
                    sub(c_low[:, MAX_SLOT, :], stage[:, MAX_SLOT, :], c_high[:, MAX_SLOT, :].bitcast(F32))\
                        .then_inc(max_low, 1)
                    dve.wait_ge(max_low, T + 1)
                    nc.vector.tensor_tensor_reduce(out=junk[:, :], in0=stage[:, MAX_SLOT, nat],
                                                   in1=twice_wb[:, s, :], scale=1.0 / INNER, scalar=bb_eps[:, s:s + 1],
                                                   op0=ALU.mult, op1=ALU.add, accum_out=max_lin[:, one])\
                        .then_inc(max_terms, 1)
                    nc.vector.tensor_tensor(max_twice, stage[:, MAX_SLOT, nat], c_low[:, MAX_SLOT, nat].bitcast(F32),
                                            ALU.add).then_inc(max_terms, 1)
                    dve.wait_ge(max_terms, 2 * T + 2)
                    dve.wait_ge(max_scores, T + 1 + CREDIT["max_scores"])
                    nc.vector.tensor_tensor_reduce(out=max_twice, in0=psum[:, GRAM, 0:DIM], in1=max_twice,
                                                   scale=1.0 / INNER, scalar=max_lin[:, one], op0=ALU.mult,
                                                   op1=ALU.add, accum_out=max_ms[:, one]).then_inc(max_summed, 1)
                    dve.wait_ge(max_rooted, T + 1)
                    dve.wait_ge(max_tile_done, T + CREDIT["max_tile_done"])
                    for half in range(2):
                        run, src = max_run[0:n, 2 * s + half, :], psum[0:n, SC + half, 0:HALF]
                        if t in (0, IMG_TILES):
                            last = nc.vector.tensor_scalar(run, src, max_root[0:n, one], None, ALU.mult)
                        else:
                            last = nc.vector.scalar_tensor_tensor(run, src, max_root[0:n, one], run, ALU.mult, ALU.max)
                    last.then_inc(max_tile_done, 1)
                dve.wait_ge(max_summed, TILES * (it + 1))
                nc.vector.tensor_tensor(max_inverse, max_ms, max_root, ALU.mult).then_inc(max_steps, 1)
                dve.wait_ge(max_steps, MAX_STEPS * it + 1)
                nc.vector.tensor_copy(inverse[:, :, 0], max_inverse).then_inc(max_steps, 1)
                dve.wait_ge(max_steps, MAX_STEPS * it + 2)
                sub(inverse[:, :, 1], max_inverse, inverse[:, :, 0].bitcast(F32)).then_inc(max_steps, 1)
                dve.wait_ge(max_flipped, it + 1)
                nc.vector.tensor_reduce(max_cols, psum[:, 0:4, :].rearrange("p a n -> p (a n)")[:, 0:2 * HS]
                                        .rearrange("p (k n) -> p k n", n=P), mybir.AxisListType.X, ALU.max)\
                    .then_inc(max_steps, 1)
                dve.wait_ge(max_steps, MAX_STEPS * it + 4)
                nc.vector.tensor_scalar(negative, max_cols, -1.0, None, ALU.mult).then_inc(max_found, 1)
                dve.wait_ge(max_stored, 64 * (it + 1))

            def no_maxima():
                dve.sem_inc(max_u_split, GB)
                dve.sem_inc(max_low, GB * TILES)
                dve.sem_inc(max_terms, 2 * GB * TILES)
                dve.sem_inc(max_summed, GB * TILES)
                dve.sem_inc(max_tile_done, GB * TILES)
                dve.sem_inc(max_steps, 4 * GB)
                dve.sem_inc(max_found, GB)

            nc.vector.memset(zeros[:, :], 0.0).then_inc(start_ready, 1)
            nc.vector.memset(p_sum[:, 0, 0:B * TILES * 2], 0.0).then_inc(start_ready, 1)
            nc.vector.memset(key_ms[:, :], 0.0).then_inc(start_ready, 1)
            nc.vector.memset(key_lin[:, :], 0.0).then_inc(start_ready, 1)
            dve.wait_ge(start_ready, START_STEPS)
            norm_terms(0, 0)
            norm(0, 0)
            with dve.Fori(0, NG) as g:
                queries(g)
                absorb(g)
                where_unsafe(dve, g, maxima, no_maxima)
                batches(dve, g, body, tail)
                outputs(g)

        @block.gpsimd
        def _(gp):
            gp.sem_inc(sum_added, CREDIT["sum_added"])
            gp.sem_inc(q_scaled, CREDIT["q_scaled"])
            gp.sem_inc(q_split, CREDIT["q_split"])

            def absorb(g):
                def scale(h, i, nth, last):
                    gp.wait_ge(q_wide_copied, g + 1)
                    gp.wait_ge(q_split, H * g + h - WRING + 1 + CREDIT["q_split"])
                    nc.gpsimd.tensor_tensor(q_hat[:, i, :], q_raw[:, ds(h, 1), :].rearrange("p a n -> p (a n)"),
                                            q_rms_wide[:, :], ALU.mult).then_inc(q_scaled, 1)

                def split(h, i, nth, last):
                    gp.wait_ge(q_high_ready, H * g + h + 1)
                    nc.gpsimd.tensor_tensor(r_low[i][:, 0:GN], q_hat[:, i, :], r_high[i][:, 0:GN].bitcast(F32),
                                            ALU.subtract).then_inc(q_split, 1)
                heads(gp, split, scale, lead=1)

            def outputs(g):
                def split(h, i, nth, last):
                    gp.wait_ge(w_high_ready, 2 * H * g + H + h + 1)
                    nc.gpsimd.tensor_tensor(w_low[i], v_stage[:, i, 0:WCOLS], w_high[i].bitcast(F32), ALU.subtract)
                    gp.wait_ge(ow_high_ready, H * g + h + 1)
                    nc.gpsimd.tensor_tensor(ow_low[i], v_stage[:, i, WCOLS:VCOLS], ow_high[i].bitcast(F32),
                                            ALU.subtract).then_inc(w_low_ready, 1)
                heads(gp, split)

            def key_root(it, t):
                gp.wait_ge(norm_summed, TILES * it + t + 1 + CREDIT["norm_summed"])
                nc.gpsimd.tensor_tensor(key_rms[:, t:t + 1], key_ms[:, t:t + 1], minus_half[:, 0:1], ALU.pow)\
                    .then_inc(key_norm, 1)

            def split_tile(it, t):
                k, st = slot(t, CTX_RING), slot(t, STAGE_RING)
                gp.wait_ge(ctx_high, TILES * it + t + 1)
                nc.gpsimd.tensor_tensor(c_low[:, k, :], stage[:, st, :], c_high[:, k, :].bitcast(F32), ALU.subtract)\
                    .then_inc(ctx_low, 1)

            def add(it, u):
                t, half = divmod(u, 2)
                s, n = int(t >= IMG_TILES), ROWS[t]
                gp.wait_ge(exp_done, UNITS * it + u + 1 + CREDIT["exp_done"])
                if t in (0, IMG_TILES):
                    gp.wait_ge(sum_split, 4 * (it - 1) + 2 * s + half + 1 + CREDIT["sum_split"])
                    before_it = zeros[0:n, :].to_broadcast([n, HALF])
                else:
                    before_it = p_sum[0:n, 2 * s + half, :]
                gp.wait_ge(sum_added, UNITS * it + u - 1 + CREDIT["sum_added"])
                nc.gpsimd.tensor_tensor(p_sum[0:n, 2 * s + half, :], probs[0:n, half, :], before_it, ALU.add)\
                    .then_inc(sum_added, 1)

            def body(it, bl, has_prev, has_next):
                for step in range(UNITS):
                    if has_prev and step == 0:
                        add(it - 1, UNITS - 1)
                    if step >= 1:
                        add(it, step - 1)
                    if step % 2 == 0:
                        key_root(*ahead(it, step // 2 + 1))
                    else:
                        split_tile(*ahead(it, step // 2 + PREP))

            def tail(it, bl):
                add(it - 1, UNITS - 1)

            def maxima(it, bl):
                for t in range(TILES):
                    gp.wait_ge(max_summed, TILES * it + t + 1)
                    nc.gpsimd.tensor_tensor(max_root[:, t:t + 1], max_ms[:, t:t + 1], minus_half[:, 0:1], ALU.pow)\
                        .then_inc(max_rooted, 1)

            def no_maxima():
                gp.sem_inc(max_rooted, GB * TILES)

            gp.wait_ge(start_ready, START_STEPS)
            for t in range(PREP):
                split_tile(0, t)
            key_root(0, 0)
            gp.wait_ge(zeros_stored, 16)
            with gp.Fori(0, NG) as g:
                gp.wait_ge(q_ms_ready, g + 1)
                nc.gpsimd.tensor_tensor(q_rms[:, :], q_ms[:, :], minus_half[0:TOK, 0:2], ALU.pow)\
                    .then_inc(q_rms_ready, 1)
                absorb(g)
                where_unsafe(gp, g, maxima, no_maxima)
                batches(gp, g, body, tail)
                outputs(g)


def experts(nc, router_in, bias_in, ffn_in, out, probs_dram, psum, xT, ident, ones, minus_half):
    ctx = ExitStack()
    with ctx:
        sb = lambda n, s, dt=F32: ctx.enter_context(nc.sbuf_tensor(n, s, dt))
        sem = lambda n: ctx.enter_context(nc.semaphore(n))
        RT = N // P
        RING = 3
        WCOLS = 3 * DIM
        credit = {"w_split": RING, "scaled": 2 * RING, "down_done": 2 * RING, "h_split": 2, "clipped": 2}
        xn = sb("ffn_xn", [P, NC, N])
        x_high, x_low = sb("ffn_x_high", [P, NC, N], F32R), sb("ffn_x_low", [P, NC, N], F32R)
        router = sb("router", [P, NC, E])
        e_bias = sb("e_bias", [P, E])
        logit, absolute, u, w, lnw, big, small, mask, score = [
            sb(n, [P, RT, E]) for n in ("logit", "absolute", "exp_abs", "one_plus", "ln_one_plus", "log1p_big",
                                        "log1p_small", "mask", "score")]
        ranked, picked = sb("ranked", [P, RT, E + 4]), sb("picked", [P, RT, E + 4])
        top = sb("top", [P, RT, 8])
        p_sum, p_rec = sb("chosen_sum", [P, RT]), sb("chosen_rec", [P, RT])
        probs = sb("router_probs", [P, RT, E])
        probs_T = sb("probs_T", [E + 1, N])
        w_stage = sb("e_stage", [P, RING, WCOLS])
        w_high, w_low = sb("e_high", [P, RING, WCOLS], F32R), sb("e_low", [P, RING, WCOLS], F32R)
        p_wide = sb("p_wide", [P, RING, N])
        gate, gated, scaled_gate, up, h = [sb(n, [P, 2, N // 2]) for n in ("gate", "gated", "scaled_gate", "up", "h")]
        h_high, h_low = sb("h_high", [P, 2, N // 2], F32R), sb("h_low", [P, 2, N // 2], F32R)
        HN = N // 2
        DOWN, GATE_UP = 0, 4

        router_loaded, x_high_ready, x_split = (
            sem("router_loaded"), sem("ffn_x_high_ready"), sem("ffn_x_split"))
        logits_done, chain, act_chain = sem("logits_done"), sem("router_chain"), sem("router_act")
        flipped, probs_stored, out_stored = sem("flipped"), sem("probs_stored"), sem("out_stored")
        w_loaded = [sem(f"e_loaded{i}") for i in range(RING)]
        p_loaded = [sem(f"p_loaded{i}") for i in range(RING)]
        p_first, p_first_copied = sem("p_first"), sem("p_first_copied")
        w_high_ready, w_split = sem("e_high_ready"), sem("e_split")
        gate_up_done, gate_clipped, up_clipped, silu_done, scaled, h_ready, h_high_ready, h_split, down_done = [
            sem(n) for n in ("gate_up_done", "gate_clipped", "up_clipped", "silu_done", "gate_scaled", "h_ready",
                             "h_high_ready", "h_split", "down_done")]
        out_ready = sem("out_ready")
        ln_pe, ln_act, ln_dve, ln_pool, ln_done = layer_norm(
            nc, ctx, "ln2", xT, lambda c: xn[:, c, :].rearrange("p (h n) -> p h n", h=2), psum[:, 0:3, :])
        block = ctx.enter_context(nc.Block())

        def triples(eng, body):
            body(0, True)
            with eng.Fori(1, (E + 1) // RING) as k:
                body(k, False)

        @block.sync
        def _(sp):
            def load_weights(e, i):
                sp.wait_ge(w_split, e - RING + 1 + credit["w_split"])
                sp.dma_start(w_stage[:, i, :], ffn_in[ds(e, 1), :, :].rearrange("a p n -> p (a n)"))\
                    .then_inc(w_loaded[i], 16)

            def load_probs(e, i):
                sp.wait_ge(scaled, 2 * (e - RING + 1) + credit["scaled"])
                sp.dma_start(p_wide[:, i, :], probs_dram[ds(e, 1), :].partition_broadcast(P))\
                    .then_inc(p_loaded[i], 16)

            sp.dma_start(router[:, :, :], router_in).then_inc(router_loaded, 16)
            sp.dma_start(e_bias[:, :], bias_in.partition_broadcast(P)).then_inc(router_loaded, 16)
            load_weights(0, 0)
            load_weights(1, 1)
            sp.wait_ge(chain, ROUTER_STEPS)
            sp.dma_start(probs_dram, probs_T[:, :]).then_inc(probs_stored, 16)
            sp.wait_ge(probs_stored, 16)

            def body(k, first):
                for i in range(RING):
                    if not (first and i == 0):
                        load_probs(RING * k + i, i)
                    load_weights(RING * k + i + 2, (i + 2) % RING)
            triples(sp, body)
            sp.wait_ge(w_loaded[(E + 2) % RING], 16 * ((E + 2) // RING + 1))
            for c in range(NC):
                sp.wait_ge(out_ready, c + 1)
                sp.dma_start(out[:, c, :], xT[:, c, :]).then_inc(out_stored, 16)
            sp.wait_ge(out_stored, 16 * NC)

        @block.gpsimd
        def _(gp):
            gp.sem_inc(scaled, credit["scaled"])
            ln_pool(gp, minus_half)

            def body(k, first):
                for j in range(2 * RING):
                    i, half, v = j // 2, j % 2, 2 * RING * k + j
                    if first and i == 0:
                        gp.wait_ge(p_first_copied, half + 1)
                    else:
                        gp.wait_ge(p_loaded[i], 16 * (k + 1 - int(i == 0)))
                    gp.wait_ge(silu_done, v + 1)
                    nc.gpsimd.tensor_tensor(scaled_gate[:, half, :], gated[:, half, :],
                                            p_wide[:, i, half * HN:(half + 1) * HN], ALU.mult).then_inc(scaled, 1)
            triples(gp, body)

        @block.tensor
        def _(pe):
            pe.sem_inc(down_done, credit["down_done"])

            def three(out, high, low, rhigh, rlow, start, stop):
                nc.tensor.matmul(out, high, rhigh, start=start, stop=False)
                nc.tensor.matmul(out, high, rlow, start=False, stop=False)
                return nc.tensor.matmul(out, low, rhigh, start=False, stop=stop)

            ln_pe(pe, ones, ident)
            pe.wait_ge(router_loaded, 32)
            pe.wait_ge(ln_done, NC)
            for i in range(RT):
                for c in range(NC):
                    last = nc.tensor.matmul(psum[:, 3, i * E:(i + 1) * E], xn[:, c, i * P:(i + 1) * P],
                                            router[:, c, :], start=c == 0, stop=c == NC - 1)
            last.then_inc(logits_done, 1)
            pe.wait_ge(x_split, NC)

            def gate_up(k, j):
                i, half, v = j // 2, j % 2, 2 * RING * k + j
                if half == 0:
                    pe.wait_ge(w_split, RING * k + i + 1 + credit["w_split"])
                pe.wait_ge(up_clipped, v - 1 + credit["clipped"])
                for m in range(2):
                    for c in range(NC):
                        cols = slice(m * DIM + c * P, m * DIM + (c + 1) * P)
                        r = slice(half * HN, (half + 1) * HN)
                        last = three(psum[:, GATE_UP + 2 * half + m, 0:HN], w_high[:, i, cols], w_low[:, i, cols],
                                     x_high[:, c, r], x_low[:, c, r], c == 0, c == NC - 1)
                last.then_inc(gate_up_done, 1)

            def down(k, j, start, stop):
                i, half, v = j // 2, j % 2, 2 * RING * k + j
                pe.wait_ge(h_split, v + 1 + credit["h_split"])
                for c in range(NC):
                    cols = slice(2 * DIM + c * P, 2 * DIM + (c + 1) * P)
                    last = three(psum[:, DOWN + 2 * half + c, 0:HN], w_high[:, i, cols], w_low[:, i, cols],
                                 h_high[:, half, :], h_low[:, half, :], start, stop)
                last.then_inc(down_done, 1)

            for j in range(2):
                gate_up(0, j)
            pe.wait_ge(chain, ROUTER_STEPS - 2)
            for i in range(RT):
                last = nc.tensor.transpose(psum[0:E, i // 4, (i % 4) * P:(i % 4 + 1) * P], probs[:, i, :],
                                           ident[:, :])
            last.then_inc(flipped, 1)
            pe.wait_ge(chain, ROUTER_STEPS)
            for half in range(2):
                nc.tensor.matmul(psum[:, 2 + half, 0:HN], ones[0:1, :], probs_T[0:1, half * HN:(half + 1) * HN],
                                 start=True, stop=True).then_inc(p_first, 1)
            pe.wait_ge(p_first_copied, 2)

            def body(k, first):
                for j in range(2 * RING):
                    if not (first and j < 2):
                        gate_up(k, j)
                    if j >= 2:
                        down(k, j - 2, first and j < 4, False)
                    elif not first:
                        down(k - 1, 2 * RING - 2 + j, False, False)
            triples(pe, body)
            for j in (4, 5):
                down((E + 1) // RING - 1, j, False, True)

        @block.scalar
        def _(act):
            copy = lambda out, in_: nc.scalar.activation(out, in_, ACT.Copy)
            def split(e, i, k_loads):
                act.wait_ge(w_loaded[i], 16 * k_loads)
                act.wait_ge(down_done, 2 * (e - RING + 1) + credit["down_done"])
                copy(w_high[:, i, :], w_stage[:, i, :]).then_inc(w_high_ready, 1)

            ln_act(act)
            split(0, 0, 1)
            for c in range(NC):
                act.wait_ge(ln_done, c + 1)
                copy(x_high[:, c, :], xn[:, c, :]).then_inc(x_high_ready, 1)
            act.wait_ge(chain, 2)
            nc.scalar.activation(u[:, :, :], absolute[:, :, :], ACT.Exp, scale=-1.0).then_inc(act_chain, 1)
            act.wait_ge(chain, 3)
            nc.scalar.activation(lnw[:, :, :], w[:, :, :], ACT.Ln).then_inc(act_chain, 1)
            act.wait_ge(chain, SOFTPLUS_STEPS)
            nc.scalar.activation(score[:, :, :], big[:, :, :], ACT.Sqrt).then_inc(act_chain, 1)

            def silu(v, half):
                act.wait_ge(gate_clipped, v + 1)
                act.wait_ge(scaled, v - 1 + credit["scaled"])
                nc.scalar.activation(gated[:, half, :], gate[:, half, :], ACT.Silu).then_inc(silu_done, 1)

            def high(v, half):
                act.wait_ge(h_ready, v + 1)
                act.wait_ge(down_done, v - 1 + credit["down_done"])
                copy(h_high[:, half, :], h[:, half, :]).then_inc(h_high_ready, 1)

            def body(k, first):
                for j in range(2 * RING):
                    v = 2 * RING * k + j
                    silu(v, j % 2)
                    if first and j == 1:
                        for half in range(2):
                            act.wait_ge(p_first, half + 1)
                            copy(p_wide[:, 0, half * HN:(half + 1) * HN], psum[:, 2 + half, 0:HN])\
                                .then_inc(p_first_copied, 1)
                    if not (first and j == 0):
                        high(v - 1, (j - 1) % 2)
                    if j % 2 == 0:
                        split(RING * k + j // 2 + 1, (j // 2 + 1) % RING, k + 1 + (j // 2 + 1) // RING)
            triples(act, body)
            high(2 * (E + 1) - 1, 1)

        @block.vector
        def _(dve):
            dve.sem_inc(w_split, credit["w_split"])
            dve.sem_inc(h_split, credit["h_split"])
            dve.sem_inc(up_clipped, credit["clipped"])
            V = nc.vector

            def split(e, i):
                dve.wait_ge(w_high_ready, e + 1)
                V.tensor_tensor(w_low[:, i, :], w_stage[:, i, :], w_high[:, i, :].bitcast(F32), ALU.subtract)\
                    .then_inc(w_split, 1)

            def clip(v, half):
                dve.wait_ge(gate_up_done, v + 1)
                V.tensor_scalar(gate[:, half, :], psum[:, GATE_UP + 2 * half, 0:HN], ALPHA, -ALPHA, ALU.min, ALU.max)\
                    .then_inc(gate_clipped, 1)
                V.tensor_scalar(up[:, half, :], psum[:, GATE_UP + 2 * half + 1, 0:HN], ALPHA, -ALPHA, ALU.min,
                                ALU.max).then_inc(up_clipped, 1)

            V.memset(probs_T[E:E + 1, :], 1.0)
            ln_dve(dve, (lambda: split(0, 0), lambda: None))
            for c in range(NC):
                dve.wait_ge(x_high_ready, c + 1)
                V.tensor_tensor(x_low[:, c, :], xn[:, c, :], x_high[:, c, :].bitcast(F32), ALU.subtract)\
                    .then_inc(x_split, 1)
            steps = [0]

            def link(ins):
                steps[0] += 1
                ins.then_inc(chain, 1)
                dve.wait_ge(chain, steps[0])

            dve.wait_ge(logits_done, 1)
            link(V.tensor_copy(logit[:, :, :], psum[:, 3, 0:RT * E].rearrange("p (t e) -> p t e", t=RT)))
            link(V.scalar_tensor_tensor(absolute[:, :, :], logit[:, :, :], -1.0, logit[:, :, :], ALU.mult, ALU.max))
            dve.wait_ge(act_chain, 1)
            link(V.tensor_scalar(w[:, :, :], u[:, :, :], 1.0, None, ALU.add))
            link(V.tensor_scalar(big[:, :, :], w[:, :, :], -1.0, 1e-30, ALU.add, ALU.max))
            link(V.reciprocal(mask[:, :, :], big[:, :, :]))
            link(V.tensor_tensor(big[:, :, :], mask[:, :, :], u[:, :, :], ALU.mult))
            dve.wait_ge(act_chain, 2)
            link(V.tensor_tensor(big[:, :, :], big[:, :, :], lnw[:, :, :], ALU.mult))
            link(V.tensor_scalar(small[:, :, :], u[:, :, :], 1 / 5, -1 / 4, ALU.mult, ALU.add))
            for term in (1 / 3, -1 / 2, 1.0):
                link(V.tensor_tensor(small[:, :, :], small[:, :, :], u[:, :, :], ALU.mult))
                link(V.tensor_scalar(small[:, :, :], small[:, :, :], term, None, ALU.add))
            link(V.tensor_tensor(small[:, :, :], small[:, :, :], u[:, :, :], ALU.mult))
            link(V.tensor_scalar(mask[:, :, :], u[:, :, :], 1 / 64, None, ALU.is_lt))
            link(V.tensor_tensor(small[:, :, :], small[:, :, :], big[:, :, :], ALU.subtract))
            link(V.tensor_tensor(small[:, :, :], small[:, :, :], mask[:, :, :], ALU.mult))
            link(V.tensor_tensor(small[:, :, :], small[:, :, :], big[:, :, :], ALU.add))
            link(V.scalar_tensor_tensor(big[:, :, :], logit[:, :, :], 0.0, small[:, :, :], ALU.max, ALU.add))
            assert steps[0] == SOFTPLUS_STEPS, steps
            link(V.memset(ranked[:, :, E:E + 4], -1e30))
            dve.wait_ge(router_loaded, 32)
            dve.wait_ge(act_chain, 3)
            link(V.tensor_tensor(ranked[:, :, 0:E], score[:, :, :], e_bias[:, :].unsqueeze(1).to_broadcast([P, RT, E]),
                                 ALU.add))
            for j in range(2):
                clip(j, j)
            for t in range(RT):
                V.max(top[:, t, :], ranked[:, t, 0:E])
            link(V.memset(small[:, :, :], 0.0))
            link(V.memset(top[:, :, K_TOP:8], -1e30))
            for t in range(RT):
                V.match_replace(picked[:, t, :], top[:, t, :], ranked[:, t, :], -3e38)
            link(V.memset(mask[:, :, :], 0.0))
            link(V.tensor_tensor(mask[:, :, :], picked[:, :, 0:E], ranked[:, :, 0:E], ALU.is_lt))
            link(V.tensor_tensor(score[:, :, :], score[:, :, :], mask[:, :, :], ALU.mult))
            link(V.tensor_reduce(p_sum[:, :], score[:, :, :], mybir.AxisListType.X, ALU.add))
            link(V.tensor_scalar(p_sum[:, :], p_sum[:, :], 1e-20, None, ALU.add))
            link(V.reciprocal(p_rec[:, :], p_sum[:, :]))
            link(V.tensor_tensor(probs[:, :, :], score[:, :, :], p_rec[:, :].unsqueeze(2).to_broadcast([P, RT, E]),
                                 ALU.mult))
            assert steps[0] == ROUTER_STEPS - 2, steps
            split(1, 1)
            dve.wait_ge(flipped, 1)
            link(V.tensor_copy(probs_T[0:E, 0:4 * P], psum[0:E, 0, 0:4 * P]))
            link(V.tensor_copy(probs_T[0:E, 4 * P:N], psum[0:E, 1, 0:N - 4 * P]))

            def multiply(v, half):
                dve.wait_ge(scaled, v + 1 + credit["scaled"])
                dve.wait_ge(up_clipped, v + 1 + credit["clipped"])
                dve.wait_ge(h_split, v - 1 + credit["h_split"])
                V.tensor_tensor(h[:, half, :], up[:, half, :], scaled_gate[:, half, :], ALU.mult).then_inc(h_ready, 1)

            def low(v, half):
                dve.wait_ge(h_high_ready, v + 1)
                V.tensor_tensor(h_low[:, half, :], h[:, half, :], h_high[:, half, :].bitcast(F32), ALU.subtract)\
                    .then_inc(h_split, 1)

            def body(k, first):
                for j in range(2 * RING):
                    v = 2 * RING * k + j
                    if j % 2 == 1 and not (first and j == 1):
                        split(RING * k + j // 2 + 1, (j // 2 + 1) % RING)
                    if not (first and j < 2):
                        clip(v, j % 2)
                    if not (first and j == 0):
                        multiply(v - 1, (j - 1) % 2)
                    if not (first and j == 0):
                        low(v - 1, (j - 1) % 2)
            triples(dve, body)
            v = 2 * (E + 1) - 1
            multiply(v, 1)
            low(v, 1)
            dve.wait_ge(down_done, 2 * (E + 1) + credit["down_done"])
            for c in range(NC):
                at = xT[:, c, :].rearrange("p (h n) -> p h n", h=2)
                acc = psum[:, DOWN:DOWN + 4, 0:HN].rearrange("p (h c) n -> p h c n", h=2)[:, :, c, :]
                V.tensor_tensor(at, at, acc, ALU.add).then_inc(out_ready, 1)


SOFTPLUS_STEPS = 20
ROUTER_STEPS = 33


def _layouts(a):
    import numpy as np
    chunks = lambda w: w.reshape(NC, P, -1).transpose(1, 0, 2)
    x = np.asarray(a["x"]).reshape(N, DIM)
    context = np.asarray(a["ctx_2048"])
    tiles = np.zeros((B, TILES, P, DIM), np.float32)
    start = 0
    for t, n in enumerate(ROWS):
        tiles[:, t, :n] = context[:, start:start + n]
        start += n
    tiles[:, LONE] = tiles[:, LONE, 0:1]
    packed = np.zeros((B * TILES + PREP, P, 2 * DIM), np.float32)
    flat = tiles.reshape(B * TILES, P, DIM)
    packed[:B * TILES, :, 0:DIM] = flat.reshape(-1, P, NC, P).transpose(0, 3, 2, 1).reshape(-1, P, DIM)
    packed[:B * TILES, :, DIM:] = flat
    g = {k[len("L0_xattn_"):]: np.asarray(v) for k, v in a.items() if k.startswith("L0_xattn_")}
    f = {k[len("L0_ffn_"):]: np.asarray(v) for k, v in a.items() if k.startswith("L0_ffn_")}
    by_head = lambda w: w.reshape(NC, P, H, D).transpose(2, 1, 0, 3).reshape(H, P, DIM)
    flipped = lambda w: w.reshape(DIM, H, D).transpose(1, 2, 0)
    row = lambda v: v.reshape(H, D).T
    small = np.concatenate([row(g["q_b"]), row(g["nq_s"]), row(g["ki_b"]), row(g["k_b"]), row(g["nki_s"]),
                            row(g["nkt_s"]), row(g["vi_b"]), row(g["v_b"]), g["o_b"].reshape(NC, P).T], axis=1)
    up_T = lambda w: w.reshape(-1, I, NC, P).transpose(0, 3, 2, 1).reshape(-1, P, DIM)
    ffn = np.zeros((E + 3, P, 3 * DIM), np.float32)
    for at, gate, up, down in ((slice(0, E), f["gate_w"], f["up_w"], f["down_w"]),
                               (slice(E, E + 1), f["shared_gate_w"][None], f["shared_up_w"][None],
                                f["shared_down_w"][None])):
        ffn[at] = np.concatenate([up_T(gate), up_T(up), down.transpose(0, 2, 1)], axis=2)
    return {
        "xT": chunks(x.T), "ctx": packed, "qw": by_head(g["q_w"]),
        "kw": np.concatenate([flipped(g["ki_w"]), flipped(g["k_w"])], axis=2),
        "kwb": np.concatenate([x for w, b in (("ki_w", "ki_b"), ("k_w", "k_b"))
                               for x in (flipped(g[w]), g[b].reshape(H, D, 1), g[b].reshape(H, D, 1))], axis=2),
        "vw": np.concatenate([by_head(g["vi_w"]), by_head(g["v_w"]), g["o_w"].reshape(H, D, DIM)], axis=2),
        "small": small, "router": chunks(f["router_w"].T), "bias": f["expert_bias"][None], "ffn": ffn,
    }


def kernel(**inputs):
    import numpy as np
    from concourse import bacc
    from concourse.bass_utils import run_bass_kernel_spmd

    nc = bacc.Bacc("TRN2", target_bir_lowering=False, num_devices=1, dynamic_dma_scratch_size=1024)
    arrays = {f"in_{k}": np.ascontiguousarray(v) for k, v in _layouts(inputs).items()}
    args = [nc.dram_tensor(k, v.shape, mybir.dt.from_np(v.dtype), kind="ExternalInput").ap()
            for k, v in arrays.items()]
    out = nc.dram_tensor("outT", (P, NC, N), F32, kind="ExternalOutput").ap()
    build(nc, *args, out)
    got = run_bass_kernel_spmd(nc, [arrays], core_ids=[0]).results[0]["outT"]
    return got.transpose(1, 0, 2).reshape(DIM, N).T.reshape(B, S, DIM)
```
